# Optimizing a Trainium2 kernel written in Bass

```python
import numpy as np
import jax
import jax.numpy as jnp

def _softmax(x, axis=-1):
    return jax.nn.softmax(x, axis=axis)

def _gelu(x):
    return jax.nn.gelu(x, approximate=True)

def _silu(x):
    return jax.nn.silu(x)

def _sigmoid(x):
    return jax.nn.sigmoid(x)

def _layernorm(x, axis=-1, eps=1e-05):
    m = jnp.mean(x, axis=axis, keepdims=True)
    v = jnp.var(x, axis=axis, keepdims=True)
    return (x - m) / jnp.sqrt(v + eps)

def _scatter_add(tgt, idx, src, axis=0):
    return tgt.at[idx].add(src)

def _segment_sum(src, seg, n):
    return jax.ops.segment_sum(src, seg, n)
kernel_name = 'mk_decoder_postln_d2_seqx_r8_702ef8'

def setup_inputs(seed: int=0):
    np.random.seed(seed)
    _w = jnp.asarray

    def _rec_inputs():
        import jax
        import jax.numpy as jnp
        _rk = jax.random.key(seed)
        x = 7.22e-05 + 1 * jax.random.normal(jax.random.fold_in(_rk, 1), (16, 100, 128), jnp.float32)
        _lenS = 100 - jax.random.randint(jax.random.fold_in(_rk, 7), (16,), 0, max(1, 100 // 4) + 1, jnp.int32)
        _lenS2 = 1444 - jax.random.randint(jax.random.fold_in(_rk, 8), (16,), 0, max(1, 1444 // 4) + 1, jnp.int32)
        _ctx_1024P = jax.random.normal(jax.random.fold_in(_rk, 11), (16, 16, 128), jnp.float32)
        _ctx_1024c = jax.random.dirichlet(jax.random.fold_in(_rk, 511), 0.3 * jnp.ones((16,), jnp.float32), (16, 1444))
        _ctx_1024t = jnp.einsum('bsk,bkd->bsd', _ctx_1024c, _ctx_1024P)
        _ctx_1024t = _ctx_1024t * jax.lax.rsqrt(jnp.mean(jnp.square(_ctx_1024t)) + 1e-12) * 0.953939
        ctx_1024 = 4.13588e-05 + 0.999923 * (_ctx_1024t + 0.3 * jax.random.normal(jax.random.fold_in(_rk, 611), (16, 1444, 128), jnp.float32))
        return (x, ctx_1024, _lenS2)
    x, ctx_1024, _lenS2 = _rec_inputs()

    def _L0_attn_setup():
        import jax, jax.numpy as jnp
        import numpy as np
        B, L, D = (8, 512, 128)
        EPS = 1e-05
        key = jax.random.key(seed)
        ks = jax.random.split(key, 8)
        s = 0.02
        return {'x': jax.random.normal(ks[0], (B, L, D), dtype=jnp.float32), 'decay': jnp.full((D,), 0.9, dtype=jnp.float32), 'Wr': jax.random.normal(ks[1], (D, D), dtype=jnp.float32) * s, 'br': jnp.zeros((D,), dtype=jnp.float32), 'Wg': jax.random.normal(ks[2], (D, D), dtype=jnp.float32) * s, 'bg': jnp.zeros((D,), dtype=jnp.float32), 'Wo': jax.random.normal(ks[3], (D, D), dtype=jnp.float32) * s, 'bo': jnp.zeros((D,), dtype=jnp.float32), 'ln_w': jnp.ones((D,), dtype=jnp.float32), 'ln_b': jnp.zeros((D,), dtype=jnp.float32)}
    _L0_attn_all = _L0_attn_setup()
    _L0_attn_in = {k: v for k, v in _L0_attn_all.items() if k in ('decay', 'Wr', 'br', 'Wg', 'bg', 'Wo', 'bo', 'ln_w', 'ln_b')}
    del _L0_attn_all

    def _L0_xattn_setup():
        import jax, jax.numpy as jnp
        import numpy as np
        DIM, HEADS, HEAD_DIM = (128, 16, 64)
        B, L, S = (4, 256, 256)
        EPS = 1e-05
        NEG_INF = -1000000000.0

        def rms_norm(x, w):
            var = jnp.mean(jnp.square(x), axis=-1, keepdims=True)
            return x * jax.lax.rsqrt(var + EPS) * w
        key = jax.random.key(seed)
        ks = jax.random.split(key, 9)
        hd = HEADS * HEAD_DIM
        scale = 1.0 / np.sqrt(DIM)
        return {'q': jax.random.normal(ks[0], (B, L, DIM), dtype=jnp.float32), 'kv': jax.random.normal(ks[1], (B, S, DIM), dtype=jnp.float32), 'x_seqlens': jax.random.randint(ks[2], (B,), 1, S + 1, dtype=jnp.int32), 'Wq': jax.random.normal(ks[3], (DIM, hd), dtype=jnp.float32) * scale, 'Wk': jax.random.normal(ks[4], (DIM, hd), dtype=jnp.float32) * scale, 'Wv': jax.random.normal(ks[5], (DIM, hd), dtype=jnp.float32) * scale, 'Wo': jax.random.normal(ks[6], (hd, DIM), dtype=jnp.float32) * (1.0 / np.sqrt(hd)), 'q_norm_w': jnp.ones((HEAD_DIM,), dtype=jnp.float32), 'k_norm_w': jnp.ones((HEAD_DIM,), dtype=jnp.float32)}
    _L0_xattn_all = _L0_xattn_setup()
    _L0_xattn_in = {k: v for k, v in _L0_xattn_all.items() if k in ('Wq', 'Wk', 'Wv', 'Wo', 'q_norm_w', 'k_norm_w')}
    del _L0_xattn_all

    def _L0_ffn_setup():
        import jax, jax.numpy as jnp
        import numpy as np
        ALPHA = 1.702
        LIMIT = 7.0
        TOP_K = 2
        key = jax.random.key(seed)
        ks = jax.random.split(key, 4)
        B, S, H, E, I = (2, 128, 128, 8, 256)
        return {'hidden_states': jax.random.normal(ks[0], (B, S, H), jnp.float32), 'router_weight': jax.random.normal(ks[1], (E, H), jnp.float32), 'router_bias': jnp.zeros((E,), jnp.float32), 'gate_up_proj': jax.random.normal(ks[2], (E, H, 2 * I), jnp.float32) * 0.02, 'gate_up_bias': jnp.zeros((E, 2 * I), jnp.float32), 'down_proj': jax.random.normal(ks[3], (E, I, H), jnp.float32) * 0.02, 'down_bias': jnp.zeros((E, H), jnp.float32)}
    _L0_ffn_all = _L0_ffn_setup()
    _L0_ffn_in = {k: v for k, v in _L0_ffn_all.items() if k in ('router_weight', 'router_bias', 'gate_up_proj', 'gate_up_bias', 'down_proj', 'down_bias')}
    del _L0_ffn_all

    def _L1_attn_setup():
        import jax, jax.numpy as jnp
        import numpy as np
        D_MODEL = 128
        N_HEADS = 16
        HEAD_DIM = D_MODEL // N_HEADS
        BATCH = 4
        SEQ = 512
        EPS = 1e-06

        def _feature_map(x):
            return jax.nn.elu(x) + 1.0
        key = jax.random.key(seed)
        ks = jax.random.split(key, 9)
        s = 1.0 / np.sqrt(D_MODEL)
        return {'x': jax.random.normal(ks[0], (BATCH, SEQ, D_MODEL), jnp.float32), 'Wq': jax.random.normal(ks[1], (D_MODEL, D_MODEL), jnp.float32) * s, 'bq': jnp.zeros((D_MODEL,), jnp.float32), 'Wk': jax.random.normal(ks[2], (D_MODEL, D_MODEL), jnp.float32) * s, 'bk': jnp.zeros((D_MODEL,), jnp.float32), 'Wv': jax.random.normal(ks[3], (D_MODEL, D_MODEL), jnp.float32) * s, 'bv': jnp.zeros((D_MODEL,), jnp.float32), 'Wo': jax.random.normal(ks[4], (D_MODEL, D_MODEL), jnp.float32) * s, 'bo': jnp.zeros((D_MODEL,), jnp.float32)}
    _L1_attn_all = _L1_attn_setup()
    _L1_attn_in = {k: v for k, v in _L1_attn_all.items() if k in ('Wq', 'bq', 'Wk', 'bk', 'Wv', 'bv', 'Wo', 'bo')}
    del _L1_attn_all

    def _L1_xattn_setup():
        import jax, jax.numpy as jnp
        import numpy as np
        B, TQ, TK = (2, 256, 256)
        X_TO_DIM = 128
        X_FROM_DIM = 128
        HIDDEN = 128
        H = 16
        DH = HIDDEN // H
        key = jax.random.key(seed)
        ks = jax.random.split(key, 10)
        s = 0.02
        return {'x_to': jax.random.normal(ks[0], (B, TQ, X_TO_DIM), dtype=jnp.float32), 'x_from': jax.random.normal(ks[1], (B, TK, X_FROM_DIM), dtype=jnp.float32), 'Wq': jax.random.normal(ks[2], (H, X_TO_DIM, DH), dtype=jnp.float32) * s, 'bq': jax.random.normal(ks[3], (H, DH), dtype=jnp.float32) * s, 'Wk': jax.random.normal(ks[4], (H, X_FROM_DIM, DH), dtype=jnp.float32) * s, 'bk': jax.random.normal(ks[5], (H, DH), dtype=jnp.float32) * s, 'Wv': jax.random.normal(ks[6], (H, X_FROM_DIM, DH), dtype=jnp.float32) * s, 'bv': jax.random.normal(ks[7], (H, DH), dtype=jnp.float32) * s, 'Wo': jax.random.normal(ks[8], (HIDDEN, HIDDEN), dtype=jnp.float32) * s, 'bo': jax.random.normal(ks[9], (HIDDEN,), dtype=jnp.float32) * s}
    _L1_xattn_all = _L1_xattn_setup()
    _L1_xattn_in = {k: v for k, v in _L1_xattn_all.items() if k in ('Wq', 'bq', 'Wk', 'bk', 'Wv', 'bv', 'Wo', 'bo')}
    del _L1_xattn_all

    def _L1_ffn_setup():
        import jax, jax.numpy as jnp
        import numpy as np
        D_MODEL = 128
        D_FF = 512
        NUM_EXPERTS = 8
        TOP_K = 2
        SEQ = 128
        BATCH = 2
        key = jax.random.key(seed)
        ks = jax.random.split(key, 7)
        s = 0.02
        x = jax.random.normal(ks[0], (SEQ, BATCH, D_MODEL), dtype=jnp.float32)
        gate_w = jax.random.normal(ks[1], (D_MODEL, NUM_EXPERTS), dtype=jnp.float32) * s
        gate_b = jnp.zeros((NUM_EXPERTS,), dtype=jnp.float32)
        W1 = jax.random.normal(ks[2], (NUM_EXPERTS, D_MODEL, D_FF), dtype=jnp.float32) * s
        b1 = jnp.zeros((NUM_EXPERTS, D_FF), dtype=jnp.float32)
        W2 = jax.random.normal(ks[3], (NUM_EXPERTS, D_FF, D_MODEL), dtype=jnp.float32) * s
        b2 = jnp.zeros((NUM_EXPERTS, D_MODEL), dtype=jnp.float32)
        return {'x': x, 'gate_w': gate_w, 'gate_b': gate_b, 'W1': W1, 'b1': b1, 'W2': W2, 'b2': b2}
    _L1_ffn_all = _L1_ffn_setup()
    _L1_ffn_in = {k: v for k, v in _L1_ffn_all.items() if k in ('gate_w', 'gate_b', 'W1', 'b1', 'W2', 'b2')}
    del _L1_ffn_all
    return {'x': x, 'ctx_1024': ctx_1024, '_lenS2': _lenS2, 'L0_attn_decay': _L0_attn_in['decay'], 'L0_attn_Wr': _L0_attn_in['Wr'], 'L0_attn_br': _L0_attn_in['br'], 'L0_attn_Wg': _L0_attn_in['Wg'], 'L0_attn_bg': _L0_attn_in['bg'], 'L0_attn_Wo': _L0_attn_in['Wo'], 'L0_attn_bo': _L0_attn_in['bo'], 'L0_attn_ln_w': _L0_attn_in['ln_w'], 'L0_attn_ln_b': _L0_attn_in['ln_b'], 'L0_xattn_Wq': _L0_xattn_in['Wq'], 'L0_xattn_Wk': _L0_xattn_in['Wk'], 'L0_xattn_Wv': _L0_xattn_in['Wv'], 'L0_xattn_Wo': _L0_xattn_in['Wo'], 'L0_xattn_q_norm_w': _L0_xattn_in['q_norm_w'], 'L0_xattn_k_norm_w': _L0_xattn_in['k_norm_w'], 'L0_ffn_router_weight': _L0_ffn_in['router_weight'], 'L0_ffn_router_bias': _L0_ffn_in['router_bias'], 'L0_ffn_gate_up_proj': _L0_ffn_in['gate_up_proj'], 'L0_ffn_gate_up_bias': _L0_ffn_in['gate_up_bias'], 'L0_ffn_down_proj': _L0_ffn_in['down_proj'], 'L0_ffn_down_bias': _L0_ffn_in['down_bias'], 'L1_attn_Wq': _L1_attn_in['Wq'], 'L1_attn_bq': _L1_attn_in['bq'], 'L1_attn_Wk': _L1_attn_in['Wk'], 'L1_attn_bk': _L1_attn_in['bk'], 'L1_attn_Wv': _L1_attn_in['Wv'], 'L1_attn_bv': _L1_attn_in['bv'], 'L1_attn_Wo': _L1_attn_in['Wo'], 'L1_attn_bo': _L1_attn_in['bo'], 'L1_xattn_Wq': _L1_xattn_in['Wq'], 'L1_xattn_bq': _L1_xattn_in['bq'], 'L1_xattn_Wk': _L1_xattn_in['Wk'], 'L1_xattn_bk': _L1_xattn_in['bk'], 'L1_xattn_Wv': _L1_xattn_in['Wv'], 'L1_xattn_bv': _L1_xattn_in['bv'], 'L1_xattn_Wo': _L1_xattn_in['Wo'], 'L1_xattn_bo': _L1_xattn_in['bo'], 'L1_ffn_gate_w': _L1_ffn_in['gate_w'], 'L1_ffn_gate_b': _L1_ffn_in['gate_b'], 'L1_ffn_W1': _L1_ffn_in['W1'], 'L1_ffn_b1': _L1_ffn_in['b1'], 'L1_ffn_W2': _L1_ffn_in['W2'], 'L1_ffn_b2': _L1_ffn_in['b2']}

def reference(x, ctx_1024, _lenS2, L0_attn_decay, L0_attn_Wr, L0_attn_br, L0_attn_Wg, L0_attn_bg, L0_attn_Wo, L0_attn_bo, L0_attn_ln_w, L0_attn_ln_b, L0_xattn_Wq, L0_xattn_Wk, L0_xattn_Wv, L0_xattn_Wo, L0_xattn_q_norm_w, L0_xattn_k_norm_w, L0_ffn_router_weight, L0_ffn_router_bias, L0_ffn_gate_up_proj, L0_ffn_gate_up_bias, L0_ffn_down_proj, L0_ffn_down_bias, L1_attn_Wq, L1_attn_bq, L1_attn_Wk, L1_attn_bk, L1_attn_Wv, L1_attn_bv, L1_attn_Wo, L1_attn_bo, L1_xattn_Wq, L1_xattn_bq, L1_xattn_Wk, L1_xattn_bk, L1_xattn_Wv, L1_xattn_bv, L1_xattn_Wo, L1_xattn_bo, L1_ffn_gate_w, L1_ffn_gate_b, L1_ffn_W1, L1_ffn_b1, L1_ffn_W2, L1_ffn_b2):
    import jax
    import jax.numpy as jnp

    def _L0_attn_ref(x, decay, Wr, br, Wg, bg, Wo, bo, ln_w, ln_b):
        import jax, jax.numpy as jnp
        import numpy as np
        B, L, D = (8, 512, 128)
        EPS = 1e-05
        b, l, d = x.shape
        decay_factor = jax.nn.sigmoid(decay)
        one_minus = 1.0 - decay_factor
        z = jax.nn.sigmoid(jnp.einsum('bld,ed->ble', x, Wg) + bg)
        x_t_first = jnp.moveaxis(x, 1, 0)
        z_t_first = jnp.moveaxis(z, 1, 0)

        def step(h, inp):
            x_t, z_t = inp
            pred_x = h @ Wr.T + br
            error = x_t - pred_x
            h_new = decay_factor * h + one_minus * (z_t * error)
            return (h_new, h_new)
        h0 = jnp.zeros((b, d), dtype=x.dtype)
        _, ys = jax.lax.scan(step, h0, (x_t_first, z_t_first))
        y = jnp.moveaxis(ys, 0, 1)
        mean = jnp.mean(y, axis=-1, keepdims=True)
        var = jnp.mean(jnp.square(y - mean), axis=-1, keepdims=True)
        y = (y - mean) * jax.lax.rsqrt(var + EPS) * ln_w + ln_b
        return jnp.einsum('bld,ed->ble', y, Wo) + bo

    def _L0_xattn_ref(q, kv, x_seqlens, Wq, Wk, Wv, Wo, q_norm_w, k_norm_w):
        import jax, jax.numpy as jnp
        import numpy as np
        DIM, HEADS, HEAD_DIM = (128, 16, 64)
        B, L, S = (4, 256, 256)
        EPS = 1e-05
        NEG_INF = -1000000000.0

        def rms_norm(x, w):
            var = jnp.mean(jnp.square(x), axis=-1, keepdims=True)
            return x * jax.lax.rsqrt(var + EPS) * w
        b, l, _ = q.shape
        s = kv.shape[1]
        qh = (q @ Wq).reshape(b, l, HEADS, HEAD_DIM).transpose(0, 2, 1, 3)
        kh = (kv @ Wk).reshape(b, s, HEADS, HEAD_DIM).transpose(0, 2, 1, 3)
        vh = (kv @ Wv).reshape(b, s, HEADS, HEAD_DIM).transpose(0, 2, 1, 3)
        qh = rms_norm(qh, q_norm_w)
        kh = rms_norm(kh, k_norm_w)
        mask = (jnp.arange(s, dtype=jnp.int32)[None, :] < x_seqlens[:, None])[:, None, None, :]
        scores = jnp.einsum('bhld,bhsd->bhls', qh, kh) * (1.0 / np.sqrt(HEAD_DIM))
        scores = jnp.where(mask, scores, NEG_INF)
        attn = jax.nn.softmax(scores, axis=-1)
        o = jnp.einsum('bhls,bhsd->bhld', attn, vh)
        o = o.transpose(0, 2, 1, 3).reshape(b, l, HEADS * HEAD_DIM)
        return o @ Wo

    def _L0_ffn_ref(hidden_states, router_weight, router_bias, gate_up_proj, gate_up_bias, down_proj, down_bias):
        import jax, jax.numpy as jnp
        import numpy as np
        ALPHA = 1.702
        LIMIT = 7.0
        TOP_K = 2
        B, S, H = hidden_states.shape
        E, _, two_I = gate_up_proj.shape
        I = two_I // 2
        flat = hidden_states.reshape(B * S, H)
        logits = flat @ router_weight.T + router_bias
        scores = jax.nn.softmax(logits, axis=-1)
        topk_w, topk_idx = jax.lax.top_k(scores, TOP_K)
        gu = jnp.einsum('th,ehn->ten', flat, gate_up_proj) + gate_up_bias
        gate = jnp.minimum(gu[..., :I], LIMIT)
        up = jnp.clip(gu[..., I:], -LIMIT, LIMIT)
        glu = gate * jax.nn.sigmoid(gate * ALPHA)
        act = (up + 1.0) * glu
        down = jnp.einsum('tei,eih->teh', act, down_proj) + down_bias
        gathered = jnp.take_along_axis(down, topk_idx[:, :, None], axis=1)
        out = (gathered * topk_w[:, :, None]).sum(axis=1)
        return out.reshape(B, S, H)

    def _L1_attn_ref(x, Wq, bq, Wk, bk, Wv, bv, Wo, bo):
        import jax, jax.numpy as jnp
        import numpy as np
        D_MODEL = 128
        N_HEADS = 16
        HEAD_DIM = D_MODEL // N_HEADS
        BATCH = 4
        SEQ = 512
        EPS = 1e-06

        def _feature_map(x):
            return jax.nn.elu(x) + 1.0
        B, S, _ = x.shape
        q = (x @ Wq + bq).reshape(B, S, N_HEADS, HEAD_DIM).transpose(0, 2, 1, 3)
        k = (x @ Wk + bk).reshape(B, S, N_HEADS, HEAD_DIM).transpose(0, 2, 1, 3)
        v = (x @ Wv + bv).reshape(B, S, N_HEADS, HEAD_DIM).transpose(0, 2, 1, 3)
        q = _feature_map(q)
        k = _feature_map(k)
        kv = jnp.einsum('bhnd,bhne->bhde', k, v)
        out = jnp.einsum('bhnd,bhde->bhne', q, kv)
        k_sum = k.sum(axis=2)
        normalizer = jnp.einsum('bhnd,bhd->bhn', q, k_sum) + EPS
        out = out / normalizer[..., None]
        out = out.transpose(0, 2, 1, 3).reshape(B, S, D_MODEL)
        return out @ Wo + bo

    def _L1_xattn_ref(x_to, x_from, Wq, bq, Wk, bk, Wv, bv, Wo, bo):
        import jax, jax.numpy as jnp
        import numpy as np
        B, TQ, TK = (2, 256, 256)
        X_TO_DIM = 128
        X_FROM_DIM = 128
        HIDDEN = 128
        H = 16
        DH = HIDDEN // H
        q = jnp.einsum('btf,hfd->bhtd', x_to, Wq) + bq[None, :, None, :]
        k = jnp.einsum('bsf,hfd->bhsd', x_from, Wk) + bk[None, :, None, :]
        v = jnp.einsum('bsf,hfd->bhsd', x_from, Wv) + bv[None, :, None, :]
        scores = jnp.einsum('bhtd,bhsd->bhts', q, k) / jnp.sqrt(jnp.float32(DH))
        attn = jax.nn.softmax(scores, axis=-1)
        out = jnp.einsum('bhts,bhsd->bhtd', attn, v)
        concat = jnp.transpose(out, (0, 2, 1, 3)).reshape(out.shape[0], out.shape[2], H * DH)
        return concat @ Wo.T + bo

    def _L1_ffn_ref(x, gate_w, gate_b, W1, b1, W2, b2):
        import jax, jax.numpy as jnp
        import numpy as np
        D_MODEL = 128
        D_FF = 512
        NUM_EXPERTS = 8
        TOP_K = 2
        SEQ = 128
        BATCH = 2
        S, B, D = x.shape
        x_flat = x.reshape(-1, D)
        scores = x_flat @ gate_w + gate_b
        topk_vals, topk_idx = jax.lax.top_k(scores, TOP_K)
        topk_probs = jax.nn.softmax(topk_vals, axis=-1)
        one_hot = jax.nn.one_hot(topk_idx, NUM_EXPERTS, dtype=x.dtype)
        combine = jnp.einsum('tk,tke->te', topk_probs, one_hot)
        h = jax.nn.relu(jnp.einsum('td,edf->etf', x_flat, W1) + b1[:, None, :])
        y = jnp.einsum('etf,efd->etd', h, W2) + b2[:, None, :]
        out = jnp.einsum('te,etd->td', combine, y)
        return out.reshape(S, B, D)
    x = _layernorm(x + _L0_attn_ref(x, L0_attn_decay, L0_attn_Wr, L0_attn_br, L0_attn_Wg, L0_attn_bg, L0_attn_Wo, L0_attn_bo, L0_attn_ln_w, L0_attn_ln_b), axis=-1)
    x = _layernorm(x + _L0_xattn_ref(x, ctx_1024, _lenS2, L0_xattn_Wq, L0_xattn_Wk, L0_xattn_Wv, L0_xattn_Wo, L0_xattn_q_norm_w, L0_xattn_k_norm_w), axis=-1)
    x = _layernorm(x + _L0_ffn_ref(x, L0_ffn_router_weight, L0_ffn_router_bias, L0_ffn_gate_up_proj, L0_ffn_gate_up_bias, L0_ffn_down_proj, L0_ffn_down_bias), axis=-1)
    x = _layernorm(x + _L1_attn_ref(x, L1_attn_Wq, L1_attn_bq, L1_attn_Wk, L1_attn_bk, L1_attn_Wv, L1_attn_bv, L1_attn_Wo, L1_attn_bo), axis=-1)
    x = _layernorm(x + _L1_xattn_ref(x, ctx_1024, L1_xattn_Wq, L1_xattn_bq, L1_xattn_Wk, L1_xattn_bk, L1_xattn_Wv, L1_xattn_bv, L1_xattn_Wo, L1_xattn_bo), axis=-1)
    x = _layernorm(x + _L1_ffn_ref(x, L1_ffn_gate_w, L1_ffn_gate_b, L1_ffn_W1, L1_ffn_b1, L1_ffn_W2, L1_ffn_b2), axis=-1)
    return x

_drawn_inputs = setup_inputs


def setup_inputs(seed=0):
    import zlib

    import numpy as np

    out = dict(_drawn_inputs(seed))
    spreads = {'L0_attn_decay': (0.8999999761581421, 0.599),
     'L0_attn_br': (0.0, 0.1),
     'L0_attn_bg': (0.0, 0.613),
     'L0_attn_bo': (0.0, 0.1),
     'L0_attn_ln_w': (1.0, 0.2),
     'L0_attn_ln_b': (0.0, 0.1),
     'L0_xattn_q_norm_w': (1.0, 0.2),
     'L0_xattn_k_norm_w': (1.0, 0.2),
     'L0_ffn_router_bias': (0.0, 2.0),
     'L0_ffn_gate_up_bias': (0.0, 0.414),
     'L0_ffn_down_bias': (0.0, 0.1),
     'L1_attn_bq': (0.0, 2.0),
     'L1_attn_bk': (0.0, 2.0),
     'L1_attn_bv': (0.0, 0.1),
     'L1_attn_bo': (0.0, 0.1),
     'L1_ffn_gate_b': (0.0, 0.1),
     'L1_ffn_b1': (0.0, 0.367),
     'L1_ffn_b2': (0.0, 0.1)}
    factors = {'L1_attn_Wq': 3.064,
     'L1_xattn_Wq': 8.0,
     'L1_xattn_bq': 45.49,
     'L1_xattn_Wk': 8.0,
     'L1_xattn_bk': 64.0,
     'L1_xattn_bv': 8.0}
    for name, (base, spread) in spreads.items():
        noise = np.random.default_rng([zlib.crc32(name.encode()), seed]).standard_normal(out[name].shape)
        drawn = base * np.exp(spread * noise) if base else spread * noise
        out[name] = jnp.asarray(drawn.astype(out[name].dtype))
    for name, factor in factors.items():
        out[name] = (out[name] * factor).astype(out[name].dtype)
    return out
```

```python
from contextlib import ExitStack

import concourse.bass as bass
from concourse import mybir

ALU = mybir.AluOpType
ACT = mybir.ActivationFunctionType
F32 = mybir.dt.float32
BF16 = mybir.dt.bfloat16
I32 = mybir.dt.int32
AX_X = mybir.AxisListType.X

B, L, D = 16, 100, 128
T = B * L
S = 1444
CH = 12
SP_FULL = S // CH
SP_MAX = SP_FULL + 1
HEADS = 16
HD0 = 64
HD1 = 8
E = 8
I0 = 256
F1 = 512
HALF = 8 * L
EPS = 1e-5
MASKED = -30000.0


def rows(c):
    return SP_MAX if c < S % CH else SP_FULL


def off(c):
    return SP_FULL * c + min(c, S % CH)


class Net:

    def __init__(self, nc):
        self.nc = nc
        self.ctx = ExitStack()

    def __enter__(self):
        self.ctx.__enter__()
        return self

    def __exit__(self, *a):
        return self.ctx.__exit__(*a)

    def sb(self, name, shape, dt=F32):
        return self.ctx.enter_context(self.nc.sbuf_tensor(name, shape, dt))

    def ps(self, name, n=1):
        return self.ctx.enter_context(self.nc.psum_tensor(name, [128, n, 512], F32))

    def sem(self, name):
        return self.ctx.enter_context(self.nc.semaphore(name))


def over_heads(col, n):
    p, m = col.shape
    return col.unsqueeze(2).to_broadcast([p, m, n])



def norm_tokens(nc, tag, k, x, xT=None, gain=None, shift=None, out=None):
    with Net(nc) as n:
        stats = n.sb(f"{tag}_stats", [L, B, 6])
        mv = n.sb(f"{tag}_mean_var", [L, B, 2])
        sd = n.sb(f"{tag}_sd", [L, B])
        rstd = n.sb(f"{tag}_rstd", [L, B])
        turned = n.ps(f"{tag}_turned", 4)
        s_stat, s_sd, s_rstd, s_norm, s_turn, s_evac, s_out = k["norm_sems"]
        c = k["norms"]
        k["norms"] = c + 1
        block = n.ctx.enter_context(nc.Block())

        @block.vector
        def _(dve):
            for b in range(B):
                dve.bn_stats(stats[:, b, :], x[:, b, :]).then_inc(s_stat, 1)
            for b in range(B):
                dve.wait_ge(s_stat, 2 * B * c + b + 1)
                dve.bn_aggr(mv[:, b, :], stats[:, b, :]).then_inc(s_stat, 1)
            dve.wait_ge(s_sd, c + 1)
            dve.reciprocal(rstd[:, :], sd[:, :]).then_inc(s_rstd, 1)
            dve.wait_ge(s_rstd, c + 1)
            for b in range(B):
                dve.tensor_scalar(x[:, b, :], x[:, b, :], mv[:, b, 0:1], rstd[:, b:b + 1],
                                  ALU.subtract, ALU.mult).then_inc(s_norm, 1)

        @block.scalar
        def _(act):
            act.wait_ge(s_stat, 2 * B * (c + 1))
            act.activation(sd[:, :], mv[:, :, 1], ACT.Sqrt, bias=k["eps"][0:L, 0:1]).then_inc(s_sd, 1)
            if xT is not None:
                for g in range(4):
                    act.wait_ge(s_turn, 4 * c + g + 1)
                    src = turned[:, g, 0:4 * L]
                    dst = xT[:, 4 * g * L:4 * (g + 1) * L]
                    if gain is None:
                        act.activation(dst, src, ACT.Copy).then_inc(s_evac, 1)
                    else:
                        act.activation(dst, src, ACT.Identity, bias=shift, scale=gain).then_inc(s_evac, 1)

        if xT is not None:
            @block.tensor
            def _(pe):
                for b in range(B):
                    pe.wait_ge(s_norm, B * c + b + 1)
                    t = pe.transpose(turned[:, b // 4, (b % 4) * L:(b % 4 + 1) * L], x[:, b, :],
                                     k["ident"][0:L, 0:L])
                    if b % 4 == 3:
                        t.then_inc(s_turn, 1)

        if out is not None:
            @block.sync
            def _(sp):
                sp.wait_ge(s_norm, B * (c + 1))
                sp.dma_start(out, x[:, :, :]).then_inc(s_out, 16)
                sp.wait_ge(s_out, 16)



def load_weights(nc, a, k, pairs):
    with Net(nc) as n:
        s_load = n.sem("s_load")
        s_const = n.sem("s_const")
        block = n.ctx.enter_context(nc.Block())

        @block.sync
        def _(sp):
            for dst, src in pairs[0::2]:
                sp.dma_start(dst, src).then_inc(s_load, 16)
            sp.wait_ge(s_load, 16 * len(pairs))

        @block.scalar
        def _(act):
            for dst, src in pairs[1::2]:
                act.dma_start(dst, src).then_inc(s_load, 16)

        @block.vector
        def _(dve):
            dve.memset(k["eps"][:, :], EPS).then_inc(s_const, 1)
            dve.memset(k["ones"][:, :], 1.0).then_inc(s_const, 1)
            dve.memset(k["ones16"][:, :], 1.0).then_inc(s_const, 1)


def load_stage(nc, tag, pairs):
    with Net(nc) as n:
        s_load = n.sem(f"{tag}_s_load")
        block = n.ctx.enter_context(nc.Block())

        @block.sync
        def _(sp):
            for dst, src in pairs:
                sp.dma_start(dst, src).then_inc(s_load, 16)
            sp.wait_ge(s_load, 16 * len(pairs))



def recurrence(nc, k, x_steps, hidden):
    with Net(nc) as n:
        forget = n.sb("forget", [D, 1])
        negkeep = n.sb("negkeep", [D, 1])
        z = n.sb("z", [D, L, B])
        c = n.sb("c", [D, L, B])
        w = n.sb("w", [D, 2, B])
        m = n.sb("m", [D, 2, B])
        zp = n.ps("zp", 4)
        pred = n.ps("pred", 2)
        s_z = n.sem("s_z")
        s_gate = n.sem("s_gate")
        s_pre = n.sem("s_pre")
        s_w = n.sem("s_w")
        s_m = n.sem("s_m")
        s_h = n.sem("s_h")
        s_pred = n.sem("s_pred")
        TG = L // 4
        xs = x_steps
        block = n.ctx.enter_context(nc.Block())

        @block.tensor
        def _(pe):
            for g in range(4):
                pe.matmul(zp[:, g, 0:TG * B], k["wgT"][:, :], xs[:, g * TG:(g + 1) * TG, :],
                          start=True, stop=True).then_inc(s_z, 1)

            def predict(t, p):
                pe.wait_ge(s_w, t)
                pe.matmul(pred[:, p, 0:B], k["wrT"][:, :], w[:, 1 - p, :], start=True, stop=False)
                pe.wait_ge(s_m, t)
                pe.matmul(pred[:, p, 0:B], k["wrT"][:, :], m[:, 1 - p, :], start=False,
                          stop=True).then_inc(s_pred, 1)

            with pe.Fori(0, (L - 2) // 2) as i:
                predict(2 * i + 1, 1)
                predict(2 * i + 2, 0)
            predict(L - 1, 1)

        @block.scalar
        def _(act):
            act.activation(forget[:, :], k["decay"][:, :], ACT.Sigmoid).then_inc(s_gate, 1)
            for g in range(4):
                act.wait_ge(s_z, g + 1)
                act.activation(z[:, g * TG:(g + 1) * TG, :].rearrange("p t b -> p (t b)"),
                               zp[:, g, 0:TG * B], ACT.Sigmoid, bias=k["bg"][:, 0:1]).then_inc(s_gate, 1)

        @block.vector
        def _(dve):
            dve.tensor_scalar(c[:, :, :], xs[:, :, :], k["br"][:, 0:1], None, ALU.subtract).then_inc(s_pre, 1)
            dve.wait_ge(s_gate, 1)
            dve.tensor_scalar(negkeep[:, :], forget[:, :], -1.0, None, ALU.add).then_inc(s_pre, 1)
            dve.wait_ge(s_gate, 5)
            dve.wait_ge(s_pre, 2)
            dve.tensor_scalar(z[:, :, :], z[:, :, :], negkeep[:, 0:1], None, ALU.mult).then_inc(s_pre, 1)
            dve.wait_ge(s_pre, 3)
            dve.scalar_tensor_tensor(out=c[:, :, :].rearrange("p t b -> p (t b)"),
                                     in0=z[:, :, :].rearrange("p t b -> p (t b)"), scalar=-1.0,
                                     in1=c[:, :, :].rearrange("p t b -> p (t b)"),
                                     op0=ALU.mult, op1=ALU.mult).then_inc(s_pre, 1)
            dve.memset(m[:, :, :], 0.0).then_inc(s_m, 1)
            dve.wait_ge(s_pre, 4)
            dve.tensor_copy(w[:, 0, :], c[:, 0, :]).then_inc(s_w, 1)
            dve.tensor_copy(hidden[:, 0, :], c[:, 0, :]).then_inc(s_h, 1)

            def step(t, p):
                dve.wait_ge(s_h, t)
                dve.scalar_tensor_tensor(out=w[:, p, :], in0=hidden[:, bass.ds(t - 1, 1), :].rearrange("p t b -> p (t b)"),
                                         scalar=forget[:, 0:1],
                                         in1=c[:, bass.ds(t, 1), :].rearrange("p t b -> p (t b)"),
                                         op0=ALU.mult, op1=ALU.add).then_inc(s_w, 1)
                dve.wait_ge(s_pred, t)
                dve.tensor_tensor(m[:, p, :], pred[:, p, 0:B],
                                  z[:, bass.ds(t, 1), :].rearrange("p t b -> p (t b)"), ALU.mult).then_inc(s_m, 1)
                dve.wait_ge(s_m, t + 1)
                dve.wait_ge(s_w, t + 1)
                dve.tensor_tensor(hidden[:, bass.ds(t, 1), :].rearrange("p t b -> p (t b)"), w[:, p, :], m[:, p, :],
                                  ALU.add).then_inc(s_h, 1)

            with dve.Fori(0, (L - 2) // 2) as i:
                step(2 * i + 1, 1)
                step(2 * i + 2, 0)
            step(L - 1, 1)


def hidden_to_tokens(nc, k, hidden, y):
    with Net(nc) as n:
        turned = n.ps("hid_turned", 4)
        s_turn = n.sem("hid_s_turned")
        s_evac = n.sem("hid_s_evac")
        block = n.ctx.enter_context(nc.Block())

        @block.tensor
        def _(pe):
            for b in range(B):
                t = pe.transpose(turned[0:L, b // 4, (b % 4) * D:(b % 4 + 1) * D], hidden[:, :, b],
                                 k["ident"][:, :])
                if b % 4 == 3:
                    t.then_inc(s_turn, 1)

        @block.vector
        def _(dve):
            for g in range(4):
                dve.wait_ge(s_turn, g + 1)
                dve.tensor_copy(y[:, 4 * g:4 * g + 4, :].rearrange("l b d -> l (b d)"),
                                turned[0:L, g, :]).then_inc(s_evac, 1)


def project_add(nc, k, tag, inT, weight, bias_row, x):
    with Net(nc) as n:
        prod = n.ps(f"{tag}_prod", 4)
        s_prod, s_bias, s_add = k["project_sems"]
        c = k["projects"]
        k["projects"] = c + 1
        block = n.ctx.enter_context(nc.Block())

        @block.tensor
        def _(pe):
            for b in range(B):
                t = pe.matmul(prod[0:L, b // 4, (b % 4) * D:(b % 4 + 1) * D], inT[:, b * L:(b + 1) * L],
                              weight, start=True, stop=True)
                if b % 4 == 3:
                    t.then_inc(s_prod, 1)

        @block.vector
        def _(dve):
            dve.tensor_tensor(x[:, :, :], x[:, :, :], bias_row.unsqueeze(1).to_broadcast([L, B, D]),
                              ALU.add).then_inc(s_bias, 1)
            dve.wait_ge(s_bias, c + 1)
            for g in range(4):
                dve.wait_ge(s_prod, 4 * c + g + 1)
                xg = x[:, 4 * g:4 * g + 4, :].rearrange("l b d -> l (b d)")
                dve.tensor_tensor(xg, xg, prod[0:L, g, :], ALU.add).then_inc(s_add, 1)



def fold_weights(nc, k, wkT, wvT, wo, wkq, wvo):
    with Net(nc) as n:
        norm_w = n.sb("norm_w", [D, 1])
        norm_row = n.sb("norm_row", [SP_MAX, HD0])
        cap = n.sb("cap", [SP_MAX, 1])
        len_f = n.sb("len_f", [SP_MAX, B])
        prod = n.ps("wvo_prod", 4)
        s_nw = n.sem("s_nw")
        s_cap = n.sem("s_cap")
        s_mask = n.sem("s_mask")
        s_wvo = n.sem("s_wvo")
        s_evac = n.sem("s_wvo_evac")
        s_wkq = n.sem("s_wkq")
        block = n.ctx.enter_context(nc.Block())

        @block.tensor
        def _(pe):
            for r in range(4):
                for h in range(4 * r, 4 * r + 4):
                    j, bank = h % 2, h % 2 + 2 * (r % 2)
                    if r >= 2 and h < 4 * r + 2:
                        pe.wait_ge(s_evac, 2 * (r - 2) + 1 + j)
                    t = pe.matmul(prod[:, bank, (h // 2 % 2) * D:(h // 2 % 2 + 1) * D],
                                  wvT[64 * j:64 * j + 64, h // 2, :], wo[64 * j:64 * j + 64, h // 2, :],
                                  start=True, stop=True)
                t.then_inc(s_wvo, 1)

        @block.vector
        def _(dve):
            dve.tensor_tensor(norm_w[:, :], k["qnw"][:, :], k["knw"][:, :], ALU.mult).then_inc(s_nw, 1)
            dve.wait_ge(s_nw, 1)
            dve.tensor_scalar(wkq[:, :, :], wkT[:, :, :], norm_w[:, 0:1], HD0 ** -0.5, ALU.mult,
                              ALU.mult).then_inc(s_wkq, 1)
            dve.tensor_tensor(norm_row[:, :], k["qnw_row"][0:SP_MAX, :], k["knw_row"][0:SP_MAX, :],
                              ALU.mult).then_inc(s_cap, 1)
            dve.wait_ge(s_cap, 1)
            dve.tensor_reduce(cap[:, :], norm_row[:, :], AX_X, ALU.max, apply_absolute_value=True).then_inc(s_cap, 1)
            dve.tensor_copy(len_f[:, :], k["lens"][:, :]).then_inc(s_cap, 1)
            dve.wait_ge(s_cap, 3)
            dve.tensor_scalar(cap[:, :], cap[:, :], HD0 ** 0.5, None, ALU.mult).then_inc(s_cap, 1)
            mask = k["mask_bias"]
            dve.tensor_tensor(mask[:, :, :], k["row_of"][:, :].unsqueeze(1).to_broadcast([SP_MAX, B, CH]),
                              over_heads(len_f[:, :], CH), ALU.is_ge).then_inc(s_mask, 1)
            dve.wait_ge(s_mask, 1)
            dve.wait_ge(s_cap, 4)
            dve.tensor_scalar(mask[:, :, :], mask[:, :, :], MASKED, cap[:, 0:1], ALU.mult,
                              ALU.subtract).then_inc(s_mask, 1)
            for r in range(4):
                dve.wait_ge(s_wvo, r + 1)
                for j in range(2):
                    dve.tensor_copy(wvo[:, 4 * r + j:4 * r + j + 3:2, :],
                                    prod[:, j + 2 * (r % 2), 0:2 * D].rearrange("p (a d) -> p a d", a=2))\
                       .then_inc(s_evac, 1)


def cross_attention_0(nc, k, ctxT_d, ctxN_d, x, xT, wq, wk, wkq, wvo):
    NS = 2 * CH
    with Net(nc) as n:
        ctxT = [n.sb(f"ctxT{u}", [D, S]) for u in range(2)]
        ctxN = [n.sb(f"ctxN{u}", [SP_MAX, CH, D]) for u in range(2)]
        sq = n.sb("sq", [SP_MAX, 2, 512])
        kss = n.sb("kss", [SP_MAX, CH, HEADS])
        ksd = n.sb("ksd", [SP_MAX, CH, HEADS])
        krs = [n.sb(f"krs{u}", [SP_MAX, CH, HEADS]) for u in range(2)]
        bias = [n.sb(f"bias{u}", [SP_MAX, CH]) for u in range(2)]
        q_in = n.sb("q_in", [D, L])
        qs = n.sb("qs", [L, HEADS, HD0])
        qsq = n.sb("qsq", [L, HEADS, HD0])
        qss = n.sb("qss", [L, HEADS])
        qsd = n.sb("qsd", [L, HEADS])
        qrs = n.sb("qrs", [L, HEADS])
        qn = n.sb("qn", [L, HEADS, HD0])
        qblk = n.sb("qblk", [D, HEADS // 2, 2, L])
        qp = [n.sb(f"qp{u}", [D, HEADS * L]) for u in range(2)]
        p = [n.sb(f"p{j}", [SP_MAX, HALF]) for j in range(4)]
        acc = [n.sb(f"acc{j}", [SP_MAX, HALF]) for j in range(2)]
        oraw = n.sb("oraw", [D, HALF])
        rden = n.sb("rden", [D, HALF])
        onorm = n.sb("onorm", [D, HALF])
        ring = n.ps("ring", 4)
        pvb = n.ps("pvb", 2)
        knb = n.ps("knb", 1)
        qb = n.ps("qb", 1)

        s_ctx = [n.sem(f"s_ctx{u}") for u in range(2)]
        s_qin = n.sem("s_qin")
        s_kn = n.sem("s_kn")
        s_sq = n.sem("s_sq")
        s_ss = n.sem("s_ss")
        s_ksd = n.sem("s_ksd")
        s_krs = n.sem("s_krs")
        s_qunit = n.sem("s_qunit")
        s_qfree = n.sem("s_qfree")
        s_qsq = n.sem("s_qsq")
        s_qss = n.sem("s_qss")
        s_qsd = n.sem("s_qsd")
        s_qrs = n.sem("s_qrs")
        s_qn = n.sem("s_qn")
        s_blk0 = n.sem("s_blk0")
        s_bias = n.sem("s_rowbias")
        s_item = n.sem("s_item")
        s_free = n.sem("s_free")
        s_exp = n.sem("s_exp")
        s_acc = n.sem("s_acc")
        s_pv = n.sem("s_pv")
        s_oraw = n.sem("s_oraw")
        s_rden = n.sem("s_rden")
        s_on = n.sem("s_on")

        ITEMS = NS + 2
        TAIL_ITEM, DEN_ITEM = 2, 15
        item_of = [s if s < 2 else s + 1 if s < 14 else s + 2 for s in range(NS)]
        UNITS = 10

        def unit(b, i):
            if isinstance(b, int) and b >= B - 1 and i > 0 or isinstance(b, int) and b >= B:
                return UNITS * B + (1 if b == B - 1 else 2)  - 1
            return UNITS * (b + 1) + i - 1

        def twice(b, i):
            return 3 if isinstance(b, int) and b == -1 and i == 8 else 1

        block = n.ctx.enter_context(nc.Block())

        @block.sync
        def _(sp):
            def load(b, u):
                sp.dma_start(ctxT[u][:, :], ctxT_d[bass.ds(b, 1), :, :].rearrange("b d s -> (b d) s"))\
                  .then_inc(s_ctx[u], 16)
                sp.dma_start(ctxN[u][0:SP_FULL, :, :].rearrange("p c d -> p (c d)"),
                             ctxN_d[bass.ds(b, 1), 0:SP_FULL * CH * D].rearrange("b (p n) -> (b p) n", p=SP_FULL))\
                  .then_inc(s_ctx[u], 16)
                sp.dma_start(ctxN[u][SP_FULL:SP_MAX, 0:S % CH, :].rearrange("p c d -> p (c d)"),
                             ctxN_d[bass.ds(b, 1), SP_FULL * CH * D:S * D]).then_inc(s_ctx[u], 16)

            load(0, 0)
            load(1, 1)
            with sp.Fori(0, (B - 2) // 2) as i:
                for u in range(2):
                    sp.wait_ge(s_pv, NS * (2 * i + u + 1))
                    load(2 * i + u + 2, u)

        def batches(eng, batch):
            batch(0, 0, 1, tail=False)
            with eng.Fori(0, (B - 2) // 2) as i:
                batch(2 * i + 1, 1, i + 2)
                batch(2 * i + 2, 0, i + 2)
            batch(B - 1, 1, 0, prep=False)

        @block.tensor
        def _(pe):
            def key_norm_unit(j, u, s):
                c = s // 2
                if not (isinstance(j, int) and j == 0 and s == 0):
                    pe.wait_ge(s_sq, NS * j + s)
                pe.matmul(knb[0:rows(c), 0, :], ctxT[u][:, off(c):off(c) + rows(c)],
                          wk[:, 512 * (s % 2):512 * (s % 2) + 512], start=True, stop=True).then_inc(s_kn, 1)

            def qbank(b, i):
                if not (isinstance(b, int) and b == -1 and i == 1):
                    pe.wait_ge(s_qfree, unit(b, i))

            def query_unit(b, i):
                qbank(b, i)
                pe.wait_ge(s_qin, b + 2)
                pe.matmul(qb[0:L, 0, :], q_in[:, :], wq[:, 512 * (i - 1):512 * i],
                          start=True, stop=True).then_inc(s_qunit, 1)

            def turn_unit(b, i):
                qbank(b, i)
                pe.wait_ge(s_qn, b + 2)
                for a in range(4):
                    h = 8 * (i - 3) + 2 * a
                    t = pe.transpose(qb[:, 0, a * L:(a + 1) * L], qn[:, h:h + 2, :].rearrange("l h e -> l (h e)"),
                                     k["ident"][0:L, 0:L])
                t.then_inc(s_qunit, 1)

            def absorb_unit(b, i):
                qbank(b, i)
                for a in range(2):
                    g = 2 * (i - 5) + a
                    t = pe.matmul(qb[:, 0, a * 2 * L:(a + 1) * 2 * L], wkq[:, g, :],
                                  qblk[:, g, :, :].rearrange("p a l -> p (a l)"), start=True, stop=True)
                t.then_inc(s_qunit, twice(b, i))

            def out_unit(b, i, half, done):
                qbank(b, i)
                pe.wait_ge(s_on, done)
                for h in range(8):
                    t = pe.matmul(qb[0:L, 0, 0:D], onorm[:, h * L:(h + 1) * L], wvo[:, 8 * half + h, :],
                                  start=(h == 0), stop=(h == 7))
                t.then_inc(s_qunit, 1)

            def slot(b, i):
                if not (isinstance(b, int) and b == 0 and i < 2):
                    pe.wait_ge(s_free, ITEMS * b + i - 1)
                return 2 * (i % 2)

            def den_item(b, i, half, done):
                r = slot(b, i)
                pe.wait_ge(s_acc, done)
                for a in range(2):
                    t = pe.matmul(ring[:, r + a, 0:4 * L], k["ones"][0:SP_MAX, :],
                                  acc[half][:, a * 4 * L:(a + 1) * 4 * L], start=True, stop=True)
                t.then_inc(s_item, 1)

            def score(b, u, s):
                half, c = s // CH, s % CH
                if c == 0:
                    pe.wait_ge(s_qfree, unit(b - 1, 9 if half else 7))
                r = slot(b, item_of[s])
                for a in range(2):
                    t = pe.matmul(ring[0:rows(c), r + a, 0:4 * L], ctxT[u][:, off(c):off(c) + rows(c)],
                                  qp[u][:, half * HALF + a * 4 * L:half * HALF + (a + 1) * 4 * L],
                                  start=True, stop=True)
                t.then_inc(s_item, 2 if isinstance(b, int) and b == 0 and s == 1 else 1)

            def weigh(b, u, s):
                c = s % CH
                if c == 0 and not (isinstance(b, int) and b == 0 and s == 0):
                    pe.wait_ge(s_oraw, 2 * b + s // CH)
                pe.wait_ge(s_exp, NS * b + s + 1)
                for a in range(2):
                    t = pe.matmul(pvb[:, a, 0:4 * L], ctxN[u][0:rows(c), c, :],
                                  p[s % 4][0:rows(c), a * 4 * L:(a + 1) * 4 * L],
                                  start=(c == 0), stop=(c == CH - 1))
                t.then_inc(s_pv, 1)

            def batch(b, u, nth, prep=True, tail=True):
                if prep:
                    pe.wait_ge(s_ctx[1 - u], 48 * nth)
                for s in range(NS):
                    if s == 2 and tail:
                        den_item(b, TAIL_ITEM, 1, NS * b)
                    if s == 14:
                        den_item(b, DEN_ITEM, 0, NS * b + CH)
                    score(b, u, s)
                    if prep:
                        key_norm_unit(b + 1, 1 - u, s)
                    if s >= 1:
                        weigh(b, u, s - 1)
                    if s == 6 and tail:
                        out_unit(b, 0, 1, 2 * b)
                    if prep and s in (7, 9):
                        query_unit(b, 1 if s == 7 else 2)
                    if prep and s in (15, 16):
                        turn_unit(b, s - 12)
                    if prep and s in (18, 19, 20, 21):
                        absorb_unit(b, s - 13)
                    if s == 22:
                        out_unit(b, 9, 0, 2 * b + 1)
                weigh(b, u, NS - 1)

            pe.wait_ge(s_ctx[0], 48)
            for s in range(NS):
                key_norm_unit(0, 0, s)
            for i in range(1, 9):
                (query_unit if i < 3 else turn_unit if i < 5 else absorb_unit)(-1, i)
            batches(pe, batch)
            den_item(B, 0, 1, NS * B)
            out_unit(B, 0, 1, 2 * B)

        @block.scalar
        def _(act):
            def square(j, s):
                r = rows(s // 2)
                act.wait_ge(s_kn, NS * j + s + 1)
                if not (isinstance(j, int) and j == 0 and s < 2):
                    act.wait_ge(s_ss, NS * j + s - 1)
                act.activation(sq[0:r, s % 2, :], knb[0:r, 0, :], ACT.Square).then_inc(s_sq, 1)

            def query_root(j):
                act.wait_ge(s_qss, j + 1)
                act.activation(qsd[:, :], qss[:, :], ACT.Sqrt, bias=k["eps"][0:L, 0:1],
                               scale=1.0 / HD0).then_inc(s_qsd, 1)

            def key_root(j):
                act.wait_ge(s_ss, NS * (j + 1))
                act.activation(ksd[:, :, :].rearrange("p c h -> p (c h)"), kss[:, :, :].rearrange("p c h -> p (c h)"),
                               ACT.Sqrt, bias=k["eps"][0:SP_MAX, 0:1], scale=1.0 / HD0).then_inc(s_ksd, 1)

            def batch(b, u, nth, prep=True, tail=True):
                for s in range(NS):
                    c = s % CH
                    r = rows(c)
                    if s == 0:
                        act.wait_ge(s_bias, b + 1)
                    act.wait_ge(s_free, ITEMS * b + item_of[s] + 1)
                    act.activation(p[s % 4][0:r, :], p[s % 4][0:r, :], ACT.Exp,
                                   bias=bias[u][0:r, c:c + 1]).then_inc(s_exp, 1)
                    if prep:
                        square(b + 1, s)
                    if prep and s == 12:
                        query_root(b + 1)
                if prep:
                    key_root(b + 1)

            for s in range(NS):
                square(0, s)
            query_root(0)
            key_root(0)
            batches(act, batch)

        @block.gpsimd
        def _(pool):
            def take_tokens(j):
                if not (isinstance(j, int) and j == 0):
                    pool.wait_ge(s_qunit, unit(j - 2, 3))
                pool.tensor_copy(q_in[:, :], xT[:, bass.ds(j * L, L)]).then_inc(s_qin, 1)

            def square_queries(j):
                pool.wait_ge(s_qfree, unit(j - 1, 3))
                pool.tensor_tensor(qsq[:, :, :], qs[:, :, :], qs[:, :, :], ALU.mult).then_inc(s_qsq, 1)

            def batch(b, u, nth, prep=True, tail=True):
                for s in range(NS):
                    half, c = s // CH, s % CH
                    r = rows(c)
                    if prep and s == 1:
                        take_tokens(b + 1)
                    if prep and s == 10:
                        square_queries(b + 1)
                    if c == 0:
                        continue
                    if c == 1:
                        if not (isinstance(b, int) and b == 0):
                            pool.wait_ge(s_item, ITEMS * b + TAIL_ITEM + 1 if half else ITEMS * (b - 1) + DEN_ITEM + 1)
                        pool.wait_ge(s_exp, NS * b + s + 1)
                        pool.tensor_tensor(acc[half][0:r, :], p[(s - 1) % 4][0:r, :], p[s % 4][0:r, :],
                                           ALU.add).then_inc(s_acc, 2)
                    else:
                        pool.wait_ge(s_exp, NS * b + s + 1)
                        pool.wait_ge(s_acc, NS * b + s)
                        pool.tensor_tensor(acc[half][0:r, :], acc[half][0:r, :], p[s % 4][0:r, :],
                                           ALU.add).then_inc(s_acc, 1)

            take_tokens(0)
            square_queries(0)
            batches(pool, batch)

        @block.vector
        def _(dve):
            def sum_squares(j, s):
                r = rows(s // 2)
                dve.wait_ge(s_sq, NS * j + s + 1)
                dve.tensor_reduce(kss[0:r, s // 2, 8 * (s % 2):8 * (s % 2) + 8],
                                  sq[0:r, s % 2, :].rearrange("p (h e) -> p h e", h=8), AX_X,
                                  ALU.add).then_inc(s_ss, 1)

            def take_queries(b, i):
                dve.wait_ge(s_qunit, unit(b, i) + 1)
                dve.tensor_copy(qs[:, 8 * (i - 1):8 * i, :].rearrange("l h e -> l (h e)"),
                                qb[0:L, 0, :]).then_inc(s_qfree, 1)

            def sum_query_squares(j):
                dve.wait_ge(s_qsq, j + 1)
                dve.tensor_reduce(qss[:, :], qsq[:, :, :], AX_X, ALU.add).then_inc(s_qss, 1)

            def norm_queries(j):
                dve.wait_ge(s_qsd, j + 1)
                dve.reciprocal(qrs[:, :], qsd[:, :]).then_inc(s_qrs, 1)
                dve.wait_ge(s_qrs, j + 1)
                dve.tensor_tensor(qn[:, :, :], qs[:, :, :], over_heads(qrs[:, :], HD0), ALU.mult).then_inc(s_qn, 1)

            def take_turned(b, i):
                dve.wait_ge(s_qunit, unit(b, i) + 1)
                src = qb[:, 0, 0:4 * L].rearrange("p (a l) -> p a l", a=4)
                g = 4 * (i - 3)
                dve.tensor_copy(qblk[0:HD0, g:g + 4, 0, :], src[0:HD0])
                dve.tensor_copy(qblk[HD0:D, g:g + 4, 1, :], src[HD0:D]).then_inc(s_qfree, 1)

            def take_absorbed(b, u, i):
                dve.wait_ge(s_qunit, unit(b, i) + 1)
                dve.tensor_copy(qp[u][:, 4 * L * (i - 5):4 * L * (i - 4)], qb[:, 0, 0:4 * L])\
                   .then_inc(s_qfree, twice(b, i))

            def add_out(b, i, to):
                dve.wait_ge(s_qunit, unit(b, i) + 1)
                dve.wait_ge(s_qfree, unit(b, i))
                xb = x[:, bass.ds(to, 1), :].rearrange("l b d -> l (b d)")
                dve.tensor_tensor(xb, xb, qb[0:L, 0, 0:D], ALU.add).then_inc(s_qfree, 1)

            def key_roots(j, u):
                dve.wait_ge(s_ksd, j + 1)
                dve.reciprocal(krs[u][:, :, :], ksd[:, :, :]).then_inc(s_krs, 1)

            def scale_scores(b, u, s):
                half, c = s // CH, s % CH
                r, i = rows(c), item_of[s]
                dve.wait_ge(s_item, ITEMS * b + i + 1)
                if s == 0:
                    dve.wait_ge(s_krs, b + 1)
                if not (isinstance(b, int) and b == 0 and s < 4):
                    dve.wait_ge(s_pv, NS * b + s - 3)
                    dve.wait_ge(s_acc, NS * b + s - 3)
                scale = krs[u][0:r, c, 8 * half:8 * half + 8].rearrange("p (a h) -> p a h", a=2)
                dve.tensor_tensor(p[s % 4][0:r, :].rearrange("p (a h l) -> p a h l", a=2, h=4),
                                  ring[0:r, 2 * (i % 2):2 * (i % 2) + 2, 0:4 * L].rearrange("p a (h l) -> p a h l", h=4),
                                  scale.unsqueeze(3).to_broadcast([r, 2, 4, L]), ALU.mult)\
                   .then_inc(s_free, 2 if isinstance(b, int) and b == 0 and s == 1 else 1)

            def take_bias(j, u):
                if not (isinstance(j, int) and j < 2):
                    dve.wait_ge(s_exp, NS * (j - 1))
                dve.tensor_scalar(bias[u][:, :], k["mask_bias"][:, bass.ds(j, 1), :].rearrange("p b c -> p (b c)"),
                                  0.0, None, ALU.add).then_inc(s_bias, 1)

            def take_sums(b, half):
                dve.wait_ge(s_pv, NS * b + CH * (half + 1))
                dve.tensor_copy(oraw[:, :].rearrange("p (a n) -> p a n", a=2), pvb[:, :, 0:4 * L]).then_inc(s_oraw, 1)

            def norm_sums(b, i, done):
                dve.wait_ge(s_item, ITEMS * b + i + 1)
                r = 2 * (i % 2)
                dve.reciprocal(rden[:, :].rearrange("p (a n) -> p a n", a=2), ring[:, r:r + 2, 0:4 * L])\
                   .then_inc(s_free, 1)
                dve.wait_ge(s_free, ITEMS * b + i + 1)
                dve.wait_ge(s_oraw, done + 1)
                dve.tensor_tensor(onorm[:, :], oraw[:, :], rden[:, :], ALU.mult).then_inc(s_on, 1)

            def batch(b, u, nth, prep=True, tail=True):
                for s in range(NS):
                    if s == 2 and tail:
                        norm_sums(b, TAIL_ITEM, 2 * b - 1)
                    if s == 14:
                        norm_sums(b, DEN_ITEM, 2 * b)
                    scale_scores(b, u, s)
                    if prep and s >= 1:
                        sum_squares(b + 1, s - 1)
                    if prep and s == 5:
                        take_bias(b + 1, 1 - u)
                    if s == 12:
                        take_sums(b, 0)
                    if s == 6 and tail:
                        add_out(b, 0, b - 1)
                    if prep and s in (7, 9):
                        take_queries(b, 1 if s == 7 else 2)
                    if prep and s == 11:
                        sum_query_squares(b + 1)
                    if prep and s == 13:
                        norm_queries(b + 1)
                    if prep and s in (15, 16):
                        take_turned(b, s - 12)
                    if prep and s in (18, 19, 20, 21):
                        take_absorbed(b, 1 - u, s - 13)
                    if s == 22:
                        add_out(b, 9, b)
                if prep:
                    sum_squares(b + 1, NS - 1)
                    key_roots(b + 1, 1 - u)
                take_sums(b, 1)

            dve.memset(qblk[:, :, :, :], 0.0)
            dve.memset(kss[:, :, :], 1.0).then_inc(s_blk0, 1)
            dve.wait_ge(s_blk0, 1)
            take_bias(0, 0)
            for s in range(NS):
                sum_squares(0, s)
            take_queries(-1, 1)
            take_queries(-1, 2)
            sum_query_squares(0)
            norm_queries(0)
            for i in (3, 4):
                take_turned(-1, i)
            for i in (5, 6, 7, 8):
                take_absorbed(-1, 0, i)
            key_roots(0, 0)
            batches(dve, batch)
            norm_sums(B, 0, 2 * B - 1)
            add_out(B, 0, B - 1)



def route(nc, tag, k, x, xT, router, router_row, down_bias, share, pair_softmax):
    with Net(nc) as n:
        def t(name, e=True, dt=F32):
            return n.sb(f"{tag}_{name}", [L, B, E] if e else [L, B], dt)

        lg, hot, best, lg2, ex = t("lg"), t("hot"), t("best"), t("lg2"), t("ex")
        m1, pick, m2, den, rden, gap, egap = [t(v, False) for v in ("m1", "pick", "m2", "den", "rden", "gap", "egap")]
        shareT = n.sb(f"{tag}_shareT", [E, T])
        lgp = n.ps(f"{tag}_lgp", 1)
        shp = n.ps(f"{tag}_shp", 4)
        s_lg = n.sem(f"{tag}_s_lg")
        s_v = n.sem(f"{tag}_s_v")
        s_ex = n.sem(f"{tag}_s_ex")
        s_share = n.sem(f"{tag}_s_share")
        s_turn = n.sem(f"{tag}_s_turn")
        s_st = n.sem(f"{tag}_s_st")
        s_bias = n.sem(f"{tag}_s_bias")
        s_add = n.sem(f"{tag}_s_add")
        wide = [L, B, E]
        block = n.ctx.enter_context(nc.Block())

        @block.tensor
        def _(pe):
            for b in range(B):
                m = pe.matmul(lgp[0:L, 0, b * E:(b + 1) * E], xT[:, b * L:(b + 1) * L], router,
                              start=True, stop=True)
            m.then_inc(s_lg, 1)
            pe.wait_ge(s_share, 1)
            for b in range(B):
                m = pe.transpose(shp[0:E, b // 4, (b % 4) * L:(b % 4 + 1) * L], share[:, b, :],
                                 k["ident"][0:L, 0:L])
                if b % 4 == 3:
                    m.then_inc(s_turn, 1)
            for b in range(B):
                pe.wait_ge(s_st, b // 4 + 1)
                m = pe.matmul(shp[0:L, b // 4, (b % 4) * D:(b % 4 + 1) * D], shareT[:, b * L:(b + 1) * L],
                              down_bias, start=True, stop=True)
                if b % 4 == 3:
                    m.then_inc(s_bias, 1)

        @block.scalar
        def _(act):
            if pair_softmax:
                act.wait_ge(s_v, 9)
                act.activation(egap[:, :], gap[:, :], ACT.Exp).then_inc(s_ex, 1)
            else:
                act.wait_ge(s_v, 10)
                act.activation(ex[:, :, :], lg2[:, :, :], ACT.Exp).then_inc(s_ex, 1)

        @block.vector
        def _(dve):
            step = [0]

            def then(ins):
                step[0] += 1
                ins.then_inc(s_v, 1)
                dve.wait_ge(s_v, step[0])

            dve.wait_ge(s_lg, 1)
            then(dve.tensor_tensor(lg[:, :, :], lgp[0:L, 0, 0:B * E].rearrange("l (b e) -> l b e", b=B),
                                   router_row.unsqueeze(1).to_broadcast(wide), ALU.add))
            rank = k["rank_row"][:, :].unsqueeze(1).to_broadcast(wide)
            then(dve.tensor_reduce(m1[:, :], lg[:, :, :], AX_X, ALU.max))
            then(dve.tensor_tensor(hot[:, :, :], lg[:, :, :], over_heads(m1[:, :], E), ALU.is_ge))
            then(dve.tensor_tensor(hot[:, :, :], hot[:, :, :], rank, ALU.mult))
            then(dve.tensor_reduce(pick[:, :], hot[:, :, :], AX_X, ALU.max))
            then(dve.tensor_tensor(best[:, :, :], hot[:, :, :], over_heads(pick[:, :], E), ALU.is_ge))
            then(dve.scalar_tensor_tensor(out=lg2[:, :, :].rearrange("l b e -> l (b e)"),
                                          in0=best[:, :, :].rearrange("l b e -> l (b e)"), scalar=-1e30,
                                          in1=lg[:, :, :].rearrange("l b e -> l (b e)"),
                                          op0=ALU.mult, op1=ALU.add))
            then(dve.tensor_reduce(m2[:, :], lg2[:, :, :], AX_X, ALU.max))
            if pair_softmax:
                then(dve.tensor_tensor(gap[:, :], m2[:, :], m1[:, :], ALU.subtract))
                then(dve.tensor_tensor(hot[:, :, :], lg2[:, :, :], over_heads(m2[:, :], E), ALU.is_ge))
            else:
                then(dve.tensor_tensor(hot[:, :, :], lg2[:, :, :], over_heads(m2[:, :], E), ALU.is_ge))
                then(dve.tensor_tensor(lg2[:, :, :], lg[:, :, :], over_heads(m1[:, :], E), ALU.subtract))
            then(dve.tensor_tensor(hot[:, :, :], hot[:, :, :], rank, ALU.mult))
            then(dve.tensor_reduce(pick[:, :], hot[:, :, :], AX_X, ALU.max))
            then(dve.tensor_tensor(hot[:, :, :], hot[:, :, :], over_heads(pick[:, :], E), ALU.is_ge))
            dve.wait_ge(s_ex, 1)
            if pair_softmax:
                then(dve.tensor_scalar(den[:, :], egap[:, :], 1.0, None, ALU.add))
                then(dve.reciprocal(rden[:, :], den[:, :]))
                then(dve.tensor_tensor(hot[:, :, :], hot[:, :, :], over_heads(egap[:, :], E), ALU.mult))
                then(dve.tensor_tensor(hot[:, :, :], hot[:, :, :], best[:, :, :], ALU.add))
                dve.tensor_tensor(share[:, :, :], hot[:, :, :], over_heads(rden[:, :], E), ALU.mult).then_inc(s_share, 1)
            else:
                then(dve.tensor_reduce(den[:, :], ex[:, :, :], AX_X, ALU.add))
                then(dve.reciprocal(rden[:, :], den[:, :]))
                then(dve.tensor_tensor(hot[:, :, :], hot[:, :, :], best[:, :, :], ALU.add))
                then(dve.tensor_tensor(hot[:, :, :], hot[:, :, :], ex[:, :, :], ALU.mult))
                dve.tensor_tensor(share[:, :, :], hot[:, :, :], over_heads(rden[:, :], E), ALU.mult).then_inc(s_share, 1)
            for g in range(4):
                dve.wait_ge(s_turn, g + 1)
                dve.tensor_copy(shareT[:, 4 * g * L:4 * (g + 1) * L], shp[0:E, g, 0:4 * L]).then_inc(s_st, 1)
            for g in range(4):
                dve.wait_ge(s_bias, g + 1)
                xg = x[:, 4 * g:4 * g + 4, :].rearrange("l b d -> l (b d)")
                dve.tensor_tensor(xg, xg, shp[0:L, g, :], ALU.add).then_inc(s_add, 1)


def down_and_share(n, pe, down, e_slot, hid, weight, chunks):
    for a in range(4):
        for j in range(chunks):
            t = pe.matmul(down[0:L, e_slot, a * D:(a + 1) * D], hid[:, j, a * L:(a + 1) * L], weight[:, j, :],
                          start=(j == 0), stop=(j == chunks - 1))
    return t


def add_shares(dve, s_share, s_free, count, down, slot, x, share, g, e):
    dve.wait_ge(s_free, count)
    for a in range(4):
        xb = x[:, bass.ds(4 * g + a, 1), :].rearrange("l b d -> l (b d)")
        t = dve.scalar_tensor_tensor(out=xb, in0=down[0:L, slot, a * D:(a + 1) * D],
                                     scalar=share[:, bass.ds(4 * g + a, 1), e], in1=xb,
                                     op0=ALU.mult, op1=ALU.add)
    t.then_inc(s_free, 1)


def gated_experts(nc, k, x, xT, w_up, b_up, w_down, share):
    N = 4 * L
    with Net(nc) as n:
        hid_ps = n.ps("ge_hid", 4)
        down = n.ps("ge_down", 2)
        gate = n.sb("gate", [D, 2, N])
        up = n.sb("up", [D, 2, N])
        sig = n.sb("sig", [D, 2, N])
        glu = n.sb("glu", [D, 2, N])
        hid = [n.sb(f"ge_hid{i}", [D, 2, N]) for i in range(2)]
        s_mm = n.sem("ge_mm")
        s_gate = n.sem("ge_gate")
        s_up = n.sem("ge_up")
        s_sig = n.sem("ge_sig")
        s_clip = n.sem("ge_clip")
        s_glu = n.sem("ge_glu")
        s_hid = n.sem("ge_hid_s")
        s_down = n.sem("ge_down_s")
        s_dfree = n.sem("ge_dfree")
        s_pre = n.sem("ge_pre")
        U = 2 * E
        block = n.ctx.enter_context(nc.Block())

        def groups(eng, group):
            group(0)
            with eng.Fori(1, 4) as g:
                group(g)

        @block.tensor
        def _(pe):
            def group(g):
                def downs(e):
                    pe.wait_ge(s_hid, U * g + 2 * e + 2)
                    if not (isinstance(g, int) and e < 2):
                        pe.wait_ge(s_dfree, E * g + e - 1)
                    down_and_share(n, pe, down, e % 2, hid[e % 2], w_down[:, e, :, :], 2).then_inc(s_down, 1)

                for e in range(E):
                    for j in range(2):
                        u = 2 * e + j
                        if not (isinstance(g, int) and u < 2):
                            pe.wait_ge(s_gate, U * g + u - 1)
                            pe.wait_ge(s_up, U * g + u - 1)
                        for v in range(2):
                            t = pe.matmul(hid_ps[:, 2 * (u % 2) + v, 0:N],
                                          w_up[:, e, v * I0 + j * D:v * I0 + (j + 1) * D],
                                          xT[:, bass.ds(g * N, N)], start=True, stop=True)
                        t.then_inc(s_mm, 1)
                    if e:
                        downs(e - 1)
                downs(E - 1)
            groups(pe, group)

        @block.scalar
        def _(act):
            def group(g):
                for u in range(U):
                    act.wait_ge(s_mm, U * g + u + 1)
                    if not (isinstance(g, int) and u < 2):
                        act.wait_ge(s_hid, U * g + u - 1)
                    act.activation(up[:, u % 2, :], hid_ps[:, 2 * (u % 2) + 1, 0:N], ACT.Identity,
                                   bias=b_up[:, u // 2, 2 + u % 2:3 + u % 2]).then_inc(s_up, 1)
                    act.wait_ge(s_gate, U * g + u + 1)
                    act.activation(sig[:, u % 2, :], gate[:, u % 2, :], ACT.Sigmoid, scale=1.702).then_inc(s_sig, 1)
            groups(act, group)

        @block.gpsimd
        def _(pool):
            def group(g):
                for u in range(U):
                    pool.wait_ge(s_sig, U * g + u + 1)
                    pool.tensor_tensor(glu[:, u % 2, :], gate[:, u % 2, :], sig[:, u % 2, :], ALU.mult).then_inc(s_glu, 1)
            groups(pool, group)

        @block.vector
        def _(dve):
            def group(g):
                def first(u):
                    dve.wait_ge(s_mm, U * g + u + 1)
                    if not (isinstance(g, int) and u < 2):
                        dve.wait_ge(s_glu, U * g + u - 1)
                    dve.tensor_scalar(gate[:, u % 2, :], hid_ps[:, 2 * (u % 2), 0:N],
                                      b_up[:, u // 2, u % 2:u % 2 + 1], 7.0, ALU.add, ALU.min).then_inc(s_gate, 1)
                    dve.wait_ge(s_up, U * g + u + 1)
                    dve.tensor_scalar(up[:, u % 2, :], up[:, u % 2, :], 7.0, -7.0, ALU.min, ALU.max).then_inc(s_clip, 1)

                def second(u):
                    dve.wait_ge(s_glu, U * g + u + 1)
                    dve.wait_ge(s_clip, U * g + u + 1)
                    e = u // 2
                    if not (isinstance(g, int) and e < 2):
                        dve.wait_ge(s_down, E * g + e - 1)
                    dve.scalar_tensor_tensor(out=hid[e % 2][:, u % 2, :], in0=up[:, u % 2, :], scalar=1.0,
                                             in1=glu[:, u % 2, :], op0=ALU.add, op1=ALU.mult).then_inc(s_hid, 1)

                def shares(e):
                    dve.wait_ge(s_down, E * g + e + 1)
                    add_shares(dve, None, s_dfree, E * g + e, down, e % 2, x, share, g, e) if not (
                        isinstance(g, int) and e == 0) else add_first(e)

                def add_first(e):
                    for a in range(4):
                        t = dve.scalar_tensor_tensor(out=x[:, a, :], in0=down[0:L, 0, a * D:(a + 1) * D],
                                                     scalar=share[:, a, e:e + 1], in1=x[:, a, :],
                                                     op0=ALU.mult, op1=ALU.add)
                    t.then_inc(s_dfree, 1)

                for u in range(U):
                    first(u)
                    if u:
                        second(u - 1)
                    if u >= 4 and u % 2 == 0:
                        shares(u // 2 - 2)
                second(U - 1)
                shares(E - 2)
                shares(E - 1)
            groups(dve, group)


def relu_experts(nc, k, x, xT, w_up, b_up, w_down, share):
    N = 4 * L
    with Net(nc) as n:
        hid_ps = n.ps("re_hid", 4)
        down = n.ps("re_down", 2)
        hid = [n.sb(f"re_hid{i}", [D, 4, N]) for i in range(2)]
        s_mm = n.sem("re_mm")
        s_hid = n.sem("re_hid_s")
        s_down = n.sem("re_down_s")
        s_dfree = n.sem("re_dfree")
        U = 4 * E
        block = n.ctx.enter_context(nc.Block())

        def groups(eng, group):
            group(0)
            with eng.Fori(1, 4) as g:
                group(g)

        @block.tensor
        def _(pe):
            def group(g):
                def downs(e):
                    pe.wait_ge(s_hid, U * g + 4 * e + 4)
                    if not (isinstance(g, int) and e < 2):
                        pe.wait_ge(s_dfree, E * g + e - 1)
                    down_and_share(n, pe, down, e % 2, hid[e % 2], w_down[:, e, :, :], 4).then_inc(s_down, 1)

                for e in range(E):
                    for j in range(4):
                        u = 4 * e + j
                        if not (isinstance(g, int) and u < 4):
                            pe.wait_ge(s_hid, U * g + u - 3)
                        pe.matmul(hid_ps[:, j, 0:N], w_up[:, e, j * D:(j + 1) * D],
                                  xT[:, bass.ds(g * N, N)], start=True, stop=True).then_inc(s_mm, 1)
                    if e:
                        downs(e - 1)
                downs(E - 1)
            groups(pe, group)

        @block.scalar
        def _(act):
            def group(g):
                for u in range(U):
                    e, j = u // 4, u % 4
                    act.wait_ge(s_mm, U * g + u + 1)
                    if not (isinstance(g, int) and e < 2):
                        act.wait_ge(s_down, E * g + e - 1)
                    act.activation(hid[e % 2][:, j, :], hid_ps[:, j, 0:N], ACT.Relu,
                                   bias=b_up[:, e, j:j + 1]).then_inc(s_hid, 1)
            groups(act, group)

        @block.vector
        def _(dve):
            def group(g):
                for e in range(E):
                    dve.wait_ge(s_down, E * g + e + 1)
                    if not (isinstance(g, int) and e == 0):
                        dve.wait_ge(s_dfree, E * g + e)
                    for a in range(4):
                        xb = x[:, bass.ds(4 * g + a, 1), :].rearrange("l b d -> l (b d)")
                        t = dve.scalar_tensor_tensor(out=xb, in0=down[0:L, e % 2, a * D:(a + 1) * D],
                                                     scalar=share[:, bass.ds(4 * g + a, 1), e], in1=xb,
                                                     op0=ALU.mult, op1=ALU.add)
                    t.then_inc(s_dfree, 1)
            groups(dve, group)



def linear_attention(nc, k, x, xT):
    W = D + 1
    WO = D + HEADS
    with Net(nc) as n:
        qlow = n.sb("la_qlow", [D, T])
        qT = n.sb("la_qT", [D, T])
        kf = n.sb("la_kf", [L, B, D])
        klow = n.sb("la_klow", [L, B, D])
        v1 = n.sb("la_v", [L, B, W])
        kv = n.sb("la_kv", [D, B, WO])
        o = n.sb("la_o", [L, B, D])
        nrm = n.sb("la_nrm", [L, B, HEADS])
        rnrm = n.sb("la_rnrm", [L, B, HEADS])
        banks = n.ps("la_banks", 8)
        s_q = n.sem("la_s_q")
        s_qe = n.sem("la_s_qe")
        s_qx = n.sem("la_s_qx")
        s_kvp = n.sem("la_s_kvp")
        s_ke = n.sem("la_s_ke")
        s_kx = n.sem("la_s_kx")
        s_f = n.sem("la_s_f")
        s_kvm = n.sem("la_s_kvm")
        s_kve = n.sem("la_s_kve")
        s_o = n.sem("la_s_o")
        s_oe = n.sem("la_s_oe")
        s_turn = n.sem("la_s_turn")
        s_te = n.sem("la_s_te")
        s_one = n.sem("la_s_one")
        block = n.ctx.enter_context(nc.Block())

        @block.tensor
        def _(pe):
            for g in range(4):
                pe.matmul(banks[:, g, 0:4 * L], k["wq1"][:, :], xT[:, 4 * g * L:4 * (g + 1) * L],
                          start=True, stop=True).then_inc(s_q, 1)
            for b in range(B):
                if b % 2 == 0 and b >= 8:
                    pe.wait_ge(s_ke, 2 * (b // 2 - 4) + 2)
                t = pe.matmul(banks[0:L, 4 + b // 2 % 4, (b % 2) * 2 * D:(b % 2 + 1) * 2 * D],
                              xT[:, b * L:(b + 1) * L], k["wkv1"][:, :], start=True, stop=True)
                if b % 2:
                    t.then_inc(s_kvp, 1)
            pe.wait_ge(s_f, 2)
            pe.wait_ge(s_qe, 8)
            for b in range(B):
                t = pe.matmul(banks[:, b // 3, (b % 3) * W:(b % 3 + 1) * W], kf[:, b, :], v1[:, b, :],
                              start=True, stop=True)
                if b % 3 == 2 or b == B - 1:
                    t.then_inc(s_kvm, 1)
            for b in range(B):
                if b % 3 == 0:
                    pe.wait_ge(s_kve, min(b + 3, B))
                t = pe.matmul(banks[0:L, b // 3, (b % 3) * WO:(b % 3 + 1) * WO], qT[:, b * L:(b + 1) * L],
                              kv[:, b, :], start=True, stop=True)
                if b % 3 == 2 or b == B - 1:
                    t.then_inc(s_o, 1)
            for b in range(B):
                if b % 4 == 0:
                    pe.wait_ge(s_oe, 6)
                t = pe.transpose(banks[:, b // 4, (b % 4) * L:(b % 4 + 1) * L], o[:, b, :], k["ident"][0:L, 0:L])
                if b % 4 == 3:
                    t.then_inc(s_turn, 1)

        @block.scalar
        def _(act):
            for g in range(4):
                act.wait_ge(s_qe, 2 * g + 2)
                act.activation(qlow[:, 4 * g * L:4 * (g + 1) * L], qlow[:, 4 * g * L:4 * (g + 1) * L],
                               ACT.Exp).then_inc(s_qx, 1)
            act.wait_ge(s_f, 1)
            act.activation(klow[:, :, :], klow[:, :, :], ACT.Exp).then_inc(s_kx, 1)
            for g in range(4):
                act.wait_ge(s_turn, g + 1)
                act.activation(xT[:, 4 * g * L:4 * (g + 1) * L], banks[:, g, 0:4 * L], ACT.Copy).then_inc(s_te, 1)

        @block.vector
        def _(dve):
            dve.memset(v1[:, :, D:W], 1.0).then_inc(s_one, 1)
            for g in range(4):
                cols = slice(4 * g * L, 4 * (g + 1) * L)
                dve.wait_ge(s_q, g + 1)
                dve.tensor_scalar(qT[:, cols], banks[:, g, 0:4 * L], k["bq1"][:, 0:1], 0.0, ALU.add,
                                  ALU.max).then_inc(s_qe, 1)
                dve.tensor_scalar(qlow[:, cols], banks[:, g, 0:4 * L], k["bq1"][:, 0:1], 0.0, ALU.add,
                                  ALU.min).then_inc(s_qe, 1)
            for r in range(B // 2):
                dve.wait_ge(s_kvp, r + 1)
                bank = banks[0:L, 4 + r % 4, :].rearrange("l (b m) -> l b m", b=2)
                dve.tensor_tensor(kf[:, 2 * r:2 * r + 2, :], bank[:, :, 0:D],
                                  k["bk1_row"][:, :].unsqueeze(1).to_broadcast([L, 2, D]), ALU.add).then_inc(s_ke, 1)
                dve.tensor_tensor(v1[:, 2 * r:2 * r + 2, 0:D], bank[:, :, D:2 * D],
                                  k["bv1_row"][:, :].unsqueeze(1).to_broadcast([L, 2, D]), ALU.add).then_inc(s_ke, 1)
            dve.wait_ge(s_ke, B)
            dve.tensor_scalar(klow[:, :, :], kf[:, :, :], 0.0, None, ALU.min).then_inc(s_f, 1)
            for g in range(4):
                cols = slice(4 * g * L, 4 * (g + 1) * L)
                dve.wait_ge(s_qx, g + 1)
                dve.tensor_tensor(qT[:, cols], qT[:, cols], qlow[:, cols], ALU.add).then_inc(s_one, 1)
            dve.wait_ge(s_kx, 1)
            dve.scalar_tensor_tensor(out=kf[:, :, :].rearrange("l b d -> l (b d)"),
                                     in0=kf[:, :, :].rearrange("l b d -> l (b d)"), scalar=0.0,
                                     in1=klow[:, :, :].rearrange("l b d -> l (b d)"),
                                     op0=ALU.max, op1=ALU.add).then_inc(s_f, 1)
            for b in range(B):
                dve.wait_ge(s_kvm, b // 3 + 1)
                m = banks[:, b // 3, (b % 3) * W:(b % 3 + 1) * W]
                dve.tensor_tensor(kv[:, b, 0:D], m[:, 0:D], k["same_head"][:, :], ALU.mult)
                dve.tensor_scalar(kv[:, b, D:WO], k["head_of"][:, :], m[:, D:W], None, ALU.mult).then_inc(s_kve, 1)
            for r in range(6):
                nb = min(3, B - 3 * r)
                dve.wait_ge(s_o, r + 1)
                src = banks[0:L, r, 0:nb * WO].rearrange("l (b m) -> l b m", b=nb)
                rows_ = slice(3 * r, 3 * r + nb)
                dve.tensor_scalar(nrm[:, rows_, :], src[:, :, D:WO], 1e-6, None, ALU.add).then_inc(s_one, 1)
                dve.wait_ge(s_one, 6 + 2 * r)
                dve.reciprocal(rnrm[:, rows_, :], nrm[:, rows_, :]).then_inc(s_one, 1)
                dve.wait_ge(s_one, 7 + 2 * r)
                for b in range(nb):
                    t = dve.tensor_tensor(o[:, 3 * r + b, :].rearrange("l (h d) -> l h d", h=HEADS),
                                          src[:, b, 0:D].rearrange("l (h d) -> l h d", h=HEADS),
                                          over_heads(rnrm[:, 3 * r + b, :], HD1), ALU.mult)
                t.then_inc(s_oe, 1)



def cross_attention_1(nc, k, ctxT_d, x, xT):
    NS = 2 * CH
    TILES = -(-HEADS * L // D)
    THIRDS = [(off(0), off(4)), (off(4), off(8)), (off(8), S)]
    with Net(nc) as n:
        ctxT = [n.sb(f"c1_ctxT{u}", [D, S]) for u in range(2)]
        kT = [n.sb(f"c1_kT{u}", [D, S]) for u in range(2)]
        k16 = n.sb("c1_k16", [D, S], BF16)
        v = [n.sb(f"c1_v{u}", [SP_MAX, CH, D]) for u in range(2)]
        qT = n.sb("c1_qT", [D, L])
        qblk = [n.sb(f"c1_qblk{u}", [D, HEADS, L]) for u in range(2)]
        q16 = n.sb("c1_q16", [D, HEADS * L], BF16)
        mx = n.sb("c1_mx", [D, TILES, 3])
        negmx = n.sb("c1_negmx", [D, TILES])
        neg16 = n.sb("c1_neg16", [TILES, D], BF16)
        negrow = [n.sb(f"c1_negrow{u}", [1, TILES * D], BF16) for u in range(2)]
        p = [n.sb(f"c1_p{j}", [SP_MAX, HALF]) for j in range(4)]
        osum = n.sb("c1_osum", [D, 4, L])
        rden = n.sb("c1_rden", [D, 4, L])
        cat = n.sb("c1_cat", [D, L])
        ring = n.ps("c1_ring", 4)
        pvb = n.ps("c1_pvb", 1)
        denb = n.ps("c1_denb", 1)
        aux = n.ps("c1_aux", 2)

        s_ctx = [n.sem(f"c1_s_ctx{u}") for u in range(2)]
        s_unit = n.sem("c1_s_unit")
        s_ufree = n.sem("c1_s_ufree")
        s_k16 = n.sem("c1_s_k16")
        s_qT = n.sem("c1_s_qT")
        s_qblk = n.sem("c1_s_qblk")
        s_q16 = n.sem("c1_s_q16")
        s_neg = n.sem("c1_s_neg")
        s_row = n.sem("c1_s_row")
        s_score = n.sem("c1_s_score")
        s_exp = n.sem("c1_s_exp")
        s_pv = n.sem("c1_s_pv")
        s_take = n.sem("c1_s_take")
        s_fin = n.sem("c1_s_fin")
        s_cat = n.sem("c1_s_cat")
        s_one = n.sem("c1_s_one")

        UNITS, TAIL, MAXIMA, TURN = 48, 7, 8, 47

        def unit(b, i):
            if isinstance(b, int) and b >= B - 1:
                return UNITS * B + b - (B - 1)
            return UNITS * (b + 1) + i

        def twice(b, i):
            return 2 if isinstance(b, int) and b <= 0 and i == TAIL - 1 else 1

        plan = {0: [0, 1], 1: [2, 3], 2: [4, 5], 3: [6], 4: [TAIL], 19: [TURN]}
        for s in range(5, 18):
            plan[s] = [MAXIMA + 3 * (s - 5) + j for j in range(3)]
        first_plan = [i for i in range(UNITS) if i != TAIL]

        block = n.ctx.enter_context(nc.Block())

        def batches(eng, batch):
            batch(0, 0, 1, tail=False)
            with eng.Fori(0, (B - 2) // 2) as i:
                batch(2 * i + 1, 1, i + 2)
                batch(2 * i + 2, 0, i + 2)
            batch(B - 1, 1, 0, prep=False)

        def planned(s, prep, tail):
            for i in plan.get(s, []):
                if tail if i == TAIL else prep:
                    yield i

        @block.sync
        def _(sp):
            def load(b, u):
                sp.dma_start(ctxT[u][:, :], ctxT_d[bass.ds(b, 1), :, :].rearrange("b d s -> (b d) s"))\
                  .then_inc(s_ctx[u], 16)

            def send_row(b, u):
                sp.wait_ge(s_ufree, unit(b - 1, TURN) + 1)
                sp.dma_start(negrow[u][:, :].rearrange("a (t p) -> a t p", t=TILES),
                             neg16[:, :]).then_inc(s_row, 16)

            load(0, 0)
            load(1, 1)
            send_row(0, 0)
            with sp.Fori(0, (B - 2) // 2) as i:
                for u in range(2):
                    b = 2 * i + u
                    sp.wait_ge(s_unit, unit(b - 1, TAIL))
                    load(b + 2, u)
                    send_row(b + 1, 1 - u)
            send_row(B - 1, 1)

        @block.tensor
        def _(pe):
            def do(b, u, i):
                before = unit(b, i)
                last = isinstance(b, int) and b >= B - 1
                if last:
                    pe.wait_ge(s_ufree, before)
                elif not (isinstance(b, int) and b == -1 and i < 2):
                    pe.wait_ge(s_ufree, before - 1)
                bank = i % 2
                if i < 3:
                    lo, hi = THIRDS[i]
                    t = pe.matmul(aux[:, bank, 0:hi - lo], k["wk2"][:, :], ctxT[u][:, lo:hi], start=True, stop=True)
                elif i == 3:
                    t = pe.matmul(aux[:, bank, 0:L], k["wq2"][:, :], xT[:, bass.ds((b + 1) * L, L)],
                                  start=True, stop=True)
                elif i < TAIL:
                    for a in range(4):
                        c = 4 * (i - 4) + a
                        t = pe.matmul(aux[0:rows(c), bank, a * D:(a + 1) * D], ctxT[u][:, off(c):off(c) + rows(c)],
                                      k["wv2"][:, :], start=True, stop=True)
                elif i == TAIL:
                    pe.wait_ge(s_cat, b)
                    t = pe.matmul(aux[0:L, bank, 0:D], cat[:, :], k["wo2T"][:, :], start=True, stop=True)
                elif i < TURN:
                    t_, part = (i - MAXIMA) // 3, (i - MAXIMA) % 3
                    lo, hi = THIRDS[part]
                    if i == MAXIMA:
                        pe.wait_ge(s_k16, b + 2)
                        pe.wait_ge(s_q16, b + 2)
                    m = min(D, HEADS * L - t_ * D)
                    t = pe.matmul(aux[0:m, bank, 0:hi - lo], q16[:, t_ * D:t_ * D + m], k16[:, lo:hi],
                                  start=True, stop=True)
                else:
                    pe.wait_ge(s_neg, b + 2)
                    t = pe.transpose(aux[0:TILES, bank, 0:D], negmx[:, :], k["ident"][:, :])
                t.then_inc(s_unit, twice(b, i))

            def score(b, u, s):
                half, c = s // CH, s % CH
                r = rows(c)
                if s == 0:
                    pe.wait_ge(s_row, 16 * (b + 1))
                    pe.wait_ge(s_qblk, b + 1)
                if not (isinstance(b, int) and b == 0 and s < 2):
                    pe.wait_ge(s_exp, NS * b + s - 1)
                for a in range(2):
                    g = 2 * half + a
                    dst = ring[0:r, 2 * (s % 2) + a, 0:4 * L]
                    pe.matmul(dst, k["ones16"][0:1, 0:r], negrow[u][0:1, 4 * g * L:4 * (g + 1) * L],
                              start=True, stop=False)
                    t = pe.matmul(dst, kT[u][:, off(c):off(c) + r],
                                  qblk[u][:, 4 * g:4 * g + 4, :].rearrange("p h l -> p (h l)"),
                                  start=False, stop=True)
                t.then_inc(s_score, 1)

            def weigh(b, u, s):
                half, c = s // CH, s % CH
                r = rows(c)
                if c == 0 and not (isinstance(b, int) and b == 0):
                    pe.wait_ge(s_take, 2 * b + half - 1)
                pe.wait_ge(s_exp, NS * b + s + 1)
                st, sp_ = c == 0, c == CH - 1
                for a in range(2):
                    g = 2 * half + a
                    pe.matmul(pvb[32 * g:32 * g + 32, 0, 0:4 * L], v[u][0:r, c, 32 * g:32 * g + 32],
                              p[s % 4][0:r, a * 4 * L:(a + 1) * 4 * L], start=st, stop=sp_)
                for a in range(2):
                    q = (2 * half + a + 2) % 4
                    t = pe.matmul(denb[32 * q:32 * q + 32, 0, 0:4 * L], k["ones"][0:r, 0:32],
                                  p[s % 4][0:r, a * 4 * L:(a + 1) * 4 * L], start=st, stop=sp_)
                t.then_inc(s_pv, 1)

            def batch(b, u, nth, prep=True, tail=True):
                if prep:
                    pe.wait_ge(s_ctx[1 - u], 16 * nth)
                for s in range(NS):
                    score(b, u, s)
                    if s >= 1:
                        weigh(b, u, s - 1)
                    for i in planned(s, prep, tail):
                        do(b, 1 - u, i)
                weigh(b, u, NS - 1)

            pe.wait_ge(s_ctx[0], 16)
            for i in first_plan:
                do(-1, 0, i)
            batches(pe, batch)
            do(B, 0, TAIL)

        @block.scalar
        def _(act):
            def narrow(j, u):
                act.wait_ge(s_ufree, unit(j - 1, 3))
                act.activation(k16[:, :], kT[u][:, :], ACT.Copy).then_inc(s_k16, 1)
                act.wait_ge(s_qblk, j + 1)
                act.activation(q16[:, :], qblk[u][:, :, :].rearrange("p h l -> p (h l)"), ACT.Copy).then_inc(s_q16, 1)

            def batch(b, u, nth, prep=True, tail=True):
                for s in range(NS):
                    r = rows(s % CH)
                    act.wait_ge(s_score, NS * b + s + 1)
                    if not (isinstance(b, int) and b == 0 and s < 4):
                        act.wait_ge(s_pv, NS * b + s - 3)
                    act.activation(p[s % 4][0:r, :].rearrange("p (a n) -> p a n", a=2),
                                   ring[0:r, 2 * (s % 2):2 * (s % 2) + 2, 0:4 * L], ACT.Exp).then_inc(s_exp, 1)
                    if prep and s == 2:
                        narrow(b + 1, 1 - u)

            narrow(0, 0)
            batches(act, batch)

        @block.vector
        def _(dve):
            def take(b, u, i):
                last = isinstance(b, int) and b >= B - 1
                dve.wait_ge(s_unit, unit(b, i) + 1)
                bank = aux[:, i % 2, :]
                j = b + 1
                if i < 3:
                    lo, hi = THIRDS[i]
                    dve.tensor_scalar(kT[u][:, lo:hi], bank[:, 0:hi - lo], k["bk2"][:, 0:1], None,
                                      ALU.add).then_inc(s_ufree, 1)
                elif i == 3:
                    dve.tensor_scalar(qT[:, :], bank[:, 0:L], k["bq2"][:, 0:1], HD1 ** -0.5, ALU.add,
                                      ALU.mult).then_inc(s_ufree, 1)
                    dve.wait_ge(s_ufree, unit(b, i) + 1)
                    dve.tensor_tensor(qblk[u][:, :, :], over_heads(k["head_of"][:, :], L),
                                      qT[:, :].unsqueeze(1).to_broadcast([D, HEADS, L]), ALU.mult).then_inc(s_qblk, 1)
                elif i < TAIL:
                    for full, lo, hi in ((True, 0, 4),):
                        c = 4 * (i - 4)
                        r = rows(c)
                        dve.tensor_copy(v[u][0:r, c:c + 4, :].rearrange("p c d -> p (c d)"), bank[0:r, :])\
                           .then_inc(s_ufree, twice(b, i))
                elif i == TAIL:
                    xb = x[:, bass.ds(b - 1, 1), :].rearrange("l b d -> l (b d)")
                    dve.tensor_tensor(xb, xb, bank[0:L, 0:D], ALU.add).then_inc(s_ufree, 1)
                elif i < TURN:
                    t_, part = (i - MAXIMA) // 3, (i - MAXIMA) % 3
                    lo, hi = THIRDS[part]
                    m = min(D, HEADS * L - t_ * D)
                    dve.tensor_reduce(mx[0:m, t_, part:part + 1], bank[0:m, 0:hi - lo], AX_X,
                                      ALU.max).then_inc(s_ufree, 1)
                    if i == TURN - 1:
                        dve.wait_ge(s_ufree, unit(b, i) + 1)
                        dve.tensor_reduce(negmx[:, :], mx[:, :, :], AX_X, ALU.max, negate=True).then_inc(s_neg, 1)
                else:
                    if not (isinstance(b, int) and b == -1):
                        dve.wait_ge(s_row, 16 * j)
                    dve.tensor_copy(neg16[:, :], bank[0:TILES, 0:D]).then_inc(s_ufree, 1)

            def take_half(b, half):
                lo = 64 * half
                dve.wait_ge(s_pv, NS * b + CH * (half + 1))
                dve.tensor_copy(osum[lo:lo + 64, :, :].rearrange("p j l -> p (j l)"), pvb[lo:lo + 64, 0, 0:4 * L])
                dve.reciprocal(rden[lo:lo + 64, :, :].rearrange("p j l -> p (j l)"),
                               denb[64 - lo:128 - lo, 0, 0:4 * L]).then_inc(s_take, 1)

            def finish(b):
                dve.wait_ge(s_take, 2 * b + 2)
                dve.tensor_tensor(osum[:, :, :], osum[:, :, :], rden[:, :, :], ALU.mult).then_inc(s_fin, 1)
                dve.wait_ge(s_fin, 3 * b + 1)
                dve.tensor_tensor(osum[:, :, :], osum[:, :, :], over_heads(k["head_in_four"][:, :], L),
                                  ALU.mult).then_inc(s_fin, 1)
                dve.wait_ge(s_fin, 3 * b + 2)
                dve.tensor_reduce(cat[:, :], osum[:, :, :].rearrange("p j l -> p l j"), AX_X, ALU.add).then_inc(s_fin, 1)
                dve.wait_ge(s_fin, 3 * b + 3)
                dve.tensor_scalar(cat[:, :], cat[:, :], k["bv2"][:, 0:1], None, ALU.add).then_inc(s_cat, 1)

            def batch(b, u, nth, prep=True, tail=True):
                for s in range(NS):
                    if s == 13:
                        take_half(b, 0)
                    for i in planned(s, prep, tail):
                        take(b, 1 - u, i)
                take_half(b, 1)
                finish(b)

            dve.memset(mx[:, :, :], 0.0).then_inc(s_one, 1)
            dve.tensor_tensor(x[:, :, :], x[:, :, :], k["bo2_row"][:, :].unsqueeze(1).to_broadcast([L, B, D]),
                              ALU.add).then_inc(s_one, 1)
            dve.wait_ge(s_one, 2)
            for i in first_plan:
                take(-1, 0, i)
            batches(dve, batch)
            take(B, 0, TAIL)



def decoder(nc, a, out, upto=99):
    with Net(nc) as n:
        def load(name, shape, src=None, dt=F32):
            t = n.sb(name, shape, dt)
            pairs.append((t[tuple(slice(None) for _ in shape)], a[name] if src is None else src))
            return t

        def row(name, m):
            return load(name, [L if m != HD0 else SP_MAX, m], a[name].partition_broadcast(L if m != HD0 else SP_MAX))

        pairs = []
        k = {}
        k["norms"] = k["projects"] = 0
        k["norm_sems"] = [n.sem(f"s_{v}") for v in ("stats", "sd", "rstd", "normed", "turned", "evacuated", "out")]
        k["project_sems"] = [n.sem(f"s_{v}") for v in ("product", "bias", "sum")]
        k["ones"] = n.sb("ones", [D, D])
        k["ones16"] = n.sb("ones16", [1, D], BF16)
        k["eps"] = n.sb("eps", [D, 1])
        k["mask_bias"] = n.sb("mask_bias", [SP_MAX, B, CH])
        x = load("x", [L, B, D])
        k["ident"] = load("ident", [D, D])
        k["row_of"] = load("row_of", [SP_MAX, CH])
        k["lens"] = load("lens", [SP_MAX, B], a["lens"].partition_broadcast(SP_MAX), I32)
        for name in ("decay", "bg", "br", "ln_w", "ln_b", "qnw", "knw"):
            k[name] = load(name, [D, 1])
        for name in ("bq1", "bk2", "bq2", "bv2"):
            k[name] = load(name, [D, 1])
        for name in ("bk1_row", "bv1_row", "bo1_row", "bo2_row"):
            k[name] = row(name, D)
        k["rank_row"] = row("rank_row", E)
        k["head_of"] = load("head_of", [D, HEADS])
        k["same_head"] = load("same_head", [D, D])
        k["head_in_four"] = load("head_in_four", [D, 4])
        k["wkv1"] = load("wkv1", [D, 2 * D])
        for name in ("wq1", "wo1", "wq2", "wk2", "wv2", "wo2T"):
            k[name] = load(name, [D, D])
        k["qnw_row"] = row("qnw_row", HD0)
        k["knw_row"] = row("knw_row", HD0)
        k["bo0_row"] = row("bo0_row", D)
        for name in ("wgT", "wrT", "woT0"):
            k[name] = load(name, [D, D])
        xT = n.sb("xT", [D, T])
        wq0 = load("wq0", [D, HEADS * HD0])
        wk0 = load("wk0", [D, HEADS * HD0])
        wkq = n.sb("wkq", [D, HEADS // 2, D])
        wvo = n.sb("wvo", [D, HEADS, D])

        with Net(nc) as n2:
            x_steps = n2.sb("x_steps", [D, L, B])
            hidden = n2.sb("hidden", [D, L, B])
            wkT = n2.sb("wkT", [D, HEADS // 2, D])
            wvT = n2.sb("wvT", [D, HEADS // 2, D])
            wo = n2.sb("wo0", [D, HEADS // 2, D])
            y = n2.sb("y", [L, B, D])
            pairs += [(x_steps[:, :, :], a["x_steps"]), (wkT[:, :, :], a["wkT0"]), (wvT[:, :, :], a["wvT0"]),
                      (wo[:, :, :], a["wo0"])]
            load_weights(nc, a, k, pairs)
            recurrence(nc, k, x_steps, hidden)
            hidden_to_tokens(nc, k, hidden, y)
            norm_tokens(nc, "n0", k, y, xT, k["ln_w"][:, 0:1], k["ln_b"][:, 0:1])
            project_add(nc, k, "p0", xT, k["woT0"][:, :], k["bo0_row"][:, :], x)
            fold_weights(nc, k, wkT, wvT, wo, wkq, wvo)
        norm_tokens(nc, "n1", k, x, xT)
        if upto > 1:
            cross_attention_0(nc, k, a["ctxT"], a["ctxN"], x, xT, wq0, wk0, wkq, wvo)
        norm_tokens(nc, "n2", k, x, xT, out=out if upto <= 2 else None)
        if upto <= 2:
            return

        share = n.sb("share", [L, B, E])
        with Net(nc) as n2:
            w_up = n2.sb("w_up0", [D, E, 2 * I0])
            b_up = n2.sb("b_up0", [D, E, 4])
            w_down = n2.sb("w_down0", [D, E, 2, D])
            b_down = n2.sb("b_down0", [E, D])
            router = n2.sb("router0", [D, E])
            r_row = n2.sb("router_row0", [L, E])
            load_stage(nc, "l2", [(w_up[:, :, :], a["w_up0"]), (b_up[:, :, :], a["b_up0"]), (w_down[:, :, :, :], a["w_down0"]),
                                  (b_down[:, :], a["b_down0"]), (router[:, :], a["router0"]),
                                  (r_row[:, :], a["router_row0"].partition_broadcast(L))])
            route(nc, "r0", k, x, xT, router[:, :], r_row[:, :], b_down[:, :], share, False)
            gated_experts(nc, k, x, xT, w_up, b_up, w_down, share)
        norm_tokens(nc, "n3", k, x, xT, out=out if upto <= 3 else None)
        if upto <= 3:
            return

        linear_attention(nc, k, x, xT)
        project_add(nc, k, "p4", xT, k["wo1"][:, :], k["bo1_row"][:, :], x)
        norm_tokens(nc, "n4", k, x, xT, out=out if upto <= 4 else None)
        if upto <= 4:
            return

        cross_attention_1(nc, k, a["ctxT"], x, xT)
        norm_tokens(nc, "n5", k, x, xT, out=out if upto <= 5 else None)
        if upto <= 5:
            return

        with Net(nc) as n2:
            w_up = n2.sb("w_up1", [D, E, F1])
            b_up = n2.sb("b_up1", [D, E, 4])
            w_down = n2.sb("w_down1", [D, E, 4, D])
            b_down = n2.sb("b_down1", [E, D])
            router = n2.sb("router1", [D, E])
            r_row = n2.sb("router_row1", [L, E])
            load_stage(nc, "l5", [(w_up[:, :, :], a["w_up1"]), (b_up[:, :, :], a["b_up1"]), (w_down[:, :, :, :], a["w_down1"]),
                                  (b_down[:, :], a["b_down1"]), (router[:, :], a["router1"]),
                                  (r_row[:, :], a["router_row1"].partition_broadcast(L))])
            route(nc, "r1", k, x, xT, router[:, :], r_row[:, :], b_down[:, :], share, True)
            relu_experts(nc, k, x, xT, w_up, b_up, w_down, share)
        norm_tokens(nc, "n6", k, x, out=out)



def lay_out(v):
    import numpy as np

    def pairs_T(w):
        return w.T.reshape(HEADS // 2, D, D).transpose(1, 0, 2)

    ctx = v["ctx_1024"]
    short = ctx[:, :SP_FULL * CH].reshape(B, SP_FULL, CH, D)
    last = ctx[:, SP_FULL * CH:]
    parts = [np.concatenate([short[:, :, c]] + ([last[:, c:c + 1]] if c < S % CH else []), axis=1)
             for c in range(CH)]
    ctxT = np.concatenate(parts, axis=1).transpose(0, 2, 1)
    col = lambda w: w.reshape(-1, 1)
    row = lambda w: w.reshape(-1)
    two = lambda w: np.concatenate([w, w]).reshape(-1, 1)
    p = "L0_attn_"
    o = {
        "x": v["x"].transpose(1, 0, 2), "x_steps": v["x"].transpose(2, 1, 0),
        "ctxT": ctxT, "ctxN": ctx.reshape(B, S * D), "lens": v["_lenS2"],
        "ident": np.eye(D, dtype=np.float32),
        "row_of": (np.arange(SP_MAX)[:, None] * CH + np.arange(CH)[None, :]).astype(np.float32),
        "decay": col(v[p + "decay"]), "bg": col(v[p + "bg"]), "br": col(v[p + "br"]),
        "ln_w": col(v[p + "ln_w"]), "ln_b": col(v[p + "ln_b"]), "bo0_row": row(v[p + "bo"]),
        "wgT": v[p + "Wg"].T, "wrT": v[p + "Wr"].T, "woT0": v[p + "Wo"].T,
    }
    p = "L0_xattn_"
    o |= {
        "qnw": two(v[p + "q_norm_w"]), "knw": two(v[p + "k_norm_w"]),
        "qnw_row": row(v[p + "q_norm_w"]), "knw_row": row(v[p + "k_norm_w"]),
        "wq0": v[p + "Wq"], "wk0": v[p + "Wk"], "wkT0": pairs_T(v[p + "Wk"]), "wvT0": pairs_T(v[p + "Wv"]),
        "wo0": v[p + "Wo"].reshape(HEADS // 2, D, D).transpose(1, 0, 2),
    }
    def hidden(b, chunks):
        return b.reshape(E, chunks, D).transpose(2, 0, 1)

    p = "L0_ffn_"
    o |= {
        "router0": v[p + "router_weight"].T, "router_row0": row(v[p + "router_bias"]),
        "w_up0": v[p + "gate_up_proj"].transpose(1, 0, 2), "b_up0": hidden(v[p + "gate_up_bias"], 4),
        "w_down0": v[p + "down_proj"].reshape(E, 2, D, D).transpose(2, 0, 1, 3), "b_down0": v[p + "down_bias"],
        "rank_row": np.arange(E, 0, -1).astype(np.float32),
    }
    p = "L1_attn_"
    head = np.arange(D) // HD1
    o |= {
        "wq1": v[p + "Wq"], "wkv1": np.concatenate([v[p + "Wk"], v[p + "Wv"]], axis=1), "wo1": v[p + "Wo"],
        "bq1": col(v[p + "bq"]), "bk1_row": row(v[p + "bk"]), "bv1_row": row(v[p + "bv"]),
        "bo1_row": row(v[p + "bo"]),
        "head_of": (head[:, None] == np.arange(HEADS)[None, :]).astype(np.float32),
        "same_head": (head[:, None] == head[None, :]).astype(np.float32),
        "head_in_four": (head[:, None] % 4 == np.arange(4)[None, :]).astype(np.float32),
    }
    p = "L1_xattn_"
    heads = lambda w: w.transpose(1, 0, 2).reshape(D, D)
    o |= {
        "wq2": heads(v[p + "Wq"]), "wk2": heads(v[p + "Wk"]), "wv2": heads(v[p + "Wv"]), "wo2T": v[p + "Wo"].T,
        "bq2": col(v[p + "bq"]), "bk2": col(v[p + "bk"]), "bv2": col(v[p + "bv"]), "bo2_row": row(v[p + "bo"]),
    }
    p = "L1_ffn_"
    o |= {
        "router1": v[p + "gate_w"], "router_row1": row(v[p + "gate_b"]),
        "w_up1": v[p + "W1"].transpose(1, 0, 2), "b_up1": hidden(v[p + "b1"], 4),
        "w_down1": v[p + "W2"].reshape(E, 4, D, D).transpose(2, 0, 1, 3), "b_down1": v[p + "b2"],
    }
    return {n: np.ascontiguousarray(w) for n, w in o.items()}


def kernel(**inputs):
    import numpy as _np
    import concourse.bacc as _bacc
    from concourse import mybir as _mybir
    from concourse.bass_utils import run_bass_kernel_spmd as _run

    nc = _bacc.Bacc("TRN2", target_bir_lowering=False, num_devices=1)
    arrays, args = {}, {}
    for name, w in lay_out({n: _np.asarray(w) for n, w in inputs.items()}).items():
        arrays[f"in_{name}"] = w
        args[name] = nc.dram_tensor(f"in_{name}", w.shape, _mybir.dt.from_np(w.dtype), kind="ExternalInput").ap()
    out = nc.dram_tensor("out", (L, B, D), _mybir.dt.float32, kind="ExternalOutput").ap()
    decoder(nc, args, out)
    r = _run(nc, [arrays], core_ids=[0])
    return r.results[0]["out"].transpose(1, 0, 2)
```

```python
from contextlib import ExitStack

import concourse.bass as bass
from concourse import mybir

ALU = mybir.AluOpType
ACT = mybir.ActivationFunctionType
F32 = mybir.dt.float32
BF16 = mybir.dt.bfloat16
F32R = mybir.dt.float32r
I32 = mybir.dt.int32
AX_X = mybir.AxisListType.X

B, L, D = 16, 100, 128
T = B * L
S = 1444
CH = 12
SP_FULL = S // CH
SP_MAX = SP_FULL + 1
HEADS = 16
HD0 = 64
HD1 = 8
E = 8
I0 = 256
F1 = 512
STACK = 3 * 4 * HD1
HALF = 8 * L
EPS = 1e-5
MASKED = -30000.0


def rows(c):
    return SP_MAX if c < S % CH else SP_FULL


def off(c):
    return SP_FULL * c + min(c, S % CH)


class Net:

    def __init__(self, nc):
        self.nc = nc
        self.ctx = ExitStack()

    def __enter__(self):
        self.ctx.__enter__()
        return self

    def __exit__(self, *a):
        return self.ctx.__exit__(*a)

    def sb(self, name, shape, dt=F32):
        return self.ctx.enter_context(self.nc.sbuf_tensor(name, shape, dt))

    def ps(self, name, n=1):
        return self.ctx.enter_context(self.nc.psum_tensor(name, [128, n, 512], F32))

    def sem(self, name):
        return self.ctx.enter_context(self.nc.semaphore(name))


def over_heads(col, n):
    p, m = col.shape
    return col.unsqueeze(2).to_broadcast([p, m, n])



def norm_tokens(nc, tag, k, x, xT=None, gain=None, shift=None, out=None):
    with Net(nc) as n:
        stats = n.sb(f"{tag}_stats", [L, B, 6])
        mv = n.sb(f"{tag}_mean_var", [L, B, 2])
        sd = n.sb(f"{tag}_sd", [L, B])
        rstd = n.sb(f"{tag}_rstd", [L, B])
        turned = n.ps(f"{tag}_turned", 4)
        s_stat, s_sd, s_rstd, s_norm, s_turn, s_evac, s_out = k["norm_sems"]
        c = k["norms"]
        k["norms"] = c + 1
        block = n.ctx.enter_context(nc.Block())

        @block.vector
        def _(dve):
            for b in range(B):
                dve.bn_stats(stats[:, b, :], x[:, b, :]).then_inc(s_stat, 1)
            for b in range(B):
                dve.wait_ge(s_stat, 2 * B * c + b + 1)
                dve.bn_aggr(mv[:, b, :], stats[:, b, :]).then_inc(s_stat, 1)
            dve.wait_ge(s_sd, c + 1)
            dve.reciprocal(rstd[:, :], sd[:, :]).then_inc(s_rstd, 1)
            dve.wait_ge(s_rstd, c + 1)
            for b in range(B):
                dve.tensor_scalar(x[:, b, :], x[:, b, :], mv[:, b, 0:1], rstd[:, b:b + 1],
                                  ALU.subtract, ALU.mult).then_inc(s_norm, 1)

        @block.scalar
        def _(act):
            act.wait_ge(s_stat, 2 * B * (c + 1))
            act.activation(sd[:, :], mv[:, :, 1], ACT.Sqrt, bias=k["eps"][0:L, 0:1]).then_inc(s_sd, 1)
            if xT is not None:
                for g in range(4):
                    act.wait_ge(s_turn, 4 * c + g + 1)
                    src = turned[:, g, 0:4 * L]
                    dst = xT[:, 4 * g * L:4 * (g + 1) * L]
                    if gain is None:
                        act.activation(dst, src, ACT.Copy).then_inc(s_evac, 1)
                    else:
                        act.activation(dst, src, ACT.Identity, bias=shift, scale=gain).then_inc(s_evac, 1)

        if xT is not None:
            @block.tensor
            def _(pe):
                for b in range(B):
                    pe.wait_ge(s_norm, B * c + b + 1)
                    t = pe.transpose(turned[:, b // 4, (b % 4) * L:(b % 4 + 1) * L], x[:, b, :],
                                     k["ident"][0:L, 0:L])
                    if b % 4 == 3:
                        t.then_inc(s_turn, 1)

        if out is not None:
            @block.sync
            def _(sp):
                sp.wait_ge(s_norm, B * (c + 1))
                sp.dma_start(out, x[:, :, :]).then_inc(s_out, 16)
                sp.wait_ge(s_out, 16)



def load_weights(nc, a, k, pairs):
    with Net(nc) as n:
        s_load = n.sem("s_load")
        s_const = n.sem("s_const")
        block = n.ctx.enter_context(nc.Block())

        @block.sync
        def _(sp):
            for dst, src in pairs[0::2]:
                sp.dma_start(dst, src).then_inc(s_load, 16)
            sp.wait_ge(s_load, 16 * len(pairs))

        @block.scalar
        def _(act):
            for dst, src in pairs[1::2]:
                act.dma_start(dst, src).then_inc(s_load, 16)

        @block.vector
        def _(dve):
            dve.memset(k["eps"][:, :], EPS).then_inc(s_const, 1)
            dve.memset(k["ones"][:, :], 1.0).then_inc(s_const, 1)


def load_stage(nc, tag, pairs):
    with Net(nc) as n:
        s_load = n.sem(f"{tag}_s_load")
        block = n.ctx.enter_context(nc.Block())

        @block.sync
        def _(sp):
            for dst, src in pairs:
                sp.dma_start(dst, src).then_inc(s_load, 16)
            sp.wait_ge(s_load, 16 * len(pairs))



def recurrence(nc, k, x_steps, hidden):
    with Net(nc) as n:
        forget = n.sb("forget", [D, 1])
        negkeep = n.sb("negkeep", [D, 1])
        z = n.sb("z", [D, L, B])
        c = n.sb("c", [D, L, B])
        w = n.sb("w", [D, 2, B])
        m = n.sb("m", [D, 2, B])
        zp = n.ps("zp", 4)
        pred = n.ps("pred", 2)
        s_z = n.sem("s_z")
        s_gate = n.sem("s_gate")
        s_pre = n.sem("s_pre")
        s_w = n.sem("s_w")
        s_m = n.sem("s_m")
        s_h = n.sem("s_h")
        s_pred = n.sem("s_pred")
        TG = L // 4
        xs = x_steps
        block = n.ctx.enter_context(nc.Block())

        @block.tensor
        def _(pe):
            for g in range(4):
                pe.matmul(zp[:, g, 0:TG * B], k["wgT"][:, :], xs[:, g * TG:(g + 1) * TG, :],
                          start=True, stop=True).then_inc(s_z, 1)

            def predict(t, p):
                pe.wait_ge(s_w, t)
                pe.matmul(pred[:, p, 0:B], k["wrT"][:, :], w[:, 1 - p, :], start=True, stop=False)
                pe.wait_ge(s_m, t)
                pe.matmul(pred[:, p, 0:B], k["wrT"][:, :], m[:, 1 - p, :], start=False,
                          stop=True).then_inc(s_pred, 1)

            with pe.Fori(0, (L - 2) // 2) as i:
                predict(2 * i + 1, 1)
                predict(2 * i + 2, 0)
            predict(L - 1, 1)

        @block.scalar
        def _(act):
            act.activation(forget[:, :], k["decay"][:, :], ACT.Sigmoid).then_inc(s_gate, 1)
            for g in range(4):
                act.wait_ge(s_z, g + 1)
                act.activation(z[:, g * TG:(g + 1) * TG, :].rearrange("p t b -> p (t b)"),
                               zp[:, g, 0:TG * B], ACT.Sigmoid, bias=k["bg"][:, 0:1]).then_inc(s_gate, 1)

        @block.vector
        def _(dve):
            dve.tensor_scalar(c[:, :, :], xs[:, :, :], k["br"][:, 0:1], None, ALU.subtract).then_inc(s_pre, 1)
            dve.wait_ge(s_gate, 1)
            dve.tensor_scalar(negkeep[:, :], forget[:, :], -1.0, None, ALU.add).then_inc(s_pre, 1)
            dve.wait_ge(s_gate, 5)
            dve.wait_ge(s_pre, 2)
            dve.tensor_scalar(z[:, :, :], z[:, :, :], negkeep[:, 0:1], None, ALU.mult).then_inc(s_pre, 1)
            dve.wait_ge(s_pre, 3)
            dve.scalar_tensor_tensor(out=c[:, :, :].rearrange("p t b -> p (t b)"),
                                     in0=z[:, :, :].rearrange("p t b -> p (t b)"), scalar=-1.0,
                                     in1=c[:, :, :].rearrange("p t b -> p (t b)"),
                                     op0=ALU.mult, op1=ALU.mult).then_inc(s_pre, 1)
            dve.memset(m[:, :, :], 0.0).then_inc(s_m, 1)
            dve.wait_ge(s_pre, 4)
            dve.tensor_copy(w[:, 0, :], c[:, 0, :]).then_inc(s_w, 1)
            dve.tensor_copy(hidden[:, 0, :], c[:, 0, :]).then_inc(s_h, 1)

            def step(t, p):
                dve.wait_ge(s_h, t)
                dve.scalar_tensor_tensor(out=w[:, p, :], in0=hidden[:, bass.ds(t - 1, 1), :].rearrange("p t b -> p (t b)"),
                                         scalar=forget[:, 0:1],
                                         in1=c[:, bass.ds(t, 1), :].rearrange("p t b -> p (t b)"),
                                         op0=ALU.mult, op1=ALU.add).then_inc(s_w, 1)
                dve.wait_ge(s_pred, t)
                dve.tensor_tensor(m[:, p, :], pred[:, p, 0:B],
                                  z[:, bass.ds(t, 1), :].rearrange("p t b -> p (t b)"), ALU.mult).then_inc(s_m, 1)
                dve.wait_ge(s_m, t + 1)
                dve.wait_ge(s_w, t + 1)
                dve.tensor_tensor(hidden[:, bass.ds(t, 1), :].rearrange("p t b -> p (t b)"), w[:, p, :], m[:, p, :],
                                  ALU.add).then_inc(s_h, 1)

            with dve.Fori(0, (L - 2) // 2) as i:
                step(2 * i + 1, 1)
                step(2 * i + 2, 0)
            step(L - 1, 1)


def hidden_to_tokens(nc, k, hidden, y):
    with Net(nc) as n:
        turned = n.ps("hid_turned", 4)
        s_turn = n.sem("hid_s_turned")
        s_evac = n.sem("hid_s_evac")
        block = n.ctx.enter_context(nc.Block())

        @block.tensor
        def _(pe):
            for b in range(B):
                t = pe.transpose(turned[0:L, b // 4, (b % 4) * D:(b % 4 + 1) * D], hidden[:, :, b],
                                 k["ident"][:, :])
                if b % 4 == 3:
                    t.then_inc(s_turn, 1)

        @block.vector
        def _(dve):
            for g in range(4):
                dve.wait_ge(s_turn, g + 1)
                dve.tensor_copy(y[:, 4 * g:4 * g + 4, :].rearrange("l b d -> l (b d)"),
                                turned[0:L, g, :]).then_inc(s_evac, 1)


def project_add(nc, k, tag, inT, weight, bias_row, x):
    with Net(nc) as n:
        prod = n.ps(f"{tag}_prod", 4)
        s_prod, s_bias, s_add = k["project_sems"]
        c = k["projects"]
        k["projects"] = c + 1
        block = n.ctx.enter_context(nc.Block())

        @block.tensor
        def _(pe):
            for b in range(B):
                t = pe.matmul(prod[0:L, b // 4, (b % 4) * D:(b % 4 + 1) * D], inT[:, b * L:(b + 1) * L],
                              weight, start=True, stop=True)
                if b % 4 == 3:
                    t.then_inc(s_prod, 1)

        @block.vector
        def _(dve):
            dve.tensor_tensor(x[:, :, :], x[:, :, :], bias_row.unsqueeze(1).to_broadcast([L, B, D]),
                              ALU.add).then_inc(s_bias, 1)
            dve.wait_ge(s_bias, c + 1)
            for g in range(4):
                dve.wait_ge(s_prod, 4 * c + g + 1)
                xg = x[:, 4 * g:4 * g + 4, :].rearrange("l b d -> l (b d)")
                dve.tensor_tensor(xg, xg, prod[0:L, g, :], ALU.add).then_inc(s_add, 1)



def fold_weights(nc, k, wkT, wvT, wo, wkq, wvo):
    with Net(nc) as n:
        norm_w = n.sb("norm_w", [D, 1])
        norm_row = n.sb("norm_row", [SP_MAX, HD0])
        cap = n.sb("cap", [SP_MAX, 1])
        len_f = n.sb("len_f", [SP_MAX, B])
        prod = n.ps("wvo_prod", 4)
        s_nw = n.sem("s_nw")
        s_cap = n.sem("s_cap")
        s_mask = n.sem("s_mask")
        s_wvo = n.sem("s_wvo")
        s_evac = n.sem("s_wvo_evac")
        s_wkq = n.sem("s_wkq")
        block = n.ctx.enter_context(nc.Block())

        @block.tensor
        def _(pe):
            for r in range(4):
                for h in range(4 * r, 4 * r + 4):
                    j, bank = h % 2, h % 2 + 2 * (r % 2)
                    if r >= 2 and h < 4 * r + 2:
                        pe.wait_ge(s_evac, 2 * (r - 2) + 1 + j)
                    t = pe.matmul(prod[:, bank, (h // 2 % 2) * D:(h // 2 % 2 + 1) * D],
                                  wvT[64 * j:64 * j + 64, h // 2, :], wo[64 * j:64 * j + 64, h // 2, :],
                                  start=True, stop=True)
                t.then_inc(s_wvo, 1)

        @block.vector
        def _(dve):
            dve.tensor_tensor(norm_w[:, :], k["qnw"][:, :], k["knw"][:, :], ALU.mult).then_inc(s_nw, 1)
            dve.wait_ge(s_nw, 1)
            dve.tensor_scalar(wkq[:, :, :], wkT[:, :, :], norm_w[:, 0:1], HD0 ** -0.5, ALU.mult,
                              ALU.mult).then_inc(s_wkq, 1)
            dve.tensor_tensor(norm_row[:, :], k["qnw_row"][0:SP_MAX, :], k["knw_row"][0:SP_MAX, :],
                              ALU.mult).then_inc(s_cap, 1)
            dve.wait_ge(s_cap, 1)
            dve.tensor_reduce(cap[:, :], norm_row[:, :], AX_X, ALU.max, apply_absolute_value=True).then_inc(s_cap, 1)
            dve.tensor_copy(len_f[:, :], k["lens"][:, :]).then_inc(s_cap, 1)
            dve.wait_ge(s_cap, 3)
            dve.tensor_scalar(cap[:, :], cap[:, :], HD0 ** 0.5, None, ALU.mult).then_inc(s_cap, 1)
            mask = k["mask_bias"]
            dve.tensor_tensor(mask[:, :, :], k["row_of"][:, :].unsqueeze(1).to_broadcast([SP_MAX, B, CH]),
                              over_heads(len_f[:, :], CH), ALU.is_ge).then_inc(s_mask, 1)
            dve.wait_ge(s_mask, 1)
            dve.wait_ge(s_cap, 4)
            dve.tensor_scalar(mask[:, :, :], mask[:, :, :], MASKED, cap[:, 0:1], ALU.mult,
                              ALU.subtract).then_inc(s_mask, 1)
            for r in range(4):
                dve.wait_ge(s_wvo, r + 1)
                for j in range(2):
                    dve.tensor_copy(wvo[:, 4 * r + j:4 * r + j + 3:2, :],
                                    prod[:, j + 2 * (r % 2), 0:2 * D].rearrange("p (a d) -> p a d", a=2))\
                       .then_inc(s_evac, 1)


def cross_attention_0(nc, k, ctxT_d, ctxN_d, x, xT, wq, wk, wkq, wvo):
    NS = 2 * CH
    with Net(nc) as n:
        ctx_in = n.sb("ctx_in", [D, S])
        ctx_high = [n.sb(f"ctx_high{u}", [D, S], F32R) for u in range(2)]
        ctx_low = [n.sb(f"ctx_low{u}", [D, S], F32R) for u in range(2)]
        wk_high = n.sb("wk_high", [D, HEADS * HD0], F32R)
        wk_low = n.sb("wk_low", [D, HEADS * HD0], F32R)
        ctxN = [n.sb(f"ctxN{u}", [SP_MAX, CH, D]) for u in range(2)]
        sq = n.sb("sq", [SP_MAX, 2, 512])
        kss = n.sb("kss", [SP_MAX, CH, HEADS])
        ksd = n.sb("ksd", [SP_MAX, CH, HEADS])
        krs = [n.sb(f"krs{u}", [SP_MAX, CH, HEADS]) for u in range(2)]
        bias = [n.sb(f"bias{u}", [SP_MAX, CH]) for u in range(2)]
        q_in = n.sb("q_in", [D, L])
        qs = n.sb("qs", [L, HEADS, HD0])
        qsq = n.sb("qsq", [L, HEADS, HD0])
        qss = n.sb("qss", [L, HEADS])
        qsd = n.sb("qsd", [L, HEADS])
        qrs = n.sb("qrs", [L, HEADS])
        qn = n.sb("qn", [L, HEADS, HD0])
        qblk = n.sb("qblk", [D, HEADS // 2, 2, L])
        qp_high = [n.sb(f"qp_high{u}", [D, HEADS * L], F32R) for u in range(2)]
        qp_low = [n.sb(f"qp_low{u}", [D, HEADS * L], F32R) for u in range(2)]
        p = [n.sb(f"p{j}", [SP_MAX, HALF]) for j in range(4)]
        acc = [n.sb(f"acc{j}", [SP_MAX, HALF]) for j in range(2)]
        oraw = n.sb("oraw", [D, HALF])
        rden = n.sb("rden", [D, HALF])
        onorm = n.sb("onorm", [D, HALF])
        ring = n.ps("ring", 4)
        pvb = n.ps("pvb", 2)
        knb = n.ps("knb", 1)
        qb = n.ps("qb", 1)

        s_ctx = [n.sem(f"s_ctx{u}") for u in range(2)]
        s_ctx_in = n.sem("s_ctx_in")
        s_split = n.sem("s_split")
        s_ctx_high = n.sem("s_ctx_high")
        s_ctx_low = n.sem("s_ctx_low")
        s_qp_high = n.sem("s_qp_high")
        s_qin = n.sem("s_qin")
        s_kn = n.sem("s_kn")
        s_sq = n.sem("s_sq")
        s_ss = n.sem("s_ss")
        s_ksd = n.sem("s_ksd")
        s_krs = n.sem("s_krs")
        s_qunit = n.sem("s_qunit")
        s_qfree = n.sem("s_qfree")
        s_qsq = n.sem("s_qsq")
        s_qss = n.sem("s_qss")
        s_qsd = n.sem("s_qsd")
        s_qrs = n.sem("s_qrs")
        s_qn = n.sem("s_qn")
        s_blk0 = n.sem("s_blk0")
        s_bias = n.sem("s_rowbias")
        s_item = n.sem("s_item")
        s_free = n.sem("s_free")
        s_exp = n.sem("s_exp")
        s_acc = n.sem("s_acc")
        s_pv = n.sem("s_pv")
        s_oraw = n.sem("s_oraw")
        s_rden = n.sem("s_rden")
        s_on = n.sem("s_on")

        ITEMS = NS + 2
        TAIL_ITEM, DEN_ITEM = 2, 15
        item_of = [s if s < 2 else s + 1 if s < 14 else s + 2 for s in range(NS)]
        UNITS = 10
        FIRST_NORM = 3
        norms_at = [[] for s in range(NS)]
        for i in range(NS):
            norms_at[FIRST_NORM + i * 3 // 4].append(i)

        def unit(b, i):
            if isinstance(b, int) and b >= B - 1 and i > 0 or isinstance(b, int) and b >= B:
                return UNITS * B + (1 if b == B - 1 else 2)  - 1
            return UNITS * (b + 1) + i - 1

        def twice(b, i):
            return 3 if isinstance(b, int) and b == -1 and i == 8 else 1

        block = n.ctx.enter_context(nc.Block())

        @block.sync
        def _(sp):
            def load_turned(b):
                sp.dma_start(ctx_in[:, :], ctxT_d[bass.ds(b, 1), :, :].rearrange("b d s -> (b d) s"))\
                  .then_inc(s_ctx_in, 16)

            def load(b, u):
                sp.dma_start(ctxN[u][0:SP_FULL, :, :].rearrange("p c d -> p (c d)"),
                             ctxN_d[bass.ds(b, 1), 0:SP_FULL * CH * D].rearrange("b (p n) -> (b p) n", p=SP_FULL))\
                  .then_inc(s_ctx[u], 16)
                sp.dma_start(ctxN[u][SP_FULL:SP_MAX, 0:S % CH, :].rearrange("p c d -> p (c d)"),
                             ctxN_d[bass.ds(b, 1), SP_FULL * CH * D:S * D]).then_inc(s_ctx[u], 16)

            load_turned(0)
            load(0, 0)
            load(1, 1)
            sp.wait_ge(s_ctx_low, 1)
            load_turned(1)
            with sp.Fori(0, (B - 2) // 2) as i:
                for u in range(2):
                    sp.wait_ge(s_ctx_low, 2 * i + u + 2)
                    load_turned(2 * i + u + 2)
                    sp.wait_ge(s_pv, NS * (2 * i + u + 1))
                    load(2 * i + u + 2, u)

        def batches(eng, batch):
            batch(0, 0, 1, tail=False)
            with eng.Fori(0, (B - 2) // 2) as i:
                batch(2 * i + 1, 1, i + 2)
                batch(2 * i + 2, 0, i + 2)
            batch(B - 1, 1, 0, prep=False)

        @block.tensor
        def _(pe):
            def key_norm_unit(j, u, s):
                c = s // 2
                if not (isinstance(j, int) and j == 0 and s == 0):
                    pe.wait_ge(s_sq, NS * j + s)
                at, heads = slice(off(c), off(c) + rows(c)), slice(512 * (s % 2), 512 * (s % 2) + 512)
                dst = knb[0:rows(c), 0, :]
                pe.matmul(dst, ctx_high[u][:, at], wk_high[:, heads], start=True, stop=False)
                pe.matmul(dst, ctx_high[u][:, at], wk_low[:, heads], start=False, stop=False)
                pe.matmul(dst, ctx_low[u][:, at], wk_high[:, heads], start=False, stop=True).then_inc(s_kn, 1)

            def qbank(b, i):
                if not (isinstance(b, int) and b == -1 and i == 1):
                    pe.wait_ge(s_qfree, unit(b, i))

            def query_unit(b, i):
                qbank(b, i)
                pe.wait_ge(s_qin, b + 2)
                pe.matmul(qb[0:L, 0, :], q_in[:, :], wq[:, 512 * (i - 1):512 * i],
                          start=True, stop=True).then_inc(s_qunit, 1)

            def turn_unit(b, i):
                qbank(b, i)
                pe.wait_ge(s_qn, b + 2)
                for a in range(4):
                    h = 8 * (i - 3) + 2 * a
                    t = pe.transpose(qb[:, 0, a * L:(a + 1) * L], qn[:, h:h + 2, :].rearrange("l h e -> l (h e)"),
                                     k["ident"][0:L, 0:L])
                t.then_inc(s_qunit, 1)

            def absorb_unit(b, i):
                qbank(b, i)
                for a in range(2):
                    g = 2 * (i - 5) + a
                    t = pe.matmul(qb[:, 0, a * 2 * L:(a + 1) * 2 * L], wkq[:, g, :],
                                  qblk[:, g, :, :].rearrange("p a l -> p (a l)"), start=True, stop=True)
                t.then_inc(s_qunit, twice(b, i))

            def out_unit(b, i, half, done):
                qbank(b, i)
                pe.wait_ge(s_on, done)
                for h in range(8):
                    t = pe.matmul(qb[0:L, 0, 0:D], onorm[:, h * L:(h + 1) * L], wvo[:, 8 * half + h, :],
                                  start=(h == 0), stop=(h == 7))
                t.then_inc(s_qunit, 1)

            def slot(b, i):
                if not (isinstance(b, int) and b == 0 and i < 2):
                    pe.wait_ge(s_free, ITEMS * b + i - 1)
                return 2 * (i % 2)

            def den_item(b, i, half, done):
                r = slot(b, i)
                pe.wait_ge(s_acc, done)
                for a in range(2):
                    t = pe.matmul(ring[:, r + a, 0:4 * L], k["ones"][0:SP_MAX, :],
                                  acc[half][:, a * 4 * L:(a + 1) * 4 * L], start=True, stop=True)
                t.then_inc(s_item, 1)

            def score(b, u, s):
                half, c = s // CH, s % CH
                if c == 0:
                    pe.wait_ge(s_qfree, unit(b - 1, 9 if half else 7))
                r = slot(b, item_of[s])
                for a in range(2):
                    at = slice(off(c), off(c) + rows(c))
                    heads = slice(half * HALF + a * 4 * L, half * HALF + (a + 1) * 4 * L)
                    dst = ring[0:rows(c), r + a, 0:4 * L]
                    pe.matmul(dst, ctx_high[u][:, at], qp_high[u][:, heads], start=True, stop=False)
                    pe.matmul(dst, ctx_high[u][:, at], qp_low[u][:, heads], start=False, stop=False)
                    t = pe.matmul(dst, ctx_low[u][:, at], qp_high[u][:, heads], start=False, stop=True)
                t.then_inc(s_item, 2 if isinstance(b, int) and b == 0 and s == 1 else 1)

            def weigh(b, u, s):
                c = s % CH
                if c == 0 and not (isinstance(b, int) and b == 0 and s == 0):
                    pe.wait_ge(s_oraw, 2 * b + s // CH)
                pe.wait_ge(s_exp, NS * b + s + 1)
                for a in range(2):
                    t = pe.matmul(pvb[:, a, 0:4 * L], ctxN[u][0:rows(c), c, :],
                                  p[s % 4][0:rows(c), a * 4 * L:(a + 1) * 4 * L],
                                  start=(c == 0), stop=(c == CH - 1))
                t.then_inc(s_pv, 1)

            def batch(b, u, nth, prep=True, tail=True):
                for s in range(NS):
                    if s == 2 and tail:
                        den_item(b, TAIL_ITEM, 1, NS * b)
                    if s == 14:
                        den_item(b, DEN_ITEM, 0, NS * b + CH)
                    score(b, u, s)
                    if s == FIRST_NORM and prep:
                        pe.wait_ge(s_ctx_low, b + 2)
                        pe.wait_ge(s_ctx[1 - u], 32 * nth)
                    for i in norms_at[s][:1] if prep else []:
                        key_norm_unit(b + 1, 1 - u, i)
                    if s >= 1:
                        weigh(b, u, s - 1)
                    for i in norms_at[s][1:] if prep else []:
                        key_norm_unit(b + 1, 1 - u, i)
                    if s == 7 and tail:
                        out_unit(b, 0, 1, 2 * b)
                    if prep and s in (8, 9):
                        query_unit(b, s - 7)
                    if prep and s in (15, 16):
                        turn_unit(b, s - 12)
                    if prep and s in (18, 19, 20, 21):
                        absorb_unit(b, s - 13)
                    if s == 22:
                        out_unit(b, 9, 0, 2 * b + 1)
                weigh(b, u, NS - 1)

            pe.wait_ge(s_ctx[0], 32)
            pe.wait_ge(s_ctx_low, 1)
            pe.wait_ge(s_split, 2)
            for s in range(NS):
                key_norm_unit(0, 0, s)
            for i in range(1, 9):
                (query_unit if i < 3 else turn_unit if i < 5 else absorb_unit)(-1, i)
            batches(pe, batch)
            den_item(B, 0, 1, NS * B)
            out_unit(B, 0, 1, 2 * B)

        @block.scalar
        def _(act):
            def keep_high(j, u):
                act.wait_ge(s_ctx_in, 16 * (j + 1))
                if not (isinstance(j, int) and j < 2):
                    act.wait_ge(s_pv, NS * (j - 1))
                act.activation(ctx_high[u][:, :], ctx_in[:, :], ACT.Copy).then_inc(s_ctx_high, 1)

            def keep_high_absorbed(b, u, i):
                act.wait_ge(s_qunit, unit(b, i) + 1)
                act.activation(qp_high[u][:, 4 * L * (i - 5):4 * L * (i - 4)], qb[:, 0, 0:4 * L],
                               ACT.Copy).then_inc(s_qp_high, 1)

            def square(j, s):
                r = rows(s // 2)
                act.wait_ge(s_kn, NS * j + s + 1)
                if not (isinstance(j, int) and j == 0 and s < 2):
                    act.wait_ge(s_ss, NS * j + s - 1)
                act.activation(sq[0:r, s % 2, :], knb[0:r, 0, :], ACT.Square).then_inc(s_sq, 1)

            def query_root(j):
                act.wait_ge(s_qss, j + 1)
                act.activation(qsd[:, :], qss[:, :], ACT.Sqrt, bias=k["eps"][0:L, 0:1],
                               scale=1.0 / HD0).then_inc(s_qsd, 1)

            def key_root(j):
                act.wait_ge(s_ss, NS * (j + 1))
                act.activation(ksd[:, :, :].rearrange("p c h -> p (c h)"), kss[:, :, :].rearrange("p c h -> p (c h)"),
                               ACT.Sqrt, bias=k["eps"][0:SP_MAX, 0:1], scale=1.0 / HD0).then_inc(s_ksd, 1)

            def batch(b, u, nth, prep=True, tail=True):
                for s in range(NS):
                    c = s % CH
                    r = rows(c)
                    if s == 0:
                        act.wait_ge(s_bias, b + 1)
                    act.wait_ge(s_free, ITEMS * b + item_of[s] + 1)
                    act.activation(p[s % 4][0:r, :], p[s % 4][0:r, :], ACT.Exp,
                                   bias=bias[u][0:r, c:c + 1]).then_inc(s_exp, 1)
                    for i in norms_at[s] if prep else []:
                        square(b + 1, i)
                    if prep and s == 0:
                        keep_high(b + 1, 1 - u)
                    if prep and s == 12:
                        query_root(b + 1)
                    if prep and s in (18, 19, 20, 21):
                        keep_high_absorbed(b, 1 - u, s - 13)
                    if prep and s == 21:
                        key_root(b + 1)

            keep_high(0, 0)
            for s in range(NS):
                square(0, s)
            query_root(0)
            for i in (5, 6, 7, 8):
                keep_high_absorbed(-1, 0, i)
            key_root(0)
            batches(act, batch)

        @block.gpsimd
        def _(pool):
            def keep_low(j, u):
                pool.wait_ge(s_ctx_high, j + 1)
                pool.tensor_tensor(ctx_low[u][:, :], ctx_in[:, :], ctx_high[u][:, :].bitcast(F32),
                                   ALU.subtract).then_inc(s_ctx_low, 1)

            def take_tokens(j):
                if not (isinstance(j, int) and j == 0):
                    pool.wait_ge(s_qunit, unit(j - 2, 3))
                pool.tensor_copy(q_in[:, :], xT[:, bass.ds(j * L, L)]).then_inc(s_qin, 1)

            def square_queries(j):
                pool.wait_ge(s_qfree, unit(j - 1, 3))
                pool.tensor_tensor(qsq[:, :, :], qs[:, :, :], qs[:, :, :], ALU.mult).then_inc(s_qsq, 1)

            def batch(b, u, nth, prep=True, tail=True):
                for s in range(NS):
                    half, c = s // CH, s % CH
                    r = rows(c)
                    if prep and s == 0:
                        keep_low(b + 1, 1 - u)
                    if prep and s == 1:
                        take_tokens(b + 1)
                    if prep and s == 10:
                        square_queries(b + 1)
                    if c == 0:
                        continue
                    if c == 1:
                        if not (isinstance(b, int) and b == 0):
                            pool.wait_ge(s_item, ITEMS * b + TAIL_ITEM + 1 if half else ITEMS * (b - 1) + DEN_ITEM + 1)
                        pool.wait_ge(s_exp, NS * b + s + 1)
                        pool.tensor_tensor(acc[half][0:r, :], p[(s - 1) % 4][0:r, :], p[s % 4][0:r, :],
                                           ALU.add).then_inc(s_acc, 2)
                    else:
                        pool.wait_ge(s_exp, NS * b + s + 1)
                        pool.wait_ge(s_acc, NS * b + s)
                        pool.tensor_tensor(acc[half][0:r, :], acc[half][0:r, :], p[s % 4][0:r, :],
                                           ALU.add).then_inc(s_acc, 1)

            keep_low(0, 0)
            take_tokens(0)
            square_queries(0)
            batches(pool, batch)

        @block.vector
        def _(dve):
            def sum_squares(j, s):
                r = rows(s // 2)
                dve.wait_ge(s_sq, NS * j + s + 1)
                dve.tensor_reduce(kss[0:r, s // 2, 8 * (s % 2):8 * (s % 2) + 8],
                                  sq[0:r, s % 2, :].rearrange("p (h e) -> p h e", h=8), AX_X,
                                  ALU.add).then_inc(s_ss, 1)

            def take_queries(b, i):
                dve.wait_ge(s_qunit, unit(b, i) + 1)
                dve.tensor_copy(qs[:, 8 * (i - 1):8 * i, :].rearrange("l h e -> l (h e)"),
                                qb[0:L, 0, :]).then_inc(s_qfree, 1)

            def sum_query_squares(j):
                dve.wait_ge(s_qsq, j + 1)
                dve.tensor_reduce(qss[:, :], qsq[:, :, :], AX_X, ALU.add).then_inc(s_qss, 1)

            def norm_queries(j):
                dve.wait_ge(s_qsd, j + 1)
                dve.reciprocal(qrs[:, :], qsd[:, :]).then_inc(s_qrs, 1)
                dve.wait_ge(s_qrs, j + 1)
                dve.tensor_tensor(qn[:, :, :], qs[:, :, :], over_heads(qrs[:, :], HD0), ALU.mult).then_inc(s_qn, 1)

            def take_turned(b, i):
                dve.wait_ge(s_qunit, unit(b, i) + 1)
                src = qb[:, 0, 0:4 * L].rearrange("p (a l) -> p a l", a=4)
                g = 4 * (i - 3)
                dve.tensor_copy(qblk[0:HD0, g:g + 4, 0, :], src[0:HD0])
                dve.tensor_copy(qblk[HD0:D, g:g + 4, 1, :], src[HD0:D]).then_inc(s_qfree, 1)

            def take_absorbed(b, u, i):
                heads = slice(4 * L * (i - 5), 4 * L * (i - 4))
                dve.wait_ge(s_qp_high, 4 * (b + 1) + i - 4)
                dve.tensor_tensor(qp_low[u][:, heads], qb[:, 0, 0:4 * L], qp_high[u][:, heads].bitcast(F32),
                                  ALU.subtract).then_inc(s_qfree, twice(b, i))

            def add_out(b, i, to):
                dve.wait_ge(s_qunit, unit(b, i) + 1)
                dve.wait_ge(s_qfree, unit(b, i))
                xb = x[:, bass.ds(to, 1), :].rearrange("l b d -> l (b d)")
                dve.tensor_tensor(xb, xb, qb[0:L, 0, 0:D], ALU.add).then_inc(s_qfree, 1)

            def key_roots(j, u):
                dve.wait_ge(s_ksd, j + 1)
                dve.reciprocal(krs[u][:, :, :], ksd[:, :, :]).then_inc(s_krs, 1)

            def scale_scores(b, u, s):
                half, c = s // CH, s % CH
                r, i = rows(c), item_of[s]
                dve.wait_ge(s_item, ITEMS * b + i + 1)
                if s == 0:
                    dve.wait_ge(s_krs, b + 1)
                if not (isinstance(b, int) and b == 0 and s < 4):
                    dve.wait_ge(s_pv, NS * b + s - 3)
                    dve.wait_ge(s_acc, NS * b + s - 3)
                scale = krs[u][0:r, c, 8 * half:8 * half + 8].rearrange("p (a h) -> p a h", a=2)
                dve.tensor_tensor(p[s % 4][0:r, :].rearrange("p (a h l) -> p a h l", a=2, h=4),
                                  ring[0:r, 2 * (i % 2):2 * (i % 2) + 2, 0:4 * L].rearrange("p a (h l) -> p a h l", h=4),
                                  scale.unsqueeze(3).to_broadcast([r, 2, 4, L]), ALU.mult)\
                   .then_inc(s_free, 2 if isinstance(b, int) and b == 0 and s == 1 else 1)

            def take_bias(j, u):
                if not (isinstance(j, int) and j < 2):
                    dve.wait_ge(s_exp, NS * (j - 1))
                dve.tensor_scalar(bias[u][:, :], k["mask_bias"][:, bass.ds(j, 1), :].rearrange("p b c -> p (b c)"),
                                  0.0, None, ALU.add).then_inc(s_bias, 1)

            def take_sums(b, half):
                dve.wait_ge(s_pv, NS * b + CH * (half + 1))
                dve.tensor_copy(oraw[:, :].rearrange("p (a n) -> p a n", a=2), pvb[:, :, 0:4 * L]).then_inc(s_oraw, 1)

            def take_softmax_sums(b, i):
                dve.wait_ge(s_item, ITEMS * b + i + 1)
                r = 2 * (i % 2)
                dve.tensor_copy(rden[:, :].rearrange("p (a n) -> p a n", a=2), ring[:, r:r + 2, 0:4 * L])\
                   .then_inc(s_free, 1)

            def invert_sums(b, i, j, done):
                dve.wait_ge(s_free, ITEMS * b + i + 1)
                dve.reciprocal(rden[:, 2 * j * L:2 * (j + 1) * L], rden[:, 2 * j * L:2 * (j + 1) * L])\
                   .then_inc(s_rden, 1)

            def norm_sums(done):
                dve.wait_ge(s_rden, 4 * (done + 1))
                dve.wait_ge(s_oraw, done + 1)
                dve.tensor_tensor(onorm[:, :], oraw[:, :], rden[:, :], ALU.mult).then_inc(s_on, 1)

            def batch(b, u, nth, prep=True, tail=True):
                for s in range(NS):
                    if s == 2 and tail:
                        take_softmax_sums(b, TAIL_ITEM)
                    if s == 14:
                        take_softmax_sums(b, DEN_ITEM)
                    scale_scores(b, u, s)
                    if s in (2, 3, 4, 5) and tail:
                        invert_sums(b, TAIL_ITEM, s - 2, 2 * b - 1)
                    if s in (14, 15, 16, 17):
                        invert_sums(b, DEN_ITEM, s - 14, 2 * b)
                    if s == 5 and tail:
                        norm_sums(2 * b - 1)
                    if s == 17:
                        norm_sums(2 * b)
                    for i in norms_at[s - 1] if prep and s >= 1 else []:
                        sum_squares(b + 1, i)
                    if prep and s == 5:
                        take_bias(b + 1, 1 - u)
                    if s == 12:
                        take_sums(b, 0)
                    if s == 7 and tail:
                        add_out(b, 0, b - 1)
                    if prep and s in (8, 9):
                        take_queries(b, s - 7)
                    if prep and s == 11:
                        sum_query_squares(b + 1)
                    if prep and s == 13:
                        norm_queries(b + 1)
                    if prep and s in (15, 16):
                        take_turned(b, s - 12)
                    if prep and s in (18, 19, 20, 21):
                        take_absorbed(b, 1 - u, s - 13)
                    if s == 22:
                        add_out(b, 9, b)
                    if prep and s == 22:
                        key_roots(b + 1, 1 - u)
                take_sums(b, 1)

            dve.tensor_copy(wk_high[:, :], wk[:, :]).then_inc(s_split, 1)
            dve.wait_ge(s_split, 1)
            dve.tensor_tensor(wk_low[:, :], wk[:, :], wk_high[:, :].bitcast(F32), ALU.subtract).then_inc(s_split, 1)
            dve.memset(qblk[:, :, :, :], 0.0)
            dve.memset(kss[:, :, :], 1.0).then_inc(s_blk0, 1)
            dve.wait_ge(s_blk0, 1)
            take_bias(0, 0)
            for s in range(NS):
                sum_squares(0, s)
            take_queries(-1, 1)
            take_queries(-1, 2)
            sum_query_squares(0)
            norm_queries(0)
            for i in (3, 4):
                take_turned(-1, i)
            for i in (5, 6, 7, 8):
                take_absorbed(-1, 0, i)
            key_roots(0, 0)
            batches(dve, batch)
            take_softmax_sums(B, 0)
            for j in range(4):
                invert_sums(B, 0, j, 2 * B - 1)
            norm_sums(2 * B - 1)
            add_out(B, 0, B - 1)



def route(nc, tag, k, x, xT, router, router_row, down_bias, share, pair_softmax):
    with Net(nc) as n:
        def t(name, e=True, dt=F32):
            return n.sb(f"{tag}_{name}", [L, B, E] if e else [L, B], dt)

        lg, hot, best, lg2, ex = t("lg"), t("hot"), t("best"), t("lg2"), t("ex")
        m1, pick, m2, den, rden, gap, egap = [t(v, False) for v in ("m1", "pick", "m2", "den", "rden", "gap", "egap")]
        shareT = n.sb(f"{tag}_shareT", [E, T])
        lgp = n.ps(f"{tag}_lgp", 1)
        shp = n.ps(f"{tag}_shp", 4)
        s_lg = n.sem(f"{tag}_s_lg")
        s_v = n.sem(f"{tag}_s_v")
        s_ex = n.sem(f"{tag}_s_ex")
        s_share = n.sem(f"{tag}_s_share")
        s_turn = n.sem(f"{tag}_s_turn")
        s_st = n.sem(f"{tag}_s_st")
        s_bias = n.sem(f"{tag}_s_bias")
        s_add = n.sem(f"{tag}_s_add")
        wide = [L, B, E]
        block = n.ctx.enter_context(nc.Block())

        @block.tensor
        def _(pe):
            for b in range(B):
                m = pe.matmul(lgp[0:L, 0, b * E:(b + 1) * E], xT[:, b * L:(b + 1) * L], router,
                              start=True, stop=True)
            m.then_inc(s_lg, 1)
            pe.wait_ge(s_share, 1)
            for b in range(B):
                m = pe.transpose(shp[0:E, b // 4, (b % 4) * L:(b % 4 + 1) * L], share[:, b, :],
                                 k["ident"][0:L, 0:L])
                if b % 4 == 3:
                    m.then_inc(s_turn, 1)
            for b in range(B):
                pe.wait_ge(s_st, b // 4 + 1)
                m = pe.matmul(shp[0:L, b // 4, (b % 4) * D:(b % 4 + 1) * D], shareT[:, b * L:(b + 1) * L],
                              down_bias, start=True, stop=True)
                if b % 4 == 3:
                    m.then_inc(s_bias, 1)

        @block.scalar
        def _(act):
            if pair_softmax:
                act.wait_ge(s_v, 9)
                act.activation(egap[:, :], gap[:, :], ACT.Exp).then_inc(s_ex, 1)
            else:
                act.wait_ge(s_v, 10)
                act.activation(ex[:, :, :], lg2[:, :, :], ACT.Exp).then_inc(s_ex, 1)

        @block.vector
        def _(dve):
            step = [0]

            def then(ins):
                step[0] += 1
                ins.then_inc(s_v, 1)
                dve.wait_ge(s_v, step[0])

            dve.wait_ge(s_lg, 1)
            then(dve.tensor_tensor(lg[:, :, :], lgp[0:L, 0, 0:B * E].rearrange("l (b e) -> l b e", b=B),
                                   router_row.unsqueeze(1).to_broadcast(wide), ALU.add))
            rank = k["rank_row"][:, :].unsqueeze(1).to_broadcast(wide)
            then(dve.tensor_reduce(m1[:, :], lg[:, :, :], AX_X, ALU.max))
            then(dve.tensor_tensor(hot[:, :, :], lg[:, :, :], over_heads(m1[:, :], E), ALU.is_ge))
            then(dve.tensor_tensor(hot[:, :, :], hot[:, :, :], rank, ALU.mult))
            then(dve.tensor_reduce(pick[:, :], hot[:, :, :], AX_X, ALU.max))
            then(dve.tensor_tensor(best[:, :, :], hot[:, :, :], over_heads(pick[:, :], E), ALU.is_ge))
            then(dve.scalar_tensor_tensor(out=lg2[:, :, :].rearrange("l b e -> l (b e)"),
                                          in0=best[:, :, :].rearrange("l b e -> l (b e)"), scalar=-1e30,
                                          in1=lg[:, :, :].rearrange("l b e -> l (b e)"),
                                          op0=ALU.mult, op1=ALU.add))
            then(dve.tensor_reduce(m2[:, :], lg2[:, :, :], AX_X, ALU.max))
            if pair_softmax:
                then(dve.tensor_tensor(gap[:, :], m2[:, :], m1[:, :], ALU.subtract))
                then(dve.tensor_tensor(hot[:, :, :], lg2[:, :, :], over_heads(m2[:, :], E), ALU.is_ge))
            else:
                then(dve.tensor_tensor(hot[:, :, :], lg2[:, :, :], over_heads(m2[:, :], E), ALU.is_ge))
                then(dve.tensor_tensor(lg2[:, :, :], lg[:, :, :], over_heads(m1[:, :], E), ALU.subtract))
            then(dve.tensor_tensor(hot[:, :, :], hot[:, :, :], rank, ALU.mult))
            then(dve.tensor_reduce(pick[:, :], hot[:, :, :], AX_X, ALU.max))
            then(dve.tensor_tensor(hot[:, :, :], hot[:, :, :], over_heads(pick[:, :], E), ALU.is_ge))
            dve.wait_ge(s_ex, 1)
            if pair_softmax:
                then(dve.tensor_scalar(den[:, :], egap[:, :], 1.0, None, ALU.add))
                then(dve.reciprocal(rden[:, :], den[:, :]))
                then(dve.tensor_tensor(hot[:, :, :], hot[:, :, :], over_heads(egap[:, :], E), ALU.mult))
                then(dve.tensor_tensor(hot[:, :, :], hot[:, :, :], best[:, :, :], ALU.add))
                dve.tensor_tensor(share[:, :, :], hot[:, :, :], over_heads(rden[:, :], E), ALU.mult).then_inc(s_share, 1)
            else:
                then(dve.tensor_reduce(den[:, :], ex[:, :, :], AX_X, ALU.add))
                then(dve.reciprocal(rden[:, :], den[:, :]))
                then(dve.tensor_tensor(hot[:, :, :], hot[:, :, :], best[:, :, :], ALU.add))
                then(dve.tensor_tensor(hot[:, :, :], hot[:, :, :], ex[:, :, :], ALU.mult))
                dve.tensor_tensor(share[:, :, :], hot[:, :, :], over_heads(rden[:, :], E), ALU.mult).then_inc(s_share, 1)
            for g in range(4):
                dve.wait_ge(s_turn, g + 1)
                dve.tensor_copy(shareT[:, 4 * g * L:4 * (g + 1) * L], shp[0:E, g, 0:4 * L]).then_inc(s_st, 1)
            for g in range(4):
                dve.wait_ge(s_bias, g + 1)
                xg = x[:, 4 * g:4 * g + 4, :].rearrange("l b d -> l (b d)")
                dve.tensor_tensor(xg, xg, shp[0:L, g, :], ALU.add).then_inc(s_add, 1)


def down_and_share(n, pe, down, e_slot, hid, weight, chunks):
    for a in range(4):
        for j in range(chunks):
            t = pe.matmul(down[0:L, e_slot, a * D:(a + 1) * D], hid[:, j, a * L:(a + 1) * L], weight[:, j, :],
                          start=(j == 0), stop=(j == chunks - 1))
    return t


def add_shares(dve, s_share, s_free, count, down, slot, x, share, g, e):
    dve.wait_ge(s_free, count)
    for a in range(4):
        xb = x[:, bass.ds(4 * g + a, 1), :].rearrange("l b d -> l (b d)")
        t = dve.scalar_tensor_tensor(out=xb, in0=down[0:L, slot, a * D:(a + 1) * D],
                                     scalar=share[:, bass.ds(4 * g + a, 1), e], in1=xb,
                                     op0=ALU.mult, op1=ALU.add)
    t.then_inc(s_free, 1)


def gated_experts(nc, k, x, xT, w_up, b_up, w_down, share):
    N = 4 * L
    with Net(nc) as n:
        hid_ps = n.ps("ge_hid", 4)
        down = n.ps("ge_down", 2)
        gate = n.sb("gate", [D, 2, N])
        up = n.sb("up", [D, 2, N])
        sig = n.sb("sig", [D, 2, N])
        glu = n.sb("glu", [D, 2, N])
        hid = [n.sb(f"ge_hid{i}", [D, 2, N]) for i in range(2)]
        s_mm = n.sem("ge_mm")
        s_gate = n.sem("ge_gate")
        s_up = n.sem("ge_up")
        s_sig = n.sem("ge_sig")
        s_clip = n.sem("ge_clip")
        s_glu = n.sem("ge_glu")
        s_hid = n.sem("ge_hid_s")
        s_down = n.sem("ge_down_s")
        s_dfree = n.sem("ge_dfree")
        s_pre = n.sem("ge_pre")
        U = 2 * E
        block = n.ctx.enter_context(nc.Block())

        def groups(eng, group):
            group(0)
            with eng.Fori(1, 4) as g:
                group(g)

        @block.tensor
        def _(pe):
            def group(g):
                def downs(e):
                    pe.wait_ge(s_hid, U * g + 2 * e + 2)
                    if not (isinstance(g, int) and e < 2):
                        pe.wait_ge(s_dfree, E * g + e - 1)
                    down_and_share(n, pe, down, e % 2, hid[e % 2], w_down[:, e, :, :], 2).then_inc(s_down, 1)

                for e in range(E):
                    for j in range(2):
                        u = 2 * e + j
                        if not (isinstance(g, int) and u < 2):
                            pe.wait_ge(s_gate, U * g + u - 1)
                            pe.wait_ge(s_up, U * g + u - 1)
                        for v in range(2):
                            t = pe.matmul(hid_ps[:, 2 * (u % 2) + v, 0:N],
                                          w_up[:, e, v * I0 + j * D:v * I0 + (j + 1) * D],
                                          xT[:, bass.ds(g * N, N)], start=True, stop=True)
                        t.then_inc(s_mm, 1)
                    if e:
                        downs(e - 1)
                downs(E - 1)
            groups(pe, group)

        @block.scalar
        def _(act):
            def group(g):
                for u in range(U):
                    act.wait_ge(s_mm, U * g + u + 1)
                    if not (isinstance(g, int) and u < 2):
                        act.wait_ge(s_hid, U * g + u - 1)
                    act.activation(up[:, u % 2, :], hid_ps[:, 2 * (u % 2) + 1, 0:N], ACT.Identity,
                                   bias=b_up[:, u // 2, 2 + u % 2:3 + u % 2]).then_inc(s_up, 1)
                    act.wait_ge(s_gate, U * g + u + 1)
                    act.activation(sig[:, u % 2, :], gate[:, u % 2, :], ACT.Sigmoid, scale=1.702).then_inc(s_sig, 1)
            groups(act, group)

        @block.gpsimd
        def _(pool):
            def group(g):
                for u in range(U):
                    pool.wait_ge(s_sig, U * g + u + 1)
                    pool.tensor_tensor(glu[:, u % 2, :], gate[:, u % 2, :], sig[:, u % 2, :], ALU.mult).then_inc(s_glu, 1)
            groups(pool, group)

        @block.vector
        def _(dve):
            def group(g):
                def first(u):
                    dve.wait_ge(s_mm, U * g + u + 1)
                    if not (isinstance(g, int) and u < 2):
                        dve.wait_ge(s_glu, U * g + u - 1)
                    dve.tensor_scalar(gate[:, u % 2, :], hid_ps[:, 2 * (u % 2), 0:N],
                                      b_up[:, u // 2, u % 2:u % 2 + 1], 7.0, ALU.add, ALU.min).then_inc(s_gate, 1)
                    dve.wait_ge(s_up, U * g + u + 1)
                    dve.tensor_scalar(up[:, u % 2, :], up[:, u % 2, :], 7.0, -7.0, ALU.min, ALU.max).then_inc(s_clip, 1)

                def second(u):
                    dve.wait_ge(s_glu, U * g + u + 1)
                    dve.wait_ge(s_clip, U * g + u + 1)
                    e = u // 2
                    if not (isinstance(g, int) and e < 2):
                        dve.wait_ge(s_down, E * g + e - 1)
                    dve.scalar_tensor_tensor(out=hid[e % 2][:, u % 2, :], in0=up[:, u % 2, :], scalar=1.0,
                                             in1=glu[:, u % 2, :], op0=ALU.add, op1=ALU.mult).then_inc(s_hid, 1)

                def shares(e):
                    dve.wait_ge(s_down, E * g + e + 1)
                    add_shares(dve, None, s_dfree, E * g + e, down, e % 2, x, share, g, e) if not (
                        isinstance(g, int) and e == 0) else add_first(e)

                def add_first(e):
                    for a in range(4):
                        t = dve.scalar_tensor_tensor(out=x[:, a, :], in0=down[0:L, 0, a * D:(a + 1) * D],
                                                     scalar=share[:, a, e:e + 1], in1=x[:, a, :],
                                                     op0=ALU.mult, op1=ALU.add)
                    t.then_inc(s_dfree, 1)

                for u in range(U):
                    first(u)
                    if u:
                        second(u - 1)
                    if u >= 4 and u % 2 == 0:
                        shares(u // 2 - 2)
                second(U - 1)
                shares(E - 2)
                shares(E - 1)
            groups(dve, group)


def relu_experts(nc, k, x, xT, w_up, b_up, w_down, share):
    N = 4 * L
    with Net(nc) as n:
        hid_ps = n.ps("re_hid", 4)
        down = n.ps("re_down", 2)
        hid = [n.sb(f"re_hid{i}", [D, 4, N]) for i in range(2)]
        s_mm = n.sem("re_mm")
        s_hid = n.sem("re_hid_s")
        s_down = n.sem("re_down_s")
        s_dfree = n.sem("re_dfree")
        U = 4 * E
        block = n.ctx.enter_context(nc.Block())

        def groups(eng, group):
            group(0)
            with eng.Fori(1, 4) as g:
                group(g)

        @block.tensor
        def _(pe):
            def group(g):
                def downs(e):
                    pe.wait_ge(s_hid, U * g + 4 * e + 4)
                    if not (isinstance(g, int) and e < 2):
                        pe.wait_ge(s_dfree, E * g + e - 1)
                    down_and_share(n, pe, down, e % 2, hid[e % 2], w_down[:, e, :, :], 4).then_inc(s_down, 1)

                for e in range(E):
                    for j in range(4):
                        u = 4 * e + j
                        if not (isinstance(g, int) and u < 4):
                            pe.wait_ge(s_hid, U * g + u - 3)
                        pe.matmul(hid_ps[:, j, 0:N], w_up[:, e, j * D:(j + 1) * D],
                                  xT[:, bass.ds(g * N, N)], start=True, stop=True).then_inc(s_mm, 1)
                    if e:
                        downs(e - 1)
                downs(E - 1)
            groups(pe, group)

        @block.scalar
        def _(act):
            def group(g):
                for u in range(U):
                    e, j = u // 4, u % 4
                    act.wait_ge(s_mm, U * g + u + 1)
                    if not (isinstance(g, int) and e < 2):
                        act.wait_ge(s_down, E * g + e - 1)
                    act.activation(hid[e % 2][:, j, :], hid_ps[:, j, 0:N], ACT.Relu,
                                   bias=b_up[:, e, j:j + 1]).then_inc(s_hid, 1)
            groups(act, group)

        @block.vector
        def _(dve):
            def group(g):
                for e in range(E):
                    dve.wait_ge(s_down, E * g + e + 1)
                    if not (isinstance(g, int) and e == 0):
                        dve.wait_ge(s_dfree, E * g + e)
                    for a in range(4):
                        xb = x[:, bass.ds(4 * g + a, 1), :].rearrange("l b d -> l (b d)")
                        t = dve.scalar_tensor_tensor(out=xb, in0=down[0:L, e % 2, a * D:(a + 1) * D],
                                                     scalar=share[:, bass.ds(4 * g + a, 1), e], in1=xb,
                                                     op0=ALU.mult, op1=ALU.add)
                    t.then_inc(s_dfree, 1)
            groups(dve, group)



def linear_attention(nc, k, x, xT):
    W = D + 1
    WO = D + HEADS
    with Net(nc) as n:
        qlow = n.sb("la_qlow", [D, T])
        qT = n.sb("la_qT", [D, T])
        kf = n.sb("la_kf", [L, B, D])
        klow = n.sb("la_klow", [L, B, D])
        v1 = n.sb("la_v", [L, B, W])
        kv = n.sb("la_kv", [D, B, WO])
        o = n.sb("la_o", [L, B, D])
        nrm = n.sb("la_nrm", [L, B, HEADS])
        rnrm = n.sb("la_rnrm", [L, B, HEADS])
        banks = n.ps("la_banks", 8)
        s_q = n.sem("la_s_q")
        s_qe = n.sem("la_s_qe")
        s_qx = n.sem("la_s_qx")
        s_kvp = n.sem("la_s_kvp")
        s_ke = n.sem("la_s_ke")
        s_kx = n.sem("la_s_kx")
        s_f = n.sem("la_s_f")
        s_kvm = n.sem("la_s_kvm")
        s_kve = n.sem("la_s_kve")
        s_o = n.sem("la_s_o")
        s_oe = n.sem("la_s_oe")
        s_turn = n.sem("la_s_turn")
        s_te = n.sem("la_s_te")
        s_one = n.sem("la_s_one")
        block = n.ctx.enter_context(nc.Block())

        @block.tensor
        def _(pe):
            for g in range(4):
                pe.matmul(banks[:, g, 0:4 * L], k["wq1"][:, :], xT[:, 4 * g * L:4 * (g + 1) * L],
                          start=True, stop=True).then_inc(s_q, 1)
            for b in range(B):
                if b % 2 == 0 and b >= 8:
                    pe.wait_ge(s_ke, 2 * (b // 2 - 4) + 2)
                t = pe.matmul(banks[0:L, 4 + b // 2 % 4, (b % 2) * 2 * D:(b % 2 + 1) * 2 * D],
                              xT[:, b * L:(b + 1) * L], k["wkv1"][:, :], start=True, stop=True)
                if b % 2:
                    t.then_inc(s_kvp, 1)
            pe.wait_ge(s_f, 2)
            pe.wait_ge(s_qe, 8)
            for b in range(B):
                t = pe.matmul(banks[:, b // 3, (b % 3) * W:(b % 3 + 1) * W], kf[:, b, :], v1[:, b, :],
                              start=True, stop=True)
                if b % 3 == 2 or b == B - 1:
                    t.then_inc(s_kvm, 1)
            for b in range(B):
                if b % 3 == 0:
                    pe.wait_ge(s_kve, min(b + 3, B))
                t = pe.matmul(banks[0:L, b // 3, (b % 3) * WO:(b % 3 + 1) * WO], qT[:, b * L:(b + 1) * L],
                              kv[:, b, :], start=True, stop=True)
                if b % 3 == 2 or b == B - 1:
                    t.then_inc(s_o, 1)
            for b in range(B):
                if b % 4 == 0:
                    pe.wait_ge(s_oe, 6)
                t = pe.transpose(banks[:, b // 4, (b % 4) * L:(b % 4 + 1) * L], o[:, b, :], k["ident"][0:L, 0:L])
                if b % 4 == 3:
                    t.then_inc(s_turn, 1)

        @block.scalar
        def _(act):
            for g in range(4):
                act.wait_ge(s_qe, 2 * g + 2)
                act.activation(qlow[:, 4 * g * L:4 * (g + 1) * L], qlow[:, 4 * g * L:4 * (g + 1) * L],
                               ACT.Exp).then_inc(s_qx, 1)
            act.wait_ge(s_f, 1)
            act.activation(klow[:, :, :], klow[:, :, :], ACT.Exp).then_inc(s_kx, 1)
            for g in range(4):
                act.wait_ge(s_turn, g + 1)
                act.activation(xT[:, 4 * g * L:4 * (g + 1) * L], banks[:, g, 0:4 * L], ACT.Copy).then_inc(s_te, 1)

        @block.vector
        def _(dve):
            dve.memset(v1[:, :, D:W], 1.0).then_inc(s_one, 1)
            for g in range(4):
                cols = slice(4 * g * L, 4 * (g + 1) * L)
                dve.wait_ge(s_q, g + 1)
                dve.tensor_scalar(qT[:, cols], banks[:, g, 0:4 * L], k["bq1"][:, 0:1], 0.0, ALU.add,
                                  ALU.max).then_inc(s_qe, 1)
                dve.tensor_scalar(qlow[:, cols], banks[:, g, 0:4 * L], k["bq1"][:, 0:1], 0.0, ALU.add,
                                  ALU.min).then_inc(s_qe, 1)
            for r in range(B // 2):
                dve.wait_ge(s_kvp, r + 1)
                bank = banks[0:L, 4 + r % 4, :].rearrange("l (b m) -> l b m", b=2)
                dve.tensor_tensor(kf[:, 2 * r:2 * r + 2, :], bank[:, :, 0:D],
                                  k["bk1_row"][:, :].unsqueeze(1).to_broadcast([L, 2, D]), ALU.add).then_inc(s_ke, 1)
                dve.tensor_tensor(v1[:, 2 * r:2 * r + 2, 0:D], bank[:, :, D:2 * D],
                                  k["bv1_row"][:, :].unsqueeze(1).to_broadcast([L, 2, D]), ALU.add).then_inc(s_ke, 1)
            dve.wait_ge(s_ke, B)
            dve.tensor_scalar(klow[:, :, :], kf[:, :, :], 0.0, None, ALU.min).then_inc(s_f, 1)
            for g in range(4):
                cols = slice(4 * g * L, 4 * (g + 1) * L)
                dve.wait_ge(s_qx, g + 1)
                dve.tensor_tensor(qT[:, cols], qT[:, cols], qlow[:, cols], ALU.add).then_inc(s_one, 1)
            dve.wait_ge(s_kx, 1)
            dve.scalar_tensor_tensor(out=kf[:, :, :].rearrange("l b d -> l (b d)"),
                                     in0=kf[:, :, :].rearrange("l b d -> l (b d)"), scalar=0.0,
                                     in1=klow[:, :, :].rearrange("l b d -> l (b d)"),
                                     op0=ALU.max, op1=ALU.add).then_inc(s_f, 1)
            for b in range(B):
                dve.wait_ge(s_kvm, b // 3 + 1)
                m = banks[:, b // 3, (b % 3) * W:(b % 3 + 1) * W]
                dve.tensor_tensor(kv[:, b, 0:D], m[:, 0:D], k["same_head"][:, :], ALU.mult)
                dve.tensor_scalar(kv[:, b, D:WO], k["head_of"][:, :], m[:, D:W], None, ALU.mult).then_inc(s_kve, 1)
            for r in range(6):
                nb = min(3, B - 3 * r)
                dve.wait_ge(s_o, r + 1)
                src = banks[0:L, r, 0:nb * WO].rearrange("l (b m) -> l b m", b=nb)
                rows_ = slice(3 * r, 3 * r + nb)
                dve.tensor_scalar(nrm[:, rows_, :], src[:, :, D:WO], 1e-6, None, ALU.add).then_inc(s_one, 1)
                dve.wait_ge(s_one, 6 + 2 * r)
                dve.reciprocal(rnrm[:, rows_, :], nrm[:, rows_, :]).then_inc(s_one, 1)
                dve.wait_ge(s_one, 7 + 2 * r)
                for b in range(nb):
                    t = dve.tensor_tensor(o[:, 3 * r + b, :].rearrange("l (h d) -> l h d", h=HEADS),
                                          src[:, b, 0:D].rearrange("l (h d) -> l h d", h=HEADS),
                                          over_heads(rnrm[:, 3 * r + b, :], HD1), ALU.mult)
                t.then_inc(s_oe, 1)



def cross_attention_1(nc, k, ctxT_d, x, xT):
    NS = 2 * CH
    TILES = -(-HEADS * L // D)
    THIRDS = [(off(0), off(4)), (off(4), off(8)), (off(8), S)]
    with Net(nc) as n:
        ctxT = [n.sb(f"c1_ctxT{u}", [D, S]) for u in range(2)]
        khigh = n.sb("c1_khigh", [D, S], F32R)
        klow = n.sb("c1_klow", [D, S], F32R)
        kstack = [n.sb(f"c1_kstack{u}", [D, 4, S], F32R) for u in range(2)]
        k16 = n.sb("c1_k16", [D, S], BF16)
        v = [n.sb(f"c1_v{u}", [SP_MAX, CH, D]) for u in range(2)]
        qT = n.sb("c1_qT", [D, L])
        qbias = n.sb("c1_qbias", [STACK, 4])
        qall = n.sb("c1_qall", [STACK, 4, L])
        qparts = n.sb("c1_qparts", [STACK, 4, L], F32R)
        qstack = [n.sb(f"c1_qstack{u}", [STACK + 1, TILES * D], F32R) for u in range(2)]
        q16 = n.sb("c1_q16", [D, HEADS * L], BF16)
        mx = n.sb("c1_mx", [D, TILES, 3])
        negmx = n.sb("c1_negmx", [D, TILES])
        neg = n.sb("c1_neg", [TILES, D], F32R)
        p = [n.sb(f"c1_p{j}", [SP_MAX, HALF]) for j in range(4)]
        own = n.sb("c1_own", [D, 4, L])
        own_den = n.sb("c1_own_den", [D, 4, L])
        rden = n.sb("c1_rden", [D, L])
        cat = n.sb("c1_cat", [D, L])
        ring = n.ps("c1_ring", 4)
        pvb = n.ps("c1_pvb", 1)
        denb = n.ps("c1_denb", 1)
        aux = n.ps("c1_aux", 2)

        s_ctx = [n.sem(f"c1_s_ctx{u}") for u in range(2)]
        s_unit = n.sem("c1_s_unit")
        s_ufree = n.sem("c1_s_ufree")
        s_high = n.sem("c1_s_high")
        s_k16 = n.sem("c1_s_k16")
        s_stack = n.sem("c1_s_stack")
        s_qhigh = n.sem("c1_s_qhigh")
        s_qlow = n.sem("c1_s_qlow")
        s_qstack = n.sem("c1_s_qstack")
        s_q16 = n.sem("c1_s_q16")
        s_neg = n.sem("c1_s_neg")
        s_row = n.sem("c1_s_row")
        s_score = n.sem("c1_s_score")
        s_exp = n.sem("c1_s_exp")
        s_pv = n.sem("c1_s_pv")
        s_take = n.sem("c1_s_take")
        s_fin = n.sem("c1_s_fin")
        s_cat = n.sem("c1_s_cat")
        s_one = n.sem("c1_s_one")
        s_ones = n.sem("c1_s_ones")

        UNITS, TAIL, MAXIMA, TURN = 48, 7, 8, 47

        def unit(b, i):
            if isinstance(b, int) and b >= B - 1:
                return UNITS * B + b - (B - 1)
            return UNITS * (b + 1) + i

        def twice(b, i):
            return 2 if isinstance(b, int) and b <= 0 and i == TAIL - 1 else 1

        plan = {0: [0], 1: [1], 2: [2, 3], 3: [4, 5], 4: [6, TAIL], 21: [TURN]}
        FIRST, AFTER = 5, 21
        for i in range(3 * TILES):
            plan.setdefault(FIRST + i * (AFTER - FIRST) // (3 * TILES), []).append(MAXIMA + i)
        first_plan = [i for i in range(UNITS) if i != TAIL]

        block = n.ctx.enter_context(nc.Block())

        def batches(eng, batch):
            batch(0, 0, 1, tail=False)
            with eng.Fori(0, (B - 2) // 2) as i:
                batch(2 * i + 1, 1, i + 2)
                batch(2 * i + 2, 0, i + 2)
            batch(B - 1, 1, 0, prep=False)

        def planned(s, prep, tail):
            for i in plan.get(s, []):
                if tail if i == TAIL else prep:
                    yield i

        @block.sync
        def _(sp):
            def load(b, u):
                sp.dma_start(ctxT[u][:, :], ctxT_d[bass.ds(b, 1), :, :].rearrange("b d s -> (b d) s"))\
                  .then_inc(s_ctx[u], 16)

            def stack_keys(b, u):
                sp.wait_ge(s_ufree, unit(b - 1, 3))
                for g in range(4):
                    for part, src in enumerate((khigh, khigh, klow)):
                        sp.dma_start(kstack[u][32 * part:32 * part + 32, g, :].bitcast(F32),
                                     src[32 * g:32 * g + 32, :].bitcast(F32)).then_inc(s_stack, 16)

            def send_row(b, u):
                sp.wait_ge(s_ufree, unit(b - 1, TURN) + 1)
                sp.dma_start(qstack[u][STACK:STACK + 1, :].bitcast(F32).rearrange("a (t p) -> a t p", t=TILES),
                             neg[:, :].bitcast(F32)).then_inc(s_row, 16)

            load(0, 0)
            load(1, 1)
            stack_keys(0, 0)
            send_row(0, 0)
            with sp.Fori(0, (B - 2) // 2) as i:
                for u in range(2):
                    b = 2 * i + u
                    sp.wait_ge(s_unit, unit(b - 1, TAIL))
                    load(b + 2, u)
                    stack_keys(b + 1, 1 - u)
                    send_row(b + 1, 1 - u)
            stack_keys(B - 1, 1)
            send_row(B - 1, 1)

        @block.tensor
        def _(pe):
            def do(b, u, i):
                before = unit(b, i)
                last = isinstance(b, int) and b >= B - 1
                if last:
                    pe.wait_ge(s_ufree, before)
                elif not (isinstance(b, int) and b == -1 and i < 2):
                    pe.wait_ge(s_ufree, before - 1)
                bank = i % 2
                if i < 3:
                    lo, hi = THIRDS[i]
                    t = pe.matmul(aux[:, bank, 0:hi - lo], k["wk2"][:, :], ctxT[u][:, lo:hi], start=True, stop=True)
                elif i == 3:
                    tokens = xT[:, bass.ds((b + 1) * L, L)]
                    for g in range(4):
                        pe.matmul(aux[0:STACK, bank, g * L:(g + 1) * L], k["wq2_thrice"][:, g, :], tokens,
                                  start=True, stop=True)
                    t = pe.matmul(aux[:, bank, 4 * L:5 * L], k["wq2"][:, :], tokens, start=True, stop=True)
                elif i < TAIL:
                    for a in range(4):
                        c = 4 * (i - 4) + a
                        t = pe.matmul(aux[0:rows(c), bank, a * D:(a + 1) * D], ctxT[u][:, off(c):off(c) + rows(c)],
                                      k["wv2"][:, :], start=True, stop=True)
                elif i == TAIL:
                    pe.wait_ge(s_cat, b)
                    t = pe.matmul(aux[0:L, bank, 0:D], cat[:, :], k["wo2T"][:, :], start=True, stop=True)
                elif i < TURN:
                    t_, part = (i - MAXIMA) // 3, (i - MAXIMA) % 3
                    lo, hi = THIRDS[part]
                    if i == MAXIMA:
                        pe.wait_ge(s_k16, b + 2)
                        pe.wait_ge(s_q16, b + 2)
                    m = min(D, HEADS * L - t_ * D)
                    t = pe.matmul(aux[0:m, bank, 0:hi - lo], q16[:, t_ * D:t_ * D + m], k16[:, lo:hi],
                                  start=True, stop=True)
                else:
                    pe.wait_ge(s_neg, b + 2)
                    t = pe.transpose(aux[0:TILES, bank, 0:D], negmx[:, :], k["ident"][:, :])
                t.then_inc(s_unit, twice(b, i))

            def score(b, u, s):
                half, c = s // CH, s % CH
                r = rows(c)
                if s == 0:
                    pe.wait_ge(s_row, 16 * (b + 1))
                    pe.wait_ge(s_stack, 12 * 16 * (b + 1))
                    pe.wait_ge(s_qstack, b + 1)
                if not (isinstance(b, int) and b == 0 and s < 2):
                    pe.wait_ge(s_exp, NS * b + s - 1)
                for a in range(2):
                    g = 2 * half + a
                    t = pe.matmul(ring[0:r, 2 * (s % 2) + a, 0:4 * L], kstack[u][0:STACK + 1, g, off(c):off(c) + r],
                                  qstack[u][:, 4 * g * L:4 * (g + 1) * L], start=True, stop=True)
                t.then_inc(s_score, 1)

            def weigh(b, u, s):
                half, c = s // CH, s % CH
                r = rows(c)
                if c == 0 and not (isinstance(b, int) and b == 0):
                    pe.wait_ge(s_take, 2 * b + half - 1)
                pe.wait_ge(s_exp, NS * b + s + 1)
                st, sp_ = c == 0, c == CH - 1
                for a in range(2):
                    g = 2 * half + a
                    pe.matmul(pvb[32 * g:32 * g + 32, 0, 0:4 * L], v[u][0:r, c, 32 * g:32 * g + 32],
                              p[s % 4][0:r, a * 4 * L:(a + 1) * 4 * L], start=st, stop=sp_)
                for a in range(2):
                    q = (2 * half + a + 2) % 4
                    t = pe.matmul(denb[32 * q:32 * q + 32, 0, 0:4 * L], k["ones"][0:r, 0:32],
                                  p[s % 4][0:r, a * 4 * L:(a + 1) * 4 * L], start=st, stop=sp_)
                t.then_inc(s_pv, 1)

            def batch(b, u, nth, prep=True, tail=True):
                if prep:
                    pe.wait_ge(s_ctx[1 - u], 16 * nth)
                for s in range(NS):
                    score(b, u, s)
                    units = list(planned(s, prep, tail))
                    for i in units[:1]:
                        do(b, 1 - u, i)
                    if s >= 1:
                        weigh(b, u, s - 1)
                    for i in units[1:]:
                        do(b, 1 - u, i)
                weigh(b, u, NS - 1)

            pe.wait_ge(s_ctx[0], 16)
            for i in first_plan:
                do(-1, 0, i)
            pe.wait_ge(s_ones, 2)
            batches(pe, batch)
            do(B, 0, TAIL)

        @block.scalar
        def _(act):
            def keep_high(b, i):
                if i == 0 and not (isinstance(b, int) and b == -1):
                    act.wait_ge(s_stack, 12 * 16 * (b + 1))
                    act.wait_ge(s_k16, b + 1)
                lo, hi = THIRDS[i]
                act.wait_ge(s_unit, unit(b, i) + 1)
                act.activation(khigh[:, lo:hi], aux[:, i % 2, 0:hi - lo], ACT.Identity,
                               bias=k["bk2"][:, 0:1]).then_inc(s_high, 1)

            def keep_high_queries(b):
                act.wait_ge(s_ufree, unit(b, 3) + 1)
                if not (isinstance(b, int) and b == -1):
                    act.wait_ge(s_qstack, b + 1)
                act.activation(qparts[:, :, :], qall[:, :, :], ACT.Copy).then_inc(s_qhigh, 1)

            def narrow(b):
                act.wait_ge(s_ufree, unit(b, 3))
                act.wait_ge(s_high, 3 * (b + 2))
                act.activation(k16[:, :], khigh[:, :].bitcast(F32), ACT.Copy).then_inc(s_k16, 1)

            def batch(b, u, nth, prep=True, tail=True):
                for s in range(NS):
                    r = rows(s % CH)
                    act.wait_ge(s_score, NS * b + s + 1)
                    if not (isinstance(b, int) and b == 0 and s < 4):
                        act.wait_ge(s_pv, NS * b + s - 3)
                    act.activation(p[s % 4][0:r, :].rearrange("p (a n) -> p a n", a=2),
                                   ring[0:r, 2 * (s % 2):2 * (s % 2) + 2, 0:4 * L], ACT.Exp).then_inc(s_exp, 1)
                    if prep and s < 3:
                        keep_high(b, s)
                    if prep and s == 2:
                        keep_high_queries(b)
                        narrow(b)

            for i in range(3):
                keep_high(-1, i)
            keep_high_queries(-1)
            narrow(-1)
            batches(act, batch)

        @block.gpsimd
        def _(pool):
            def stack_queries(b, u):
                pool.wait_ge(s_ufree, unit(b, 3) + 1)
                if not (isinstance(b, int) and b == -1):
                    pool.wait_ge(s_neg, b + 1)
                pool.tensor_tensor(q16[:, :].rearrange("p (h l) -> p h l", h=HEADS), over_heads(k["head_of"][:, :], L),
                                   qT[:, :].unsqueeze(1).to_broadcast([D, HEADS, L]), ALU.mult).then_inc(s_q16, 1)
                pool.wait_ge(s_qhigh, b + 2)
                pool.wait_ge(s_q16, b + 2)
                low = slice(32, 64)
                pool.tensor_tensor(qparts[low, :, :], qall[low, :, :], qparts[low, :, :].bitcast(F32),
                                   ALU.subtract).then_inc(s_qlow, 1)
                pool.wait_ge(s_qlow, b + 2)
                for g in range(4):
                    t = pool.tensor_tensor(
                        qstack[u][0:STACK, 4 * g * L:4 * (g + 1) * L].rearrange("p (h l) -> p h l", h=4),
                        over_heads(k["head_in_four"][0:STACK, :], L),
                        qparts[:, g, :].bitcast(F32).unsqueeze(1).to_broadcast([STACK, 4, L]), ALU.mult)
                t.then_inc(s_qstack, 1)

            def batch(b, u, nth, prep=True, tail=True):
                if prep:
                    stack_queries(b, 1 - u)

            stack_queries(-1, 0)
            batches(pool, batch)

        @block.vector
        def _(dve):
            def take(b, u, i):
                last = isinstance(b, int) and b >= B - 1
                dve.wait_ge(s_unit, unit(b, i) + 1)
                bank = aux[:, i % 2, :]
                j = b + 1
                if i < 3:
                    lo, hi = THIRDS[i]
                    dve.wait_ge(s_high, 3 * j + i + 1)
                    dve.scalar_tensor_tensor(out=klow[:, lo:hi], in0=bank[:, 0:hi - lo], scalar=k["bk2"][:, 0:1],
                                             in1=khigh[:, lo:hi].bitcast(F32), op0=ALU.add,
                                             op1=ALU.subtract).then_inc(s_ufree, 1)
                elif i == 3:
                    if not (isinstance(b, int) and b == -1):
                        dve.wait_ge(s_q16, j)
                        dve.wait_ge(s_qlow, j)
                    dve.tensor_scalar(qT[:, :], bank[:, 4 * L:5 * L], k["bq2"][:, 0:1], HD1 ** -0.5, ALU.add, ALU.mult)
                    dve.scalar_tensor_tensor(out=qall[:, :, :], in0=bank[0:STACK, 0:4 * L].rearrange("p (g l) -> p g l", g=4),
                                             scalar=HD1 ** -0.5, in1=over_heads(qbias[:, :], L), op0=ALU.mult,
                                             op1=ALU.add).then_inc(s_ufree, 1)
                elif i < TAIL:
                    c = 4 * (i - 4)
                    r = rows(c)
                    dve.tensor_copy(v[u][0:r, c:c + 4, :].rearrange("p c d -> p (c d)"), bank[0:r, :])\
                       .then_inc(s_ufree, twice(b, i))
                elif i == TAIL:
                    xb = x[:, bass.ds(b - 1, 1), :].rearrange("l b d -> l (b d)")
                    dve.tensor_tensor(xb, xb, bank[0:L, 0:D], ALU.add).then_inc(s_ufree, 1)
                elif i < TURN:
                    t_, part = (i - MAXIMA) // 3, (i - MAXIMA) % 3
                    lo, hi = THIRDS[part]
                    m = min(D, HEADS * L - t_ * D)
                    dve.tensor_reduce(mx[0:m, t_, part:part + 1], bank[0:m, 0:hi - lo], AX_X,
                                      ALU.max).then_inc(s_ufree, 1)
                    if i == TURN - 1:
                        dve.wait_ge(s_ufree, unit(b, i) + 1)
                        dve.tensor_reduce(negmx[:, :], mx[:, :, :], AX_X, ALU.max, negate=True).then_inc(s_neg, 1)
                else:
                    if not (isinstance(b, int) and b == -1):
                        dve.wait_ge(s_row, 16 * j)
                    dve.tensor_copy(neg[:, :], bank[0:TILES, 0:D]).then_inc(s_ufree, 1)

            def take_half(b, half):
                lo = 64 * half
                for dst, src, at in ((own, pvb, lo), (own_den, denb, 64 - lo)):
                    dve.wait_ge(s_pv, NS * b + CH * (half + 1))
                    t = dve.tensor_tensor(dst[lo:lo + 64, :, :],
                                          src[at:at + 64, 0, 0:4 * L].rearrange("p (j l) -> p j l", j=4),
                                          over_heads(k["head_in_four"][at:at + 64, :], L), ALU.mult)
                t.then_inc(s_take, 1)

            def finish(b):
                dve.wait_ge(s_take, 2 * b + 2)
                dve.tensor_reduce(rden[:, :], own_den[:, :, :].rearrange("p j l -> p l j"), AX_X, ALU.add).then_inc(s_fin, 1)
                dve.tensor_reduce(cat[:, :], own[:, :, :].rearrange("p j l -> p l j"), AX_X, ALU.add)
                dve.wait_ge(s_fin, 3 * b + 1)
                dve.reciprocal(rden[:, :], rden[:, :]).then_inc(s_fin, 1)
                dve.wait_ge(s_fin, 3 * b + 2)
                dve.tensor_tensor(cat[:, :], cat[:, :], rden[:, :], ALU.mult).then_inc(s_fin, 1)
                dve.wait_ge(s_fin, 3 * b + 3)
                dve.tensor_scalar(cat[:, :], cat[:, :], k["bv2"][:, 0:1], None, ALU.add).then_inc(s_cat, 1)

            def batch(b, u, nth, prep=True, tail=True):
                for s in range(NS):
                    if s == 13:
                        take_half(b, 0)
                    for i in planned(s, prep, tail):
                        take(b, 1 - u, i)
                take_half(b, 1)
                finish(b)

            for u in range(2):
                dve.memset(kstack[u][STACK:STACK + 1, :, :].bitcast(F32), 1.0).then_inc(s_ones, 1)
            dve.tensor_scalar(qbias[:, :], k["bq2_thrice"][:, :], HD1 ** -0.5, None, ALU.mult).then_inc(s_one, 1)
            dve.memset(mx[:, :, :], 0.0).then_inc(s_one, 1)
            dve.tensor_tensor(x[:, :, :], x[:, :, :], k["bo2_row"][:, :].unsqueeze(1).to_broadcast([L, B, D]),
                              ALU.add).then_inc(s_one, 1)
            dve.wait_ge(s_one, 3)
            for i in first_plan:
                take(-1, 0, i)
            batches(dve, batch)
            take(B, 0, TAIL)



def decoder(nc, a, out, upto=99):
    with Net(nc) as n:
        def load(name, shape, src=None, dt=F32):
            t = n.sb(name, shape, dt)
            pairs.append((t[tuple(slice(None) for _ in shape)], a[name] if src is None else src))
            return t

        def row(name, m):
            return load(name, [L if m != HD0 else SP_MAX, m], a[name].partition_broadcast(L if m != HD0 else SP_MAX))

        pairs = []
        k = {}
        k["norms"] = k["projects"] = 0
        k["norm_sems"] = [n.sem(f"s_{v}") for v in ("stats", "sd", "rstd", "normed", "turned", "evacuated", "out")]
        k["project_sems"] = [n.sem(f"s_{v}") for v in ("product", "bias", "sum")]
        k["ones"] = n.sb("ones", [D, D])
        k["eps"] = n.sb("eps", [D, 1])
        k["mask_bias"] = n.sb("mask_bias", [SP_MAX, B, CH])
        x = load("x", [L, B, D])
        k["ident"] = load("ident", [D, D])
        k["row_of"] = load("row_of", [SP_MAX, CH])
        k["lens"] = load("lens", [SP_MAX, B], a["lens"].partition_broadcast(SP_MAX), I32)
        for name in ("decay", "bg", "br", "ln_w", "ln_b", "qnw", "knw"):
            k[name] = load(name, [D, 1])
        for name in ("bq1", "bk2", "bq2", "bv2"):
            k[name] = load(name, [D, 1])
        for name in ("bk1_row", "bv1_row", "bo1_row", "bo2_row"):
            k[name] = row(name, D)
        k["rank_row"] = row("rank_row", E)
        k["head_of"] = load("head_of", [D, HEADS])
        k["same_head"] = load("same_head", [D, D])
        k["head_in_four"] = load("head_in_four", [D, 4])
        k["wkv1"] = load("wkv1", [D, 2 * D])
        for name in ("wq1", "wo1", "wq2", "wk2", "wv2", "wo2T"):
            k[name] = load(name, [D, D])
        k["wq2_thrice"] = load("wq2_thrice", [D, 4, STACK])
        k["bq2_thrice"] = load("bq2_thrice", [STACK, 4])
        k["qnw_row"] = row("qnw_row", HD0)
        k["knw_row"] = row("knw_row", HD0)
        k["bo0_row"] = row("bo0_row", D)
        for name in ("wgT", "wrT", "woT0"):
            k[name] = load(name, [D, D])
        xT = n.sb("xT", [D, T])
        wq0 = load("wq0", [D, HEADS * HD0])
        wk0 = load("wk0", [D, HEADS * HD0])
        wkq = n.sb("wkq", [D, HEADS // 2, D])
        wvo = n.sb("wvo", [D, HEADS, D])

        with Net(nc) as n2:
            x_steps = n2.sb("x_steps", [D, L, B])
            hidden = n2.sb("hidden", [D, L, B])
            wkT = n2.sb("wkT", [D, HEADS // 2, D])
            wvT = n2.sb("wvT", [D, HEADS // 2, D])
            wo = n2.sb("wo0", [D, HEADS // 2, D])
            y = n2.sb("y", [L, B, D])
            pairs += [(x_steps[:, :, :], a["x_steps"]), (wkT[:, :, :], a["wkT0"]), (wvT[:, :, :], a["wvT0"]),
                      (wo[:, :, :], a["wo0"])]
            load_weights(nc, a, k, pairs)
            recurrence(nc, k, x_steps, hidden)
            hidden_to_tokens(nc, k, hidden, y)
            norm_tokens(nc, "n0", k, y, xT, k["ln_w"][:, 0:1], k["ln_b"][:, 0:1])
            project_add(nc, k, "p0", xT, k["woT0"][:, :], k["bo0_row"][:, :], x)
            fold_weights(nc, k, wkT, wvT, wo, wkq, wvo)
        norm_tokens(nc, "n1", k, x, xT)
        if upto > 1:
            cross_attention_0(nc, k, a["ctxT"], a["ctxN"], x, xT, wq0, wk0, wkq, wvo)
        norm_tokens(nc, "n2", k, x, xT, out=out if upto <= 2 else None)
        if upto <= 2:
            return

        share = n.sb("share", [L, B, E])
        with Net(nc) as n2:
            w_up = n2.sb("w_up0", [D, E, 2 * I0])
            b_up = n2.sb("b_up0", [D, E, 4])
            w_down = n2.sb("w_down0", [D, E, 2, D])
            b_down = n2.sb("b_down0", [E, D])
            router = n2.sb("router0", [D, E])
            r_row = n2.sb("router_row0", [L, E])
            load_stage(nc, "l2", [(w_up[:, :, :], a["w_up0"]), (b_up[:, :, :], a["b_up0"]), (w_down[:, :, :, :], a["w_down0"]),
                                  (b_down[:, :], a["b_down0"]), (router[:, :], a["router0"]),
                                  (r_row[:, :], a["router_row0"].partition_broadcast(L))])
            route(nc, "r0", k, x, xT, router[:, :], r_row[:, :], b_down[:, :], share, False)
            gated_experts(nc, k, x, xT, w_up, b_up, w_down, share)
        norm_tokens(nc, "n3", k, x, xT, out=out if upto <= 3 else None)
        if upto <= 3:
            return

        linear_attention(nc, k, x, xT)
        project_add(nc, k, "p4", xT, k["wo1"][:, :], k["bo1_row"][:, :], x)
        norm_tokens(nc, "n4", k, x, xT, out=out if upto <= 4 else None)
        if upto <= 4:
            return

        cross_attention_1(nc, k, a["ctxT"], x, xT)
        norm_tokens(nc, "n5", k, x, xT, out=out if upto <= 5 else None)
        if upto <= 5:
            return

        with Net(nc) as n2:
            w_up = n2.sb("w_up1", [D, E, F1])
            b_up = n2.sb("b_up1", [D, E, 4])
            w_down = n2.sb("w_down1", [D, E, 4, D])
            b_down = n2.sb("b_down1", [E, D])
            router = n2.sb("router1", [D, E])
            r_row = n2.sb("router_row1", [L, E])
            load_stage(nc, "l5", [(w_up[:, :, :], a["w_up1"]), (b_up[:, :, :], a["b_up1"]), (w_down[:, :, :, :], a["w_down1"]),
                                  (b_down[:, :], a["b_down1"]), (router[:, :], a["router1"]),
                                  (r_row[:, :], a["router_row1"].partition_broadcast(L))])
            route(nc, "r1", k, x, xT, router[:, :], r_row[:, :], b_down[:, :], share, True)
            relu_experts(nc, k, x, xT, w_up, b_up, w_down, share)
        norm_tokens(nc, "n6", k, x, out=out)



def lay_out(v):
    import numpy as np

    def pairs_T(w):
        return w.T.reshape(HEADS // 2, D, D).transpose(1, 0, 2)

    ctx = v["ctx_1024"]
    short = ctx[:, :SP_FULL * CH].reshape(B, SP_FULL, CH, D)
    last = ctx[:, SP_FULL * CH:]
    parts = [np.concatenate([short[:, :, c]] + ([last[:, c:c + 1]] if c < S % CH else []), axis=1)
             for c in range(CH)]
    ctxT = np.concatenate(parts, axis=1).transpose(0, 2, 1)
    col = lambda w: w.reshape(-1, 1)
    row = lambda w: w.reshape(-1)
    two = lambda w: np.concatenate([w, w]).reshape(-1, 1)
    p = "L0_attn_"
    o = {
        "x": v["x"].transpose(1, 0, 2), "x_steps": v["x"].transpose(2, 1, 0),
        "ctxT": ctxT, "ctxN": ctx.reshape(B, S * D), "lens": v["_lenS2"],
        "ident": np.eye(D, dtype=np.float32),
        "row_of": (np.arange(SP_MAX)[:, None] * CH + np.arange(CH)[None, :]).astype(np.float32),
        "decay": col(v[p + "decay"]), "bg": col(v[p + "bg"]), "br": col(v[p + "br"]),
        "ln_w": col(v[p + "ln_w"]), "ln_b": col(v[p + "ln_b"]), "bo0_row": row(v[p + "bo"]),
        "wgT": v[p + "Wg"].T, "wrT": v[p + "Wr"].T, "woT0": v[p + "Wo"].T,
    }
    p = "L0_xattn_"
    o |= {
        "qnw": two(v[p + "q_norm_w"]), "knw": two(v[p + "k_norm_w"]),
        "qnw_row": row(v[p + "q_norm_w"]), "knw_row": row(v[p + "k_norm_w"]),
        "wq0": v[p + "Wq"], "wk0": v[p + "Wk"], "wkT0": pairs_T(v[p + "Wk"]), "wvT0": pairs_T(v[p + "Wv"]),
        "wo0": v[p + "Wo"].reshape(HEADS // 2, D, D).transpose(1, 0, 2),
    }
    def hidden(b, chunks):
        return b.reshape(E, chunks, D).transpose(2, 0, 1)

    p = "L0_ffn_"
    o |= {
        "router0": v[p + "router_weight"].T, "router_row0": row(v[p + "router_bias"]),
        "w_up0": v[p + "gate_up_proj"].transpose(1, 0, 2), "b_up0": hidden(v[p + "gate_up_bias"], 4),
        "w_down0": v[p + "down_proj"].reshape(E, 2, D, D).transpose(2, 0, 1, 3), "b_down0": v[p + "down_bias"],
        "rank_row": np.arange(E, 0, -1).astype(np.float32),
    }
    p = "L1_attn_"
    head = np.arange(D) // HD1
    o |= {
        "wq1": v[p + "Wq"], "wkv1": np.concatenate([v[p + "Wk"], v[p + "Wv"]], axis=1), "wo1": v[p + "Wo"],
        "bq1": col(v[p + "bq"]), "bk1_row": row(v[p + "bk"]), "bv1_row": row(v[p + "bv"]),
        "bo1_row": row(v[p + "bo"]),
        "head_of": (head[:, None] == np.arange(HEADS)[None, :]).astype(np.float32),
        "same_head": (head[:, None] == head[None, :]).astype(np.float32),
        "head_in_four": (head[:, None] % 4 == np.arange(4)[None, :]).astype(np.float32),
    }
    p = "L1_xattn_"
    heads = lambda w: w.transpose(1, 0, 2).reshape(D, D)
    o |= {
        "wq2": heads(v[p + "Wq"]), "wk2": heads(v[p + "Wk"]), "wv2": heads(v[p + "Wv"]), "wo2T": v[p + "Wo"].T,
        "bq2": col(v[p + "bq"]), "bk2": col(v[p + "bk"]), "bv2": col(v[p + "bv"]), "bo2_row": row(v[p + "bo"]),
    }
    thrice = lambda w: np.stack([np.tile(w[:, 32 * g:32 * g + 32], 3) for g in range(4)], axis=1)
    o |= {"wq2_thrice": thrice(o["wq2"]), "bq2_thrice": thrice(o["bq2"].T)[0].T}
    p = "L1_ffn_"
    o |= {
        "router1": v[p + "gate_w"], "router_row1": row(v[p + "gate_b"]),
        "w_up1": v[p + "W1"].transpose(1, 0, 2), "b_up1": hidden(v[p + "b1"], 4),
        "w_down1": v[p + "W2"].reshape(E, 4, D, D).transpose(2, 0, 1, 3), "b_down1": v[p + "b2"],
    }
    return {n: np.ascontiguousarray(w) for n, w in o.items()}


def kernel(**inputs):
    import numpy as _np
    import concourse.bacc as _bacc
    from concourse import mybir as _mybir
    from concourse.bass_utils import run_bass_kernel_spmd as _run

    nc = _bacc.Bacc("TRN2", target_bir_lowering=False, num_devices=1)
    arrays, args = {}, {}
    for name, w in lay_out({n: _np.asarray(w) for n, w in inputs.items()}).items():
        arrays[f"in_{name}"] = w
        args[name] = nc.dram_tensor(f"in_{name}", w.shape, _mybir.dt.from_np(w.dtype), kind="ExternalInput").ap()
    out = nc.dram_tensor("out", (L, B, D), _mybir.dt.float32, kind="ExternalOutput").ap()
    decoder(nc, args, out)
    r = _run(nc, [arrays], core_ids=[0])
    return r.results[0]["out"].transpose(1, 0, 2)
```

```python
from contextlib import ExitStack

import concourse.bass as bass
from concourse import mybir

ALU = mybir.AluOpType
ACT = mybir.ActivationFunctionType
F32 = mybir.dt.float32
BF16 = mybir.dt.bfloat16
F32R = mybir.dt.float32r
I32 = mybir.dt.int32
AX_X = mybir.AxisListType.X

B, L, D = 16, 100, 128
T = B * L
S = 1444
CH = 12
SP_FULL = S // CH
SP_MAX = SP_FULL + 1
HEADS = 16
HD0 = 64
HD1 = 8
E = 8
I0 = 256
F1 = 512
STACK = 3 * 4 * HD1
HALF = 8 * L
EPS = 1e-5
MASKED = -30000.0


def rows(c):
    return SP_MAX if c < S % CH else SP_FULL


def off(c):
    return SP_FULL * c + min(c, S % CH)


class Net:

    def __init__(self, nc):
        self.nc = nc
        self.ctx = ExitStack()

    def __enter__(self):
        self.ctx.__enter__()
        return self

    def __exit__(self, *a):
        return self.ctx.__exit__(*a)

    def sb(self, name, shape, dt=F32):
        return self.ctx.enter_context(self.nc.sbuf_tensor(name, shape, dt))

    def ps(self, name, n=1):
        return self.ctx.enter_context(self.nc.psum_tensor(name, [128, n, 512], F32))

    def sem(self, name):
        return self.ctx.enter_context(self.nc.semaphore(name))


def over_heads(col, n):
    p, m = col.shape
    return col.unsqueeze(2).to_broadcast([p, m, n])



def norm_tokens(nc, tag, k, x, xT=None, gain=None, shift=None, out=None):
    with Net(nc) as n:
        stats = n.sb(f"{tag}_stats", [L, B, 6])
        mv = n.sb(f"{tag}_mean_var", [L, B, 2])
        sd = n.sb(f"{tag}_sd", [L, B])
        rstd = n.sb(f"{tag}_rstd", [L, B])
        turned = n.ps(f"{tag}_turned", 4)
        s_stat, s_sd, s_rstd, s_norm, s_turn, s_evac, s_out = k["norm_sems"]
        c = k["norms"]
        k["norms"] = c + 1
        block = n.ctx.enter_context(nc.Block())

        @block.vector
        def _(dve):
            for b in range(B):
                dve.bn_stats(stats[:, b, :], x[:, b, :]).then_inc(s_stat, 1)
            for b in range(B):
                dve.wait_ge(s_stat, 2 * B * c + b + 1)
                dve.bn_aggr(mv[:, b, :], stats[:, b, :]).then_inc(s_stat, 1)
            dve.wait_ge(s_sd, c + 1)
            dve.reciprocal(rstd[:, :], sd[:, :]).then_inc(s_rstd, 1)
            dve.wait_ge(s_rstd, c + 1)
            for b in range(B):
                dve.tensor_scalar(x[:, b, :], x[:, b, :], mv[:, b, 0:1], rstd[:, b:b + 1],
                                  ALU.subtract, ALU.mult).then_inc(s_norm, 1)

        @block.scalar
        def _(act):
            act.wait_ge(s_stat, 2 * B * (c + 1))
            act.activation(sd[:, :], mv[:, :, 1], ACT.Sqrt, bias=k["eps"][0:L, 0:1]).then_inc(s_sd, 1)
            if xT is not None:
                for g in range(4):
                    act.wait_ge(s_turn, 4 * c + g + 1)
                    src = turned[:, g, 0:4 * L]
                    dst = xT[:, 4 * g * L:4 * (g + 1) * L]
                    if gain is None:
                        act.activation(dst, src, ACT.Copy).then_inc(s_evac, 1)
                    else:
                        act.activation(dst, src, ACT.Identity, bias=shift, scale=gain).then_inc(s_evac, 1)

        if xT is not None:
            @block.tensor
            def _(pe):
                for b in range(B):
                    pe.wait_ge(s_norm, B * c + b + 1)
                    t = pe.transpose(turned[:, b // 4, (b % 4) * L:(b % 4 + 1) * L], x[:, b, :],
                                     k["ident"][0:L, 0:L])
                    if b % 4 == 3:
                        t.then_inc(s_turn, 1)

        if out is not None:
            @block.sync
            def _(sp):
                sp.wait_ge(s_norm, B * (c + 1))
                sp.dma_start(out, x[:, :, :]).then_inc(s_out, 16)
                sp.wait_ge(s_out, 16)



def load_first(nc, k, pairs):
    with Net(nc) as n:
        s_needed = n.sem("s_needed")
        s_const = n.sem("s_const")
        block = n.ctx.enter_context(nc.Block())

        @block.sync
        def _(sp):
            for dst, src in pairs[0::2]:
                sp.dma_start(dst, src).then_inc(s_needed, 16)
            sp.wait_ge(s_needed, 16 * len(pairs))

        @block.scalar
        def _(act):
            for dst, src in pairs[1::2]:
                act.dma_start(dst, src).then_inc(s_needed, 16)

        @block.vector
        def _(dve):
            dve.memset(k["eps"][:, :], EPS).then_inc(s_const, 1)
            dve.memset(k["zero"][:, :], 0.0).then_inc(s_const, 1)
            dve.memset(k["ones"][:, :], 1.0).then_inc(s_const, 1)



def recurrence(nc, k, x_steps, hidden, pairs):
    with Net(nc) as n:
        forget = n.sb("forget", [D, 1])
        negkeep = n.sb("negkeep", [D, 1])
        z = n.sb("z", [D, L, B])
        c = n.sb("c", [D, L, B])
        w = n.sb("w", [D, 2, B])
        m = n.sb("m", [D, 2, B])
        zp = n.ps("zp", 4)
        pred = n.ps("pred", 2)
        s_z = n.sem("s_z")
        s_gate = n.sem("s_gate")
        s_pre = n.sem("s_pre")
        s_w = n.sem("s_w")
        s_m = n.sem("s_m")
        s_h = n.sem("s_h")
        s_pred = n.sem("s_pred")
        s_late = n.sem("s_late")
        s_load = n.sem("s_load")
        TG = L // 4
        EARLY = (TG - 1) // 2
        xs = x_steps

        def group_of(t, g):
            return t[:, g * TG:(g + 1) * TG, :].rearrange("p t b -> p (t b)")

        block = n.ctx.enter_context(nc.Block())

        @block.tensor
        def _(pe):
            for g in range(4):
                pe.matmul(zp[:, g, 0:TG * B], k["wgT"][:, :], xs[:, g * TG:(g + 1) * TG, :],
                          start=True, stop=True).then_inc(s_z, 1)

            def predict(t, p):
                pe.wait_ge(s_w, t)
                pe.matmul(pred[:, p, 0:B], k["wrT"][:, :], w[:, 1 - p, :], start=True, stop=False)
                pe.wait_ge(s_m, t)
                pe.matmul(pred[:, p, 0:B], k["wrT"][:, :], m[:, 1 - p, :], start=False,
                          stop=True).then_inc(s_pred, 1)

            with pe.Fori(0, (L - 2) // 2) as i:
                predict(2 * i + 1, 1)
                predict(2 * i + 2, 0)
            predict(L - 1, 1)

        @block.sync
        def _(sp):
            for dst, src in pairs:
                sp.dma_start(dst, src).then_inc(s_load, 16)
            sp.wait_ge(s_load, 16 * len(pairs))

        @block.gpsimd
        def _(pool):
            pool.wait_ge(s_pre, 2)
            for g in range(1, 4):
                pool.wait_ge(s_gate, g + 2)
                zg, cg = group_of(z, g), group_of(c, g)
                pool.tensor_scalar(zg, zg, negkeep[:, 0:1], None, ALU.mult).then_inc(s_late, 1)
                pool.wait_ge(s_late, 2 * g - 1)
                pool.tensor_tensor(cg, zg, cg, ALU.mult).then_inc(s_late, 1)

        @block.scalar
        def _(act):
            act.activation(forget[:, :], k["decay"][:, :], ACT.Sigmoid).then_inc(s_gate, 1)
            for g in range(4):
                act.wait_ge(s_z, g + 1)
                act.activation(z[:, g * TG:(g + 1) * TG, :].rearrange("p t b -> p (t b)"),
                               zp[:, g, 0:TG * B], ACT.Sigmoid, bias=k["bg"][:, 0:1]).then_inc(s_gate, 1)

        @block.vector
        def _(dve):
            dve.tensor_scalar(c[:, :, :], xs[:, :, :], -1.0, k["br"][:, 0:1], ALU.mult, ALU.add).then_inc(s_pre, 1)
            dve.wait_ge(s_gate, 1)
            dve.tensor_scalar(negkeep[:, :], forget[:, :], -1.0, None, ALU.add).then_inc(s_pre, 1)
            dve.wait_ge(s_gate, 2)
            dve.wait_ge(s_pre, 2)
            z0, c0 = group_of(z, 0), group_of(c, 0)
            dve.tensor_scalar(z0, z0, negkeep[:, 0:1], None, ALU.mult).then_inc(s_pre, 1)
            dve.wait_ge(s_pre, 3)
            dve.tensor_tensor(c0, z0, c0, ALU.mult).then_inc(s_pre, 1)
            dve.memset(m[:, :, :], 0.0).then_inc(s_m, 1)
            dve.wait_ge(s_pre, 4)
            dve.tensor_copy(w[:, 0, :], c[:, 0, :]).then_inc(s_w, 1)
            dve.tensor_copy(hidden[:, 0, :], c[:, 0, :]).then_inc(s_h, 1)

            def step(t, p):
                dve.wait_ge(s_h, t)
                dve.scalar_tensor_tensor(out=w[:, p, :], in0=hidden[:, bass.ds(t - 1, 1), :].rearrange("p t b -> p (t b)"),
                                         scalar=forget[:, 0:1],
                                         in1=c[:, bass.ds(t, 1), :].rearrange("p t b -> p (t b)"),
                                         op0=ALU.mult, op1=ALU.add).then_inc(s_w, 1)
                dve.wait_ge(s_pred, t)
                dve.tensor_tensor(m[:, p, :], pred[:, p, 0:B],
                                  z[:, bass.ds(t, 1), :].rearrange("p t b -> p (t b)"), ALU.mult).then_inc(s_m, 1)
                dve.wait_ge(s_m, t + 1)
                dve.wait_ge(s_w, t + 1)
                dve.tensor_tensor(hidden[:, bass.ds(t, 1), :].rearrange("p t b -> p (t b)"), w[:, p, :], m[:, p, :],
                                  ALU.add).then_inc(s_h, 1)

            with dve.Fori(0, EARLY) as i:
                step(2 * i + 1, 1)
                step(2 * i + 2, 0)
            dve.wait_ge(s_late, 6)
            with dve.Fori(EARLY, (L - 2) // 2) as i:
                step(2 * i + 1, 1)
                step(2 * i + 2, 0)
            step(L - 1, 1)


def hidden_to_tokens(nc, k, hidden, y):
    with Net(nc) as n:
        turned = n.ps("hid_turned", 4)
        s_turn = n.sem("hid_s_turned")
        s_evac = n.sem("hid_s_evac")
        block = n.ctx.enter_context(nc.Block())

        @block.tensor
        def _(pe):
            for b in range(B):
                t = pe.transpose(turned[0:L, b // 4, (b % 4) * D:(b % 4 + 1) * D], hidden[:, :, b],
                                 k["ident"][:, :])
                if b % 4 == 3:
                    t.then_inc(s_turn, 1)

        @block.vector
        def _(dve):
            for g in range(4):
                dve.wait_ge(s_turn, g + 1)
                dve.tensor_copy(y[:, 4 * g:4 * g + 4, :].rearrange("l b d -> l (b d)"),
                                turned[0:L, g, :]).then_inc(s_evac, 1)


def project_add(nc, k, tag, inT, weight, bias_row, x):
    with Net(nc) as n:
        prod = n.ps(f"{tag}_prod", 4)
        s_prod, s_bias, s_add = k["project_sems"]
        c = k["projects"]
        k["projects"] = c + 1
        block = n.ctx.enter_context(nc.Block())

        @block.tensor
        def _(pe):
            for b in range(B):
                t = pe.matmul(prod[0:L, b // 4, (b % 4) * D:(b % 4 + 1) * D], inT[:, b * L:(b + 1) * L],
                              weight, start=True, stop=True)
                if b % 4 == 3:
                    t.then_inc(s_prod, 1)

        @block.vector
        def _(dve):
            dve.tensor_tensor(x[:, :, :], x[:, :, :], bias_row.unsqueeze(1).to_broadcast([L, B, D]),
                              ALU.add).then_inc(s_bias, 1)
            dve.wait_ge(s_bias, c + 1)
            for g in range(4):
                dve.wait_ge(s_prod, 4 * c + g + 1)
                xg = x[:, 4 * g:4 * g + 4, :].rearrange("l b d -> l (b d)")
                dve.tensor_tensor(xg, xg, prod[0:L, g, :], ALU.add).then_inc(s_add, 1)



def fold_weights(nc, k, wkT, wvT, wo, wkq, wvo, parts):
    with Net(nc) as n:
        norm_w = n.sb("norm_w", [D, 1])
        norm_row = n.sb("norm_row", [SP_MAX, HD0])
        cap = n.sb("cap", [SP_MAX, 1])
        len_f = n.sb("len_f", [SP_MAX, B])
        prod = n.ps("wvo_prod", 4)
        s_nw = n.sem("s_nw")
        s_high = n.sem("fold_s_high")
        s_low = n.sem("fold_s_low")
        s_cap = n.sem("s_cap")
        s_mask = n.sem("s_mask")
        s_wvo = n.sem("s_wvo")
        s_evac = n.sem("s_wvo_evac")
        s_wkq = n.sem("s_wkq")
        block = n.ctx.enter_context(nc.Block())

        @block.tensor
        def _(pe):
            for r in range(4):
                for h in range(4 * r, 4 * r + 4):
                    j, bank = h % 2, h % 2 + 2 * (r % 2)
                    if r >= 2 and h < 4 * r + 2:
                        pe.wait_ge(s_evac, 2 * (r - 2) + 1 + j)
                    t = pe.matmul(prod[:, bank, (h // 2 % 2) * D:(h // 2 % 2 + 1) * D],
                                  wvT[64 * j:64 * j + 64, h // 2, :], wo[64 * j:64 * j + 64, h // 2, :],
                                  start=True, stop=True)
                t.then_inc(s_wvo, 1)

        @block.scalar
        def _(act):
            for whole, high, low in parts:
                act.activation(high, whole, ACT.Copy).then_inc(s_high, 1)

        @block.gpsimd
        def _(pool):
            for i, (whole, high, low) in enumerate(parts):
                pool.wait_ge(s_high, i + 1)
                pool.tensor_tensor(low, whole, high.bitcast(F32), ALU.subtract).then_inc(s_low, 1)

        @block.vector
        def _(dve):
            dve.tensor_tensor(norm_w[:, :], k["qnw"][:, :], k["knw"][:, :], ALU.mult).then_inc(s_nw, 1)
            dve.wait_ge(s_nw, 1)
            dve.tensor_scalar(wkq[:, :, :], wkT[:, :, :], norm_w[:, 0:1], HD0 ** -0.5, ALU.mult,
                              ALU.mult).then_inc(s_wkq, 1)
            dve.tensor_tensor(norm_row[:, :], k["qnw_row"][0:SP_MAX, :], k["knw_row"][0:SP_MAX, :],
                              ALU.mult).then_inc(s_cap, 1)
            dve.wait_ge(s_cap, 1)
            dve.tensor_reduce(cap[:, :], norm_row[:, :], AX_X, ALU.max, apply_absolute_value=True).then_inc(s_cap, 1)
            dve.tensor_copy(len_f[:, :], k["lens"][:, :]).then_inc(s_cap, 1)
            dve.wait_ge(s_cap, 3)
            dve.tensor_scalar(cap[:, :], cap[:, :], HD0 ** 0.5, None, ALU.mult).then_inc(s_cap, 1)
            mask = k["mask_bias"]
            dve.tensor_tensor(mask[:, :, :], k["row_of"][:, :].unsqueeze(1).to_broadcast([SP_MAX, B, CH]),
                              over_heads(len_f[:, :], CH), ALU.is_ge).then_inc(s_mask, 1)
            dve.wait_ge(s_mask, 1)
            dve.wait_ge(s_cap, 4)
            dve.tensor_scalar(mask[:, :, :], mask[:, :, :], MASKED, cap[:, 0:1], ALU.mult,
                              ALU.subtract).then_inc(s_mask, 1)
            for r in range(4):
                dve.wait_ge(s_wvo, r + 1)
                for j in range(2):
                    dve.tensor_copy(wvo[:, 4 * r + j:4 * r + j + 3:2, :],
                                    prod[:, j + 2 * (r % 2), 0:2 * D].rearrange("p (a d) -> p a d", a=2))\
                       .then_inc(s_evac, 1)


def cross_attention_0(nc, k, ctxT_d, ctxN_d, x, xT, wq, wkq, wvo, ctx_in, ctx_high, ctx_low, wk_high, wk_low, ahead):
    NS = 2 * CH
    with Net(nc) as n:
        ctx_high = [ctx_high, n.sb("ctx_high1", [D, S], F32R)]
        ctx_low = [ctx_low, n.sb("ctx_low1", [D, S], F32R)]
        ctxN = [n.sb(f"ctxN{u}", [SP_MAX, CH, D]) for u in range(2)]
        sq = n.sb("sq", [SP_MAX, 2, 512])
        kss = n.sb("kss", [SP_MAX, CH, HEADS])
        ksd = n.sb("ksd", [SP_MAX, CH, HEADS])
        krs = [n.sb(f"krs{u}", [SP_MAX, CH, HEADS]) for u in range(2)]
        bias = [n.sb(f"bias{u}", [SP_MAX, CH]) for u in range(2)]
        q_in = n.sb("q_in", [D, L])
        qs = n.sb("qs", [L, HEADS, HD0])
        qsq = n.sb("qsq", [L, HEADS, HD0])
        qss = n.sb("qss", [L, HEADS])
        qsd = n.sb("qsd", [L, HEADS])
        qrs = n.sb("qrs", [L, HEADS])
        qn = n.sb("qn", [L, HEADS, HD0])
        qblk = n.sb("qblk", [D, HEADS // 2, 2, L])
        qp_high = [n.sb(f"qp_high{u}", [D, HEADS * L], F32R) for u in range(2)]
        qp_low = [n.sb(f"qp_low{u}", [D, HEADS * L], F32R) for u in range(2)]
        p = [n.sb(f"p{j}", [SP_MAX, HALF]) for j in range(4)]
        acc = [n.sb(f"acc{j}", [SP_MAX, HALF]) for j in range(2)]
        oraw = n.sb("oraw", [D, HALF])
        rden = n.sb("rden", [D, HALF])
        onorm = n.sb("onorm", [D, HALF])
        ring = n.ps("ring", 4)
        pvb = n.ps("pvb", 2)
        knb = n.ps("knb", 1)
        qb = n.ps("qb", 1)

        s_ctx = [n.sem(f"s_ctx{u}") for u in range(2)]
        s_ahead = n.sem("s_ahead")
        s_ctx_in = n.sem("s_ctx_in")
        s_ctx_high = n.sem("s_ctx_high")
        s_ctx_low = n.sem("s_ctx_low")
        s_qp_high = n.sem("s_qp_high")
        s_qin = n.sem("s_qin")
        s_kn = n.sem("s_kn")
        s_sq = n.sem("s_sq")
        s_ss = n.sem("s_ss")
        s_ksd = n.sem("s_ksd")
        s_krs = n.sem("s_krs")
        s_qunit = n.sem("s_qunit")
        s_qfree = n.sem("s_qfree")
        s_qsq = n.sem("s_qsq")
        s_qss = n.sem("s_qss")
        s_qsd = n.sem("s_qsd")
        s_qrs = n.sem("s_qrs")
        s_qn = n.sem("s_qn")
        s_blk0 = n.sem("s_blk0")
        s_bias = n.sem("s_rowbias")
        s_item = n.sem("s_item")
        s_free = n.sem("s_free")
        s_exp = n.sem("s_exp")
        s_acc = n.sem("s_acc")
        s_pv = n.sem("s_pv")
        s_oraw = n.sem("s_oraw")
        s_rden = n.sem("s_rden")
        s_on = n.sem("s_on")

        ITEMS = NS + 2
        TAIL_STEP, DEN_STEP = 3, 15
        TAIL_ITEM, DEN_ITEM = TAIL_STEP, DEN_STEP + 1
        item_of = [s + (s >= TAIL_STEP) + (s >= DEN_STEP) for s in range(NS)]
        INVERT_STEPS = (DEN_STEP, DEN_STEP + 3, DEN_STEP + 4, DEN_STEP + 5)
        LAG = 2
        UNITS = 10
        FIRST_NORM = 3
        norms_at = [[] for s in range(NS)]
        for i in range(NS):
            norms_at[FIRST_NORM + (3 * i + 1) // 4].append(i)

        def unit(b, i):
            if isinstance(b, int) and b >= B - 1 and i > 0 or isinstance(b, int) and b >= B:
                return UNITS * B + (1 if b == B - 1 else 2)  - 1
            return UNITS * (b + 1) + i - 1

        def twice(b, i):
            return 3 if isinstance(b, int) and b == -1 and i == 8 else 1

        before = [("q", 1), ("q", 2)] + [("k", s) for s in range(8)] + [("t", 3), ("t", 4)]
        for s in range(8, NS):
            before.append(("k", s))
            if s in (10, 12, 14, 16):
                before.append(("a", 5 + (s - 10) // 2))

        def norm_bank(j, s):
            return pvb if isinstance(j, int) and j == 0 and s % 2 else knb

        block = n.ctx.enter_context(nc.Block())

        @block.sync
        def _(sp):
            def load_turned(b):
                sp.dma_start(ctx_in[:, :], ctxT_d[bass.ds(b, 1), :, :].rearrange("b d s -> (b d) s"))\
                  .then_inc(s_ctx_in, 16)

            def load(b, u):
                sp.dma_start(ctxN[u][0:SP_FULL, :, :].rearrange("p c d -> p (c d)"),
                             ctxN_d[bass.ds(b, 1), 0:SP_FULL * CH * D].rearrange("b (p n) -> (b p) n", p=SP_FULL))\
                  .then_inc(s_ctx[u], 16)
                sp.dma_start(ctxN[u][SP_FULL:SP_MAX, 0:S % CH, :].rearrange("p c d -> p (c d)"),
                             ctxN_d[bass.ds(b, 1), SP_FULL * CH * D:S * D]).then_inc(s_ctx[u], 16)

            load_turned(1)
            load(0, 0)
            load(1, 1)
            for dst, src in ahead:
                sp.dma_start(dst, src).then_inc(s_ahead, 16)
            with sp.Fori(0, (B - 2) // 2) as i:
                for u in range(2):
                    sp.wait_ge(s_ctx_low, 2 * i + u + 1)
                    load_turned(2 * i + u + 2)
                    sp.wait_ge(s_pv, NS * (2 * i + u + 1))
                    load(2 * i + u + 2, u)
            sp.wait_ge(s_ahead, 16 * len(ahead))

        def batches(eng, batch):
            batch(0, 0, 1, tail=False)
            with eng.Fori(0, (B - 2) // 2) as i:
                batch(2 * i + 1, 1, i + 2)
                batch(2 * i + 2, 0, i + 2)
            batch(B - 1, 1, 0, prep=False)

        @block.tensor
        def _(pe):
            def key_norm_unit(j, u, s):
                c = s // 2
                if not (isinstance(j, int) and j == 0):
                    pe.wait_ge(s_sq, NS * j + s)
                elif s >= 2:
                    pe.wait_ge(s_sq, s - 1)
                at, heads = slice(off(c), off(c) + rows(c)), slice(512 * (s % 2), 512 * (s % 2) + 512)
                dst = norm_bank(j, s)[0:rows(c), 0, :]
                pe.matmul(dst, ctx_high[u][:, at], wk_high[:, heads], start=True, stop=False)
                pe.matmul(dst, ctx_high[u][:, at], wk_low[:, heads], start=False, stop=False)
                pe.matmul(dst, ctx_low[u][:, at], wk_high[:, heads], start=False, stop=True).then_inc(s_kn, 1)

            def qbank(b, i):
                if not (isinstance(b, int) and b == -1 and i == 1):
                    pe.wait_ge(s_qfree, unit(b, i))

            def query_unit(b, i):
                qbank(b, i)
                pe.wait_ge(s_qin, b + 2)
                pe.matmul(qb[0:L, 0, :], q_in[:, :], wq[:, 512 * (i - 1):512 * i],
                          start=True, stop=True).then_inc(s_qunit, 1)

            def turn_unit(b, i):
                qbank(b, i)
                pe.wait_ge(s_qn, b + 2)
                for a in range(4):
                    h = 8 * (i - 3) + 2 * a
                    t = pe.transpose(qb[:, 0, a * L:(a + 1) * L], qn[:, h:h + 2, :].rearrange("l h e -> l (h e)"),
                                     k["ident"][0:L, 0:L])
                t.then_inc(s_qunit, 1)

            def absorb_unit(b, i):
                qbank(b, i)
                for a in range(2):
                    g = 2 * (i - 5) + a
                    t = pe.matmul(qb[:, 0, a * 2 * L:(a + 1) * 2 * L], wkq[:, g, :],
                                  qblk[:, g, :, :].rearrange("p a l -> p (a l)"), start=True, stop=True)
                t.then_inc(s_qunit, twice(b, i))

            def out_unit(b, i, half, done):
                qbank(b, i)
                pe.wait_ge(s_on, done)
                for h in range(8):
                    t = pe.matmul(qb[0:L, 0, 0:D], onorm[:, h * L:(h + 1) * L], wvo[:, 8 * half + h, :],
                                  start=(h == 0), stop=(h == 7))
                t.then_inc(s_qunit, 1)

            def slot(b, i):
                if not (isinstance(b, int) and b == 0 and i < 2):
                    pe.wait_ge(s_free, ITEMS * b + i - 1)
                return 2 * (i % 2)

            def den_item(b, i, half, done):
                r = slot(b, i)
                pe.wait_ge(s_acc, done)
                for a in range(2):
                    t = pe.matmul(ring[:, r + a, 0:4 * L], k["ones"][0:SP_MAX, :],
                                  acc[half][:, a * 4 * L:(a + 1) * 4 * L], start=True, stop=True)
                t.then_inc(s_item, 1)

            def score(b, u, s):
                half, c = s // CH, s % CH
                if c == 0:
                    pe.wait_ge(s_qfree, unit(b - 1, 9 if half else 7))
                r = slot(b, item_of[s])
                for a in range(2):
                    at = slice(off(c), off(c) + rows(c))
                    heads = slice(half * HALF + a * 4 * L, half * HALF + (a + 1) * 4 * L)
                    dst = ring[0:rows(c), r + a, 0:4 * L]
                    pe.matmul(dst, ctx_high[u][:, at], qp_high[u][:, heads], start=True, stop=False)
                    pe.matmul(dst, ctx_high[u][:, at], qp_low[u][:, heads], start=False, stop=False)
                    t = pe.matmul(dst, ctx_low[u][:, at], qp_high[u][:, heads], start=False, stop=True)
                t.then_inc(s_item, 2 if isinstance(b, int) and b == 0 and s == TAIL_STEP - 1 else 1)

            def weigh(b, u, s):
                c = s % CH
                if c == 0 and not (isinstance(b, int) and b == 0 and s == 0):
                    pe.wait_ge(s_oraw, 2 * b + s // CH)
                pe.wait_ge(s_exp, NS * b + s + 1)
                for a in range(2):
                    t = pe.matmul(pvb[:, a, 0:4 * L], ctxN[u][0:rows(c), c, :],
                                  p[s % 4][0:rows(c), a * 4 * L:(a + 1) * 4 * L],
                                  start=(c == 0), stop=(c == CH - 1))
                t.then_inc(s_pv, 1)

            def batch(b, u, nth, prep=True, tail=True):
                for s in range(NS):
                    if s == TAIL_STEP and tail:
                        den_item(b, TAIL_ITEM, 1, NS * b)
                    if s == DEN_STEP:
                        den_item(b, DEN_ITEM, 0, NS * b + CH)
                    score(b, u, s)
                    if s == FIRST_NORM and prep:
                        pe.wait_ge(s_ctx_low, b + 1)
                        pe.wait_ge(s_ctx[1 - u], 32 * nth)
                    for i in norms_at[s][:1] if prep else []:
                        key_norm_unit(b + 1, 1 - u, i)
                    if s >= LAG:
                        weigh(b, u, s - LAG)
                    elif tail:
                        weigh(b - 1, 1 - u, NS - LAG + s)
                    for i in norms_at[s][1:] if prep else []:
                        key_norm_unit(b + 1, 1 - u, i)
                    if s == 8 and tail:
                        out_unit(b, 0, 1, 2 * b)
                    if prep and s in (9, 10):
                        query_unit(b, s - 8)
                    if prep and s in (16, 17):
                        turn_unit(b, s - 13)
                    if prep and s in (18, 19, 20, 21):
                        absorb_unit(b, s - 13)
                    if s == 22:
                        out_unit(b, 9, 0, 2 * b + 1)
            for what, i in before:
                if what == "k":
                    key_norm_unit(0, 0, i)
                else:
                    {"q": query_unit, "t": turn_unit, "a": absorb_unit}[what](-1, i)
            pe.wait_ge(s_ctx[0], 32)
            batches(pe, batch)
            for s in range(NS - LAG, NS):
                weigh(B - 1, 1, s)
            den_item(B, 0, 1, NS * B)
            out_unit(B, 0, 1, 2 * B)

        @block.scalar
        def _(act):
            def keep_high(j, u):
                act.wait_ge(s_ctx_in, 16 * j)
                if not (isinstance(j, int) and j < 2):
                    act.wait_ge(s_free, ITEMS * (j - 1))
                act.activation(ctx_high[u][:, :], ctx_in[:, :], ACT.Copy).then_inc(s_ctx_high, 1)

            def keep_high_absorbed(b, u, i):
                act.wait_ge(s_qunit, unit(b, i) + 1)
                act.activation(qp_high[u][:, 4 * L * (i - 5):4 * L * (i - 4)], qb[:, 0, 0:4 * L],
                               ACT.Copy).then_inc(s_qp_high, 1)

            def square(j, s):
                r = rows(s // 2)
                act.wait_ge(s_kn, NS * j + s + 1)
                if not (isinstance(j, int) and j == 0 and s < 2):
                    act.wait_ge(s_ss, NS * j + s - 1)
                act.activation(sq[0:r, s % 2, :], norm_bank(j, s)[0:r, 0, :], ACT.Square).then_inc(s_sq, 1)

            def query_root(j):
                act.wait_ge(s_qss, j + 1)
                act.activation(qsd[:, :], qss[:, :], ACT.Sqrt, bias=k["eps"][0:L, 0:1],
                               scale=1.0 / HD0).then_inc(s_qsd, 1)

            def key_root(j):
                act.wait_ge(s_ss, NS * (j + 1))
                act.activation(ksd[:, :, :].rearrange("p c h -> p (c h)"), kss[:, :, :].rearrange("p c h -> p (c h)"),
                               ACT.Sqrt, bias=k["eps"][0:SP_MAX, 0:1], scale=1.0 / HD0).then_inc(s_ksd, 1)

            def batch(b, u, nth, prep=True, tail=True):
                for s in range(NS):
                    c = s % CH
                    r = rows(c)
                    if s == 0:
                        act.wait_ge(s_bias, b + 1)
                    for i in norms_at[s][:1] if prep else []:
                        square(b + 1, i)
                    act.wait_ge(s_free, ITEMS * b + item_of[s] + 1)
                    act.activation(p[s % 4][0:r, :], p[s % 4][0:r, :], ACT.Exp,
                                   bias=bias[u][0:r, c:c + 1]).then_inc(s_exp, 1)
                    for i in norms_at[s][1:] if prep else []:
                        square(b + 1, i)
                    if prep and s == 0:
                        keep_high(b + 1, 1 - u)
                    if prep and s == 13:
                        query_root(b + 1)
                    if prep and s in (18, 19, 20, 21):
                        keep_high_absorbed(b, 1 - u, s - 13)
                    if prep and s == 21:
                        key_root(b + 1)

            for what, i in before:
                if what == "k":
                    square(0, i)
                if what == "a":
                    keep_high_absorbed(-1, 0, i)
                if (what, i) == ("k", 3):
                    query_root(0)
            key_root(0)
            batches(act, batch)

        @block.gpsimd
        def _(pool):
            def keep_low(j, u):
                pool.wait_ge(s_ctx_high, j)
                pool.tensor_tensor(ctx_low[u][:, :], ctx_in[:, :], ctx_high[u][:, :].bitcast(F32),
                                   ALU.subtract).then_inc(s_ctx_low, 1)

            def take_tokens(j):
                if not (isinstance(j, int) and j == 0):
                    pool.wait_ge(s_qunit, unit(j - 2, 3))
                pool.tensor_copy(q_in[:, :], xT[:, bass.ds(j * L, L)]).then_inc(s_qin, 1)

            def square_queries(j):
                pool.wait_ge(s_qfree, unit(j - 1, 3))
                pool.tensor_tensor(qsq[:, :, :], qs[:, :, :], qs[:, :, :], ALU.mult).then_inc(s_qsq, 1)

            def batch(b, u, nth, prep=True, tail=True):
                for s in range(NS):
                    half, c = s // CH, s % CH
                    r = rows(c)
                    if prep and s == 0:
                        keep_low(b + 1, 1 - u)
                    if prep and s == 1:
                        take_tokens(b + 1)
                    if prep and s == 11:
                        square_queries(b + 1)
                    if c == 0:
                        continue
                    if c == 1:
                        if not (isinstance(b, int) and b == 0):
                            pool.wait_ge(s_item, ITEMS * b + TAIL_ITEM + 1 if half else ITEMS * (b - 1) + DEN_ITEM + 1)
                        pool.wait_ge(s_exp, NS * b + s + 1)
                        pool.tensor_tensor(acc[half][0:r, :], p[(s - 1) % 4][0:r, :], p[s % 4][0:r, :],
                                           ALU.add).then_inc(s_acc, 2)
                    else:
                        pool.wait_ge(s_exp, NS * b + s + 1)
                        pool.wait_ge(s_acc, NS * b + s)
                        pool.tensor_tensor(acc[half][0:r, :], acc[half][0:r, :], p[s % 4][0:r, :],
                                           ALU.add).then_inc(s_acc, 1)

            take_tokens(0)
            square_queries(0)
            batches(pool, batch)

        @block.vector
        def _(dve):
            def sum_squares(j, s):
                r = rows(s // 2)
                dve.wait_ge(s_sq, NS * j + s + 1)
                dve.tensor_reduce(kss[0:r, s // 2, 8 * (s % 2):8 * (s % 2) + 8],
                                  sq[0:r, s % 2, :].rearrange("p (h e) -> p h e", h=8), AX_X,
                                  ALU.add).then_inc(s_ss, 1)

            def take_queries(b, i):
                dve.wait_ge(s_qunit, unit(b, i) + 1)
                dve.tensor_copy(qs[:, 8 * (i - 1):8 * i, :].rearrange("l h e -> l (h e)"),
                                qb[0:L, 0, :]).then_inc(s_qfree, 1)

            def sum_query_squares(j):
                dve.wait_ge(s_qsq, j + 1)
                dve.tensor_reduce(qss[:, :], qsq[:, :, :], AX_X, ALU.add).then_inc(s_qss, 1)

            def norm_queries(j):
                dve.wait_ge(s_qsd, j + 1)
                dve.reciprocal(qrs[:, :], qsd[:, :]).then_inc(s_qrs, 1)
                dve.wait_ge(s_qrs, j + 1)
                dve.tensor_tensor(qn[:, :, :], qs[:, :, :], over_heads(qrs[:, :], HD0), ALU.mult).then_inc(s_qn, 1)

            def take_turned(b, i):
                dve.wait_ge(s_qunit, unit(b, i) + 1)
                src = qb[:, 0, 0:4 * L].rearrange("p (a l) -> p a l", a=4)
                g = 4 * (i - 3)
                dve.tensor_copy(qblk[0:HD0, g:g + 4, 0, :], src[0:HD0])
                dve.tensor_copy(qblk[HD0:D, g:g + 4, 1, :], src[HD0:D]).then_inc(s_qfree, 1)

            def take_absorbed(b, u, i):
                heads = slice(4 * L * (i - 5), 4 * L * (i - 4))
                dve.wait_ge(s_qp_high, 4 * (b + 1) + i - 4)
                dve.tensor_tensor(qp_low[u][:, heads], qb[:, 0, 0:4 * L], qp_high[u][:, heads].bitcast(F32),
                                  ALU.subtract).then_inc(s_qfree, twice(b, i))

            def add_out(b, i, to):
                dve.wait_ge(s_qunit, unit(b, i) + 1)
                dve.wait_ge(s_qfree, unit(b, i))
                xb = x[:, bass.ds(to, 1), :].rearrange("l b d -> l (b d)")
                dve.tensor_tensor(xb, xb, qb[0:L, 0, 0:D], ALU.add).then_inc(s_qfree, 1)

            def key_roots(j, u):
                dve.wait_ge(s_ksd, j + 1)
                dve.reciprocal(krs[u][:, :, :], ksd[:, :, :]).then_inc(s_krs, 1)

            def scale_scores(b, u, s):
                half, c = s // CH, s % CH
                r, i = rows(c), item_of[s]
                dve.wait_ge(s_item, ITEMS * b + i + 1)
                if s == 0:
                    dve.wait_ge(s_krs, b + 1)
                if not (isinstance(b, int) and b == 0 and s < 4):
                    dve.wait_ge(s_pv, NS * b + s - 3)
                    dve.wait_ge(s_acc, NS * b + s - 3)
                scale = krs[u][0:r, c, 8 * half:8 * half + 8].rearrange("p (a h) -> p a h", a=2)
                dve.tensor_tensor(p[s % 4][0:r, :].rearrange("p (a h l) -> p a h l", a=2, h=4),
                                  ring[0:r, 2 * (i % 2):2 * (i % 2) + 2, 0:4 * L].rearrange("p a (h l) -> p a h l", h=4),
                                  scale.unsqueeze(3).to_broadcast([r, 2, 4, L]), ALU.mult)\
                   .then_inc(s_free, 2 if isinstance(b, int) and b == 0 and s == TAIL_STEP - 1 else 1)

            def take_bias(j, u):
                if not (isinstance(j, int) and j < 2):
                    dve.wait_ge(s_exp, NS * (j - 1))
                dve.tensor_scalar(bias[u][:, :], k["mask_bias"][:, bass.ds(j, 1), :].rearrange("p b c -> p (b c)"),
                                  0.0, None, ALU.add).then_inc(s_bias, 1)

            def take_sums(b, half):
                dve.wait_ge(s_pv, NS * b + CH * (half + 1))
                dve.tensor_copy(oraw[:, :].rearrange("p (a n) -> p a n", a=2), pvb[:, :, 0:4 * L]).then_inc(s_oraw, 1)

            def take_softmax_sums(b, i):
                dve.wait_ge(s_item, ITEMS * b + i + 1)
                r = 2 * (i % 2)
                dve.tensor_copy(rden[:, :].rearrange("p (a n) -> p a n", a=2), ring[:, r:r + 2, 0:4 * L])\
                   .then_inc(s_free, 1)

            def invert_sums(b, i, j, done):
                dve.wait_ge(s_free, ITEMS * b + i + 1)
                dve.reciprocal(rden[:, 2 * j * L:2 * (j + 1) * L], rden[:, 2 * j * L:2 * (j + 1) * L])\
                   .then_inc(s_rden, 1)

            def norm_sums(done):
                dve.wait_ge(s_rden, 4 * (done + 1))
                dve.wait_ge(s_oraw, done + 1)
                dve.tensor_tensor(onorm[:, :], oraw[:, :], rden[:, :], ALU.mult).then_inc(s_on, 1)

            def batch(b, u, nth, prep=True, tail=True):
                for s in range(NS):
                    if s == LAG and tail:
                        take_sums(b - 1, 1)
                    if s == CH + LAG:
                        take_sums(b, 0)
                    if s == TAIL_STEP and tail:
                        take_softmax_sums(b, TAIL_ITEM)
                    if s == DEN_STEP:
                        take_softmax_sums(b, DEN_ITEM)
                    scale_scores(b, u, s)
                    if 0 <= s - TAIL_STEP < 4 and tail:
                        invert_sums(b, TAIL_ITEM, s - TAIL_STEP, 2 * b - 1)
                    if s in INVERT_STEPS:
                        invert_sums(b, DEN_ITEM, INVERT_STEPS.index(s), 2 * b)
                    if s == TAIL_STEP + 4 and tail:
                        norm_sums(2 * b - 1)
                    if s == INVERT_STEPS[-1] + 1:
                        norm_sums(2 * b)
                    for i in norms_at[s - 1] if prep and s >= 1 else []:
                        sum_squares(b + 1, i)
                    if prep and s == 5:
                        take_bias(b + 1, 1 - u)
                    if s == 8 and tail:
                        add_out(b, 0, b - 1)
                    if prep and s in (9, 10):
                        take_queries(b, s - 8)
                    if prep and s == 12:
                        sum_query_squares(b + 1)
                    if prep and s == 14:
                        norm_queries(b + 1)
                    if prep and s in (16, 17):
                        take_turned(b, s - 13)
                    if prep and s in (18, 19, 20, 21):
                        take_absorbed(b, 1 - u, s - 13)
                    if s == 22:
                        add_out(b, 9, b)
                    if prep and s == 22:
                        key_roots(b + 1, 1 - u)

            dve.memset(qblk[:, :, :, :], 0.0)
            dve.memset(kss[:, :, :], 1.0).then_inc(s_blk0, 1)
            dve.wait_ge(s_blk0, 1)
            take_bias(0, 0)
            for what, i in before:
                if what == "k":
                    sum_squares(0, i)
                if what == "q":
                    take_queries(-1, i)
                if what == "t":
                    take_turned(-1, i)
                if what == "a":
                    take_absorbed(-1, 0, i)
                if (what, i) == ("k", 1):
                    sum_query_squares(0)
                if (what, i) == ("k", 5):
                    norm_queries(0)
            key_roots(0, 0)
            batches(dve, batch)
            take_sums(B - 1, 1)
            take_softmax_sums(B, 0)
            for j in range(4):
                invert_sums(B, 0, j, 2 * B - 1)
            norm_sums(2 * B - 1)
            add_out(B, 0, B - 1)



def route(nc, tag, k, xT, router, router_row, parts, shareT, pair_softmax):
    with Net(nc) as n:
        def t(name, e=True, dt=F32):
            return n.sb(f"{tag}_{name}", [L, B, E] if e else [L, B], dt)

        lg, hot, best, lg2, ex, share = t("lg"), t("hot"), t("best"), t("lg2"), t("ex"), t("share")
        m1, pick, m2, den, rden, gap, egap = [t(v, False) for v in ("m1", "pick", "m2", "den", "rden", "gap", "egap")]
        share2 = n.sb(f"{tag}_share2", [L, B, 2 * E], F32R)
        lgp = n.ps(f"{tag}_lgp", 1)
        shp = n.ps(f"{tag}_shp", 4)
        s_lg = n.sem(f"{tag}_s_lg")
        s_v = n.sem(f"{tag}_s_v")
        s_ex = n.sem(f"{tag}_s_ex")
        s_share = n.sem(f"{tag}_s_share")
        s_turn = n.sem(f"{tag}_s_turn")
        s_st = n.sem(f"{tag}_s_st")
        s_high = n.sem(f"{tag}_s_high")
        s_low = n.sem(f"{tag}_s_low")
        wide = [L, B, E]
        block = n.ctx.enter_context(nc.Block())

        @block.tensor
        def _(pe):
            for b in range(B):
                m = pe.matmul(lgp[0:L, 0, b * E:(b + 1) * E], xT[:, b * L:(b + 1) * L], router,
                              start=True, stop=True)
            m.then_inc(s_lg, 1)
            pe.wait_ge(s_share, 1)
            for b in range(B):
                m = pe.transpose(shp[0:2 * E, b // 4, (b % 4) * L:(b % 4 + 1) * L], share2[:, b, :].bitcast(F32),
                                 k["ident"][0:L, 0:L])
                if b % 4 == 3:
                    m.then_inc(s_turn, 1)

        @block.scalar
        def _(act):
            for whole, high, low in parts:
                act.activation(high, whole, ACT.Copy).then_inc(s_high, 1)
            if pair_softmax:
                act.wait_ge(s_v, 9)
                act.activation(egap[:, :], gap[:, :], ACT.Exp).then_inc(s_ex, 1)
            else:
                act.wait_ge(s_v, 10)
                act.activation(ex[:, :, :], lg2[:, :, :], ACT.Exp).then_inc(s_ex, 1)

        @block.gpsimd
        def _(pool):
            for i, (whole, high, low) in enumerate(parts):
                if low is None:
                    continue
                pool.wait_ge(s_high, i + 1)
                pool.tensor_tensor(low, whole, high.bitcast(F32), ALU.subtract).then_inc(s_low, 1)

        @block.vector
        def _(dve):
            step = [0]

            def then(ins):
                step[0] += 1
                ins.then_inc(s_v, 1)
                dve.wait_ge(s_v, step[0])

            dve.wait_ge(s_lg, 1)
            then(dve.tensor_tensor(lg[:, :, :], lgp[0:L, 0, 0:B * E].rearrange("l (b e) -> l b e", b=B),
                                   router_row.unsqueeze(1).to_broadcast(wide), ALU.add))
            rank = k["rank_row"][:, :].unsqueeze(1).to_broadcast(wide)
            then(dve.tensor_reduce(m1[:, :], lg[:, :, :], AX_X, ALU.max))
            then(dve.tensor_tensor(hot[:, :, :], lg[:, :, :], over_heads(m1[:, :], E), ALU.is_ge))
            then(dve.tensor_tensor(hot[:, :, :], hot[:, :, :], rank, ALU.mult))
            then(dve.tensor_reduce(pick[:, :], hot[:, :, :], AX_X, ALU.max))
            then(dve.tensor_tensor(best[:, :, :], hot[:, :, :], over_heads(pick[:, :], E), ALU.is_ge))
            then(dve.scalar_tensor_tensor(out=lg2[:, :, :].rearrange("l b e -> l (b e)"),
                                          in0=best[:, :, :].rearrange("l b e -> l (b e)"), scalar=-1e30,
                                          in1=lg[:, :, :].rearrange("l b e -> l (b e)"),
                                          op0=ALU.mult, op1=ALU.add))
            then(dve.tensor_reduce(m2[:, :], lg2[:, :, :], AX_X, ALU.max))
            if pair_softmax:
                then(dve.tensor_tensor(gap[:, :], m2[:, :], m1[:, :], ALU.subtract))
                then(dve.tensor_tensor(hot[:, :, :], lg2[:, :, :], over_heads(m2[:, :], E), ALU.is_ge))
            else:
                then(dve.tensor_tensor(hot[:, :, :], lg2[:, :, :], over_heads(m2[:, :], E), ALU.is_ge))
                then(dve.tensor_tensor(lg2[:, :, :], lg[:, :, :], over_heads(m1[:, :], E), ALU.subtract))
            then(dve.tensor_tensor(hot[:, :, :], hot[:, :, :], rank, ALU.mult))
            then(dve.tensor_reduce(pick[:, :], hot[:, :, :], AX_X, ALU.max))
            then(dve.tensor_tensor(hot[:, :, :], hot[:, :, :], over_heads(pick[:, :], E), ALU.is_ge))
            dve.wait_ge(s_ex, 1)
            if pair_softmax:
                then(dve.tensor_scalar(den[:, :], egap[:, :], 1.0, None, ALU.add))
                then(dve.reciprocal(rden[:, :], den[:, :]))
                then(dve.tensor_tensor(hot[:, :, :], hot[:, :, :], over_heads(egap[:, :], E), ALU.mult))
                then(dve.tensor_tensor(hot[:, :, :], hot[:, :, :], best[:, :, :], ALU.add))
                then(dve.tensor_tensor(share[:, :, :], hot[:, :, :], over_heads(rden[:, :], E), ALU.mult))
            else:
                then(dve.tensor_reduce(den[:, :], ex[:, :, :], AX_X, ALU.add))
                then(dve.reciprocal(rden[:, :], den[:, :]))
                then(dve.tensor_tensor(hot[:, :, :], hot[:, :, :], best[:, :, :], ALU.add))
                then(dve.tensor_tensor(hot[:, :, :], hot[:, :, :], ex[:, :, :], ALU.mult))
                then(dve.tensor_tensor(share[:, :, :], hot[:, :, :], over_heads(rden[:, :], E), ALU.mult))
            then(dve.tensor_copy(share2[:, :, 0:E], share[:, :, :]))
            dve.tensor_tensor(share2[:, :, E:2 * E], share[:, :, :], share2[:, :, 0:E].bitcast(F32),
                              ALU.subtract).then_inc(s_share, 1)
            dve.wait_ge(s_high, 3)
            for g in range(4):
                dve.wait_ge(s_turn, g + 1)
                dve.tensor_copy(shareT[0:2 * E, 4 * g * L:4 * (g + 1) * L], shp[0:2 * E, g, 0:4 * L]).then_inc(s_st, 1)


def experts(nc, tag, k, x, x_high, x_low, w_high, w_low, b_up, w_down, b_downT, shareT, pick, gated):
    N = 4 * L
    chunks, products = (2, 2) if gated else (4, 1)
    LAG, BUFS = (2, 4) if gated else (1, 2)
    with Net(nc) as n:
        banks = n.ps(f"{tag}_banks", 4)
        down = n.ps(f"{tag}_down", 2)
        wide = n.ps(f"{tag}_wide", 1)
        turned = n.ps(f"{tag}_turned", 1)
        hid = [n.sb(f"{tag}_hid{i}", [D, chunks, N]) for i in range(BUFS)]
        share = [n.sb(f"{tag}_share{i}", [D, N]) for i in range(BUFS)]
        part = [n.sb(f"{tag}_part{i}", [D, N]) for i in range(2)]
        total = n.sb(f"{tag}_total", [D, N])
        s_mm = n.sem(f"{tag}_mm")
        s_gate = n.sem(f"{tag}_gate") if gated else None
        s_up = n.sem(f"{tag}_up") if gated else None
        s_hid = n.sem(f"{tag}_hid_s")
        s_wide = n.sem(f"{tag}_wide_s")
        s_share = n.sem(f"{tag}_share")
        s_down = n.sem(f"{tag}_down_s")
        s_part = n.sem(f"{tag}_part")
        s_total = n.sem(f"{tag}_total_s")
        s_turn = n.sem(f"{tag}_turn")
        s_add = n.sem(f"{tag}_add")
        U = chunks * E
        SLOTS = 4 // products
        block = n.ctx.enter_context(nc.Block())

        def groups(eng, group):
            group(0)
            with eng.Fori(1, 4) as g:
                group(g)

        def lagged(g, e):
            return (g, e) if e >= 0 else (g - 1, E + e)

        def first(g, e=0, m=1):
            return isinstance(g, int) and g == 0 and e < m

        @block.tensor
        def _(pe):
            def spread(g, e):
                if not first(g, e):
                    pe.wait_ge(s_share, E * g + e)
                pe.matmul(wide[:, 0, 0:N], pick[:, e, :], shareT[:, bass.ds(g * N, N)],
                          start=True, stop=True).then_inc(s_wide, 1)

            def ups(g, e):
                for j in range(chunks):
                    u = chunks * e + j
                    if not first(g, u, SLOTS):
                        if gated:
                            pe.wait_ge(s_gate, U * g + u + 1 - SLOTS)
                            pe.wait_ge(s_up, U * g + u + 1 - SLOTS)
                        else:
                            pe.wait_ge(s_hid, U * g + u + 1 - SLOTS)
                    for v in range(products):
                        dst = banks[:, products * (u % SLOTS) + v, 0:N]
                        at = slice((v * chunks + j) * D, (v * chunks + j + 1) * D)
                        tokens = bass.ds(g * N, N)
                        pe.matmul(dst, w_high[:, e, at], x_high[:, tokens], start=True, stop=False)
                        pe.matmul(dst, w_high[:, e, at], x_low[:, tokens], start=False, stop=False)
                        t = pe.matmul(dst, w_low[:, e, at], x_high[:, tokens], start=False, stop=True)
                    t.then_inc(s_mm, 1)

            def downs(g, e):
                pe.wait_ge(s_hid, U * g + chunks * (e + 1))
                if not first(g, e, 2):
                    pe.wait_ge(s_part, E * g + e - 1)
                for j in range(chunks):
                    t = pe.matmul(down[:, e % 2, 0:N], w_down[:, e, j, :], hid[e % BUFS][:, j, :],
                                  start=(j == 0), stop=(j == chunks - 1))
                t.then_inc(s_down, 1)

            def turn(g):
                pe.wait_ge(s_total, (E - 1) * (g + 1))
                if not first(g):
                    pe.wait_ge(s_add, g)
                for a in range(4):
                    t = pe.transpose(turned[0:L, 0, a * D:(a + 1) * D], total[:, a * L:(a + 1) * L], k["ident"][:, :])
                t.then_inc(s_turn, 1)

            def group(g):
                for e in range(E):
                    spread(g, e)
                    ups(g, e)
                    if e == LAG and not first(g):
                        turn(g - 1)
                    if e >= LAG or not first(g):
                        downs(*lagged(g, e - LAG))
            groups(pe, group)
            for e in range(E - LAG, E):
                downs(3, e)
            turn(3)

        def take_shares(act, g, e):
            act.wait_ge(s_wide, E * g + e + 1)
            if not first(g, e, BUFS):
                act.wait_ge(s_part, E * g + e + 1 - BUFS)
            act.activation(share[e % BUFS][:, :], wide[:, 0, 0:N], ACT.Copy).then_inc(s_share, 1)

        def weigh(dve, g, e):
            dve.wait_ge(s_down, E * g + e + 1)
            dve.wait_ge(s_share, E * g + e + 1)
            if e == 0 and not first(g):
                dve.wait_ge(s_turn, g)
            if e == 1 and not first(g):
                dve.wait_ge(s_total, (E - 1) * g)
            if e >= 3:
                dve.wait_ge(s_total, (E - 1) * g + e - 2)
            dve.scalar_tensor_tensor(out=(part[e % 2] if e else total)[:, :], in0=down[:, e % 2, 0:N],
                                     scalar=b_downT[:, e:e + 1], in1=share[e % BUFS][:, :], op0=ALU.add,
                                     op1=ALU.mult).then_inc(s_part, 1)

        def add_turned(dve, g):
            dve.wait_ge(s_turn, g + 1)
            xg = x[:, bass.ds(4 * g, 4), :].rearrange("l b d -> l (b d)")
            dve.tensor_tensor(xg, xg, turned[0:L, 0, :], ALU.add).then_inc(s_add, 1)

        def add_up(pool, g, e):
            pool.wait_ge(s_part, E * g + e + 1)
            if not first(g, e, 2):
                pool.wait_ge(s_total, (E - 1) * g + e - 1)
            pool.tensor_tensor(total[:, :], total[:, :], part[e % 2][:, :], ALU.add).then_inc(s_total, 1)

        if gated:
            gate, up, sig, glu = [n.sb(v, [D, 2, N]) for v in ("gate", "up", "sig", "glu")]
            s_sig, s_clip, s_glu = n.sem("ge_sig"), n.sem("ge_clip"), n.sem("ge_glu")

            @block.scalar
            def _(act):
                def group(g):
                    for u in range(U):
                        if u % 2 == 0:
                            take_shares(act, g, u // 2)
                        act.wait_ge(s_mm, U * g + u + 1)
                        if not first(g, u, 2):
                            act.wait_ge(s_hid, U * g + u - 1)
                        act.activation(up[:, u % 2, :], banks[:, 2 * (u % 2) + 1, 0:N], ACT.Identity,
                                       bias=b_up[:, u // 2, 2 + u % 2:3 + u % 2]).then_inc(s_up, 1)
                        act.wait_ge(s_gate, U * g + u + 1)
                        act.activation(sig[:, u % 2, :], gate[:, u % 2, :], ACT.Sigmoid, scale=1.702).then_inc(s_sig, 1)
                groups(act, group)

            @block.gpsimd
            def _(pool):
                def group(g):
                    for u in range(U):
                        pool.wait_ge(s_sig, U * g + u + 1)
                        pool.tensor_tensor(glu[:, u % 2, :], gate[:, u % 2, :], sig[:, u % 2, :], ALU.mult).then_inc(s_glu, 1)
                        if u % 2 and u != 5 and (u >= 5 or not first(g)):
                            add_up(pool, *lagged(g, u // 2 - LAG))
                groups(pool, group)
                for e in range(E - LAG, E):
                    add_up(pool, 3, e)

            @block.vector
            def _(dve):
                def group(g):
                    def clip(u):
                        dve.wait_ge(s_mm, U * g + u + 1)
                        if not first(g, u, 2):
                            dve.wait_ge(s_glu, U * g + u - 1)
                        dve.tensor_scalar(gate[:, u % 2, :], banks[:, 2 * (u % 2), 0:N],
                                          b_up[:, u // 2, u % 2:u % 2 + 1], 7.0, ALU.add, ALU.min).then_inc(s_gate, 1)
                        dve.wait_ge(s_up, U * g + u + 1)
                        dve.tensor_scalar(up[:, u % 2, :], up[:, u % 2, :], 7.0, -7.0, ALU.min, ALU.max).then_inc(s_clip, 1)

                    def join(g, u):
                        dve.wait_ge(s_glu, U * g + u + 1)
                        dve.wait_ge(s_clip, U * g + u + 1)
                        e = u // 2
                        if not first(g, e, BUFS):
                            dve.wait_ge(s_down, E * g + e + 1 - BUFS)
                        dve.scalar_tensor_tensor(out=hid[e % BUFS][:, u % 2, :], in0=up[:, u % 2, :], scalar=1.0,
                                                 in1=glu[:, u % 2, :], op0=ALU.add, op1=ALU.mult).then_inc(s_hid, 1)

                    for u in range(U):
                        clip(u)
                        if u:
                            join(g, u - 1)
                        elif not first(g):
                            join(g - 1, U - 1)
                        if u % 2 and (u >= 2 * LAG or not first(g)):
                            weigh(dve, *lagged(g, u // 2 - LAG))
                        if u == 2 * LAG + 3 and not first(g):
                            add_turned(dve, g - 1)
                    return join

                group(0)
                with dve.Fori(1, 4) as g:
                    join = group(g)
                join(3, U - 1)
                for e in range(E - LAG, E):
                    weigh(dve, 3, e)
                add_turned(dve, 3)

        else:
            @block.scalar
            def _(act):
                def group(g):
                    for u in range(U):
                        e, j = u // 4, u % 4
                        if j == 0:
                            take_shares(act, g, e)
                        act.wait_ge(s_mm, U * g + u + 1)
                        if not first(g, e, 2):
                            act.wait_ge(s_down, E * g + e - 1)
                        act.activation(hid[e % 2][:, j, :], banks[:, u % 4, 0:N], ACT.Relu,
                                       bias=b_up[:, e, j:j + 1]).then_inc(s_hid, 1)
                groups(act, group)

            @block.gpsimd
            def _(pool):
                def group(g):
                    for e in range(1, E):
                        add_up(pool, g, e)
                groups(pool, group)

            @block.vector
            def _(dve):
                def group(g):
                    for e in range(E):
                        if e == 0 and not first(g):
                            add_turned(dve, g - 1)
                        weigh(dve, g, e)
                groups(dve, group)
                add_turned(dve, 3)



def linear_attention(nc, k, x, xT):
    W = D + 1
    WO = D + HEADS
    with Net(nc) as n:
        qlow = n.sb("la_qlow", [D, T])
        qT = n.sb("la_qT", [D, T])
        kf = n.sb("la_kf", [L, B, D])
        klow = n.sb("la_klow", [L, B, D])
        v1 = n.sb("la_v", [L, B, W])
        kv = n.sb("la_kv", [D, B, WO])
        o = n.sb("la_o", [L, B, D])
        nrm = n.sb("la_nrm", [L, B, HEADS])
        rnrm = n.sb("la_rnrm", [L, B, HEADS])
        banks = n.ps("la_banks", 8)
        s_q = n.sem("la_s_q")
        s_qe = n.sem("la_s_qe")
        s_qx = n.sem("la_s_qx")
        s_kvp = n.sem("la_s_kvp")
        s_ke = n.sem("la_s_ke")
        s_kx = n.sem("la_s_kx")
        s_f = n.sem("la_s_f")
        s_kvm = n.sem("la_s_kvm")
        s_kve = n.sem("la_s_kve")
        s_o = n.sem("la_s_o")
        s_oe = n.sem("la_s_oe")
        s_turn = n.sem("la_s_turn")
        s_te = n.sem("la_s_te")
        s_one = n.sem("la_s_one")
        block = n.ctx.enter_context(nc.Block())

        @block.tensor
        def _(pe):
            for g in range(4):
                pe.matmul(banks[:, g, 0:4 * L], k["wq1"][:, :], xT[:, 4 * g * L:4 * (g + 1) * L],
                          start=True, stop=True).then_inc(s_q, 1)
            for b in range(B):
                if b % 2 == 0 and b >= 8:
                    pe.wait_ge(s_ke, 2 * (b // 2 - 4) + 2)
                t = pe.matmul(banks[0:L, 4 + b // 2 % 4, (b % 2) * 2 * D:(b % 2 + 1) * 2 * D],
                              xT[:, b * L:(b + 1) * L], k["wkv1"][:, :], start=True, stop=True)
                if b % 2:
                    t.then_inc(s_kvp, 1)
            pe.wait_ge(s_f, 2)
            pe.wait_ge(s_qe, 8)
            for b in range(B):
                t = pe.matmul(banks[:, b // 3, (b % 3) * W:(b % 3 + 1) * W], kf[:, b, :], v1[:, b, :],
                              start=True, stop=True)
                if b % 3 == 2 or b == B - 1:
                    t.then_inc(s_kvm, 1)
            for b in range(B):
                if b % 3 == 0:
                    pe.wait_ge(s_kve, min(b + 3, B))
                t = pe.matmul(banks[0:L, b // 3, (b % 3) * WO:(b % 3 + 1) * WO], qT[:, b * L:(b + 1) * L],
                              kv[:, b, :], start=True, stop=True)
                if b % 3 == 2 or b == B - 1:
                    t.then_inc(s_o, 1)
            for b in range(B):
                if b % 4 == 0:
                    pe.wait_ge(s_oe, 6)
                t = pe.transpose(banks[:, b // 4, (b % 4) * L:(b % 4 + 1) * L], o[:, b, :], k["ident"][0:L, 0:L])
                if b % 4 == 3:
                    t.then_inc(s_turn, 1)

        @block.scalar
        def _(act):
            for g in range(4):
                act.wait_ge(s_qe, 2 * g + 2)
                act.activation(qlow[:, 4 * g * L:4 * (g + 1) * L], qlow[:, 4 * g * L:4 * (g + 1) * L],
                               ACT.Exp).then_inc(s_qx, 1)
            act.wait_ge(s_f, 1)
            act.activation(klow[:, :, :], klow[:, :, :], ACT.Exp).then_inc(s_kx, 1)
            for g in range(4):
                act.wait_ge(s_turn, g + 1)
                act.activation(xT[:, 4 * g * L:4 * (g + 1) * L], banks[:, g, 0:4 * L], ACT.Copy).then_inc(s_te, 1)

        @block.vector
        def _(dve):
            dve.memset(v1[:, :, D:W], 1.0).then_inc(s_one, 1)
            for g in range(4):
                cols = slice(4 * g * L, 4 * (g + 1) * L)
                dve.wait_ge(s_q, g + 1)
                dve.tensor_scalar(qT[:, cols], banks[:, g, 0:4 * L], k["bq1"][:, 0:1], 0.0, ALU.add,
                                  ALU.max).then_inc(s_qe, 1)
                dve.tensor_scalar(qlow[:, cols], banks[:, g, 0:4 * L], k["bq1"][:, 0:1], 0.0, ALU.add,
                                  ALU.min).then_inc(s_qe, 1)
            for r in range(B // 2):
                dve.wait_ge(s_kvp, r + 1)
                bank = banks[0:L, 4 + r % 4, :].rearrange("l (b m) -> l b m", b=2)
                dve.tensor_tensor(kf[:, 2 * r:2 * r + 2, :], bank[:, :, 0:D],
                                  k["bk1_row"][:, :].unsqueeze(1).to_broadcast([L, 2, D]), ALU.add).then_inc(s_ke, 1)
                dve.tensor_tensor(v1[:, 2 * r:2 * r + 2, 0:D], bank[:, :, D:2 * D],
                                  k["bv1_row"][:, :].unsqueeze(1).to_broadcast([L, 2, D]), ALU.add).then_inc(s_ke, 1)
            dve.wait_ge(s_ke, B)
            dve.tensor_scalar(klow[:, :, :], kf[:, :, :], 0.0, None, ALU.min).then_inc(s_f, 1)
            for g in range(4):
                cols = slice(4 * g * L, 4 * (g + 1) * L)
                dve.wait_ge(s_qx, g + 1)
                dve.tensor_tensor(qT[:, cols], qT[:, cols], qlow[:, cols], ALU.add).then_inc(s_one, 1)
            dve.wait_ge(s_kx, 1)
            dve.scalar_tensor_tensor(out=kf[:, :, :].rearrange("l b d -> l (b d)"),
                                     in0=kf[:, :, :].rearrange("l b d -> l (b d)"), scalar=0.0,
                                     in1=klow[:, :, :].rearrange("l b d -> l (b d)"),
                                     op0=ALU.max, op1=ALU.add).then_inc(s_f, 1)
            for b in range(B):
                dve.wait_ge(s_kvm, b // 3 + 1)
                m = banks[:, b // 3, (b % 3) * W:(b % 3 + 1) * W]
                dve.tensor_tensor(kv[:, b, 0:D], m[:, 0:D], k["same_head"][:, :], ALU.mult)
                dve.tensor_scalar(kv[:, b, D:WO], k["head_of"][:, :], m[:, D:W], None, ALU.mult).then_inc(s_kve, 1)
            for r in range(6):
                nb = min(3, B - 3 * r)
                dve.wait_ge(s_o, r + 1)
                src = banks[0:L, r, 0:nb * WO].rearrange("l (b m) -> l b m", b=nb)
                rows_ = slice(3 * r, 3 * r + nb)
                dve.tensor_scalar(nrm[:, rows_, :], src[:, :, D:WO], 1e-6, None, ALU.add).then_inc(s_one, 1)
                dve.wait_ge(s_one, 6 + 2 * r)
                dve.reciprocal(rnrm[:, rows_, :], nrm[:, rows_, :]).then_inc(s_one, 1)
                dve.wait_ge(s_one, 7 + 2 * r)
                for b in range(nb):
                    t = dve.tensor_tensor(o[:, 3 * r + b, :].rearrange("l (h d) -> l h d", h=HEADS),
                                          src[:, b, 0:D].rearrange("l (h d) -> l h d", h=HEADS),
                                          over_heads(rnrm[:, 3 * r + b, :], HD1), ALU.mult)
                t.then_inc(s_oe, 1)



def cross_attention_1(nc, k, ctxT_d, x, xT, ahead):
    NS = 2 * CH
    SLOTS = 3
    LAG = 2
    TILES = -(-HEADS * L // D)
    THIRDS = [(off(0), off(4)), (off(4), off(8)), (off(8), S)]
    with Net(nc) as n:
        ctxT = [n.sb(f"c1_ctxT{u}", [D, S]) for u in range(2)]
        khigh = n.sb("c1_khigh", [D, S], F32R)
        klow = n.sb("c1_klow", [D, S], F32R)
        kstack = [n.sb(f"c1_kstack{u}", [D, 4, S], F32R) for u in range(2)]
        k16 = n.sb("c1_k16", [D, S], BF16)
        v = [n.sb(f"c1_v{u}", [SP_MAX, CH, D]) for u in range(2)]
        qT = n.sb("c1_qT", [D, L])
        qbias = n.sb("c1_qbias", [STACK, 4])
        qall = n.sb("c1_qall", [STACK, 4, L])
        qparts = n.sb("c1_qparts", [STACK, 4, L], F32R)
        qstack = [n.sb(f"c1_qstack{u}", [STACK + 1, TILES * D], F32R) for u in range(2)]
        q16 = n.sb("c1_q16", [D, HEADS * L], BF16)
        mx = n.sb("c1_mx", [D, TILES, 3])
        negmx = n.sb("c1_negmx", [D, TILES])
        neg = n.sb("c1_neg", [TILES, D], F32R)
        p = [n.sb(f"c1_p{j}", [SP_MAX, HALF]) for j in range(4)]
        own = n.sb("c1_own", [D, 4, L])
        own_den = n.sb("c1_own_den", [D, 4, L])
        rden = n.sb("c1_rden", [D, L])
        cat = n.sb("c1_cat", [D, L])
        ring = n.ps("c1_ring", SLOTS)
        pvb = n.ps("c1_pvb", 1)
        denb = n.ps("c1_denb", 1)
        aux = n.ps("c1_aux", SLOTS)

        s_ctx = [n.sem(f"c1_s_ctx{u}") for u in range(2)]
        s_unit = n.sem("c1_s_unit")
        s_ufree = n.sem("c1_s_ufree")
        s_ahead = n.sem("c1_s_ahead")
        s_high = n.sem("c1_s_high")
        s_k16 = n.sem("c1_s_k16")
        s_stack = n.sem("c1_s_stack")
        s_qhigh = n.sem("c1_s_qhigh")
        s_qlow = n.sem("c1_s_qlow")
        s_qstack = n.sem("c1_s_qstack")
        s_q16 = n.sem("c1_s_q16")
        s_neg = n.sem("c1_s_neg")
        s_row = n.sem("c1_s_row")
        s_score = n.sem("c1_s_score")
        s_exp = n.sem("c1_s_exp")
        s_pv = n.sem("c1_s_pv")
        s_take = n.sem("c1_s_take")
        s_fin = n.sem("c1_s_fin")
        s_cat = n.sem("c1_s_cat")
        s_one = n.sem("c1_s_one")
        s_ones = n.sem("c1_s_ones")

        UNITS, TAIL, MAXIMA, TURN = 48, 7, 8, 47

        def unit(b, i):
            if isinstance(b, int) and b >= B - 1:
                return UNITS * B + b - (B - 1)
            return UNITS * (b + 1) + i

        def twice(b, i):
            return 2 if isinstance(b, int) and b <= 0 and i == TAIL - 1 else 1

        plan = {0: [0], 1: [1], 2: [2, 3], 3: [4, 5], 4: [6], 5: [TAIL], 21: [TURN]}
        FIRST, AFTER = 5, 20
        for i in range(3 * TILES):
            plan.setdefault(FIRST + i * (AFTER - FIRST) // (3 * TILES), []).append(MAXIMA + i)
        first_plan = [i for i in range(UNITS) if i != TAIL]

        block = n.ctx.enter_context(nc.Block())

        def batches(eng, batch):
            batch(0, 0, 1, tail=False)
            with eng.Fori(0, (B - 2) // 2) as i:
                batch(2 * i + 1, 1, i + 2)
                batch(2 * i + 2, 0, i + 2)
            batch(B - 1, 1, 0, prep=False)

        def planned(s, prep, tail):
            for i in plan.get(s, []):
                if tail if i == TAIL else prep:
                    yield i

        @block.sync
        def _(sp):
            def load(b, u):
                sp.dma_start(ctxT[u][:, :], ctxT_d[bass.ds(b, 1), :, :].rearrange("b d s -> (b d) s"))\
                  .then_inc(s_ctx[u], 16)

            def stack_keys(b, u):
                sp.wait_ge(s_ufree, unit(b - 1, 3))
                for g in range(4):
                    for part, src in enumerate((khigh, khigh, klow)):
                        sp.dma_start(kstack[u][32 * part:32 * part + 32, g, :].bitcast(F32),
                                     src[32 * g:32 * g + 32, :].bitcast(F32)).then_inc(s_stack, 16)

            def send_row(b, u):
                sp.wait_ge(s_ufree, unit(b - 1, TURN) + 1)
                sp.dma_start(qstack[u][STACK:STACK + 1, :].bitcast(F32).rearrange("a (t p) -> a t p", t=TILES),
                             neg[:, :].bitcast(F32)).then_inc(s_row, 16)

            load(0, 0)
            load(1, 1)
            stack_keys(0, 0)
            for dst, src in ahead:
                sp.dma_start(dst, src).then_inc(s_ahead, 16)
            send_row(0, 0)
            with sp.Fori(0, (B - 2) // 2) as i:
                for u in range(2):
                    b = 2 * i + u
                    sp.wait_ge(s_unit, unit(b - 1, TAIL))
                    load(b + 2, u)
                    stack_keys(b + 1, 1 - u)
                    send_row(b + 1, 1 - u)
            stack_keys(B - 1, 1)
            send_row(B - 1, 1)
            sp.wait_ge(s_ahead, 16 * len(ahead))

        @block.tensor
        def _(pe):
            def do(b, u, i):
                before = unit(b, i)
                last = isinstance(b, int) and b >= B - 1
                if last:
                    pe.wait_ge(s_ufree, before)
                elif not (isinstance(b, int) and b == -1 and i < SLOTS):
                    pe.wait_ge(s_ufree, before + 1 - SLOTS)
                bank = i % SLOTS
                if i < 3:
                    lo, hi = THIRDS[i]
                    t = pe.matmul(aux[:, bank, 0:hi - lo], k["wk2"][:, :], ctxT[u][:, lo:hi], start=True, stop=True)
                elif i == 3:
                    tokens = xT[:, bass.ds((b + 1) * L, L)]
                    for g in range(4):
                        pe.matmul(aux[0:STACK, bank, g * L:(g + 1) * L], k["wq2_thrice"][:, g, :], tokens,
                                  start=True, stop=True)
                    t = pe.matmul(aux[:, bank, 4 * L:5 * L], k["wq2"][:, :], tokens, start=True, stop=True)
                elif i < TAIL:
                    for a in range(4):
                        c = 4 * (i - 4) + a
                        t = pe.matmul(aux[0:rows(c), bank, a * D:(a + 1) * D], ctxT[u][:, off(c):off(c) + rows(c)],
                                      k["wv2"][:, :], start=True, stop=True)
                elif i == TAIL:
                    pe.wait_ge(s_cat, b)
                    t = pe.matmul(aux[0:L, bank, 0:D], cat[:, :], k["wo2T"][:, :], start=True, stop=True)
                elif i < TURN:
                    t_, part = (i - MAXIMA) // 3, (i - MAXIMA) % 3
                    lo, hi = THIRDS[part]
                    if i == MAXIMA:
                        pe.wait_ge(s_k16, b + 2)
                        pe.wait_ge(s_q16, b + 2)
                    m = min(D, HEADS * L - t_ * D)
                    t = pe.matmul(aux[0:m, bank, 0:hi - lo], q16[:, t_ * D:t_ * D + m], k16[:, lo:hi],
                                  start=True, stop=True)
                else:
                    pe.wait_ge(s_neg, b + 2)
                    t = pe.transpose(aux[0:TILES, bank, 0:D], negmx[:, :], k["ident"][:, :])
                t.then_inc(s_unit, twice(b, i))

            def score(b, u, s):
                half, c = s // CH, s % CH
                r = rows(c)
                if s == 0:
                    pe.wait_ge(s_row, 16 * (b + 1))
                    pe.wait_ge(s_stack, 12 * 16 * (b + 1))
                    pe.wait_ge(s_qstack, b + 1)
                if not (isinstance(b, int) and b == 0 and s == 0):
                    pe.wait_ge(s_exp, 2 * (NS * b + s) - 1)
                for a in range(2):
                    g, i = 2 * half + a, 2 * s + a
                    t = pe.matmul(ring[0:r, i % SLOTS, 0:4 * L], kstack[u][0:STACK + 1, g, off(c):off(c) + r],
                                  qstack[u][:, 4 * g * L:4 * (g + 1) * L], start=True, stop=True)
                t.then_inc(s_score, 1)

            def weigh(b, u, s):
                half, c = s // CH, s % CH
                r = rows(c)
                if c == 0 and not (isinstance(b, int) and b == 0):
                    pe.wait_ge(s_take, 2 * b + half - 1)
                pe.wait_ge(s_exp, 2 * (NS * b + s + 1))
                st, sp_ = c == 0, c == CH - 1
                for a in range(2):
                    g = 2 * half + a
                    pe.matmul(pvb[32 * g:32 * g + 32, 0, 0:4 * L], v[u][0:r, c, 32 * g:32 * g + 32],
                              p[s % 4][0:r, a * 4 * L:(a + 1) * 4 * L], start=st, stop=sp_)
                for a in range(2):
                    q = (2 * half + a + 2) % 4
                    t = pe.matmul(denb[32 * q:32 * q + 32, 0, 0:4 * L], k["ones"][0:r, 0:32],
                                  p[s % 4][0:r, a * 4 * L:(a + 1) * 4 * L], start=st, stop=sp_)
                t.then_inc(s_pv, 1)

            def batch(b, u, nth, prep=True, tail=True):
                if prep:
                    pe.wait_ge(s_ctx[1 - u], 16 * nth)
                for s in range(NS):
                    units = list(planned(s, prep, tail))
                    first = max(0, len(units) - 2)
                    for i in units[:first]:
                        do(b, 1 - u, i)
                    score(b, u, s)
                    for i in units[first:first + 1]:
                        do(b, 1 - u, i)
                    if s >= LAG:
                        weigh(b, u, s - LAG)
                    elif tail:
                        weigh(b - 1, 1 - u, NS - LAG + s)
                    for i in units[first + 1:]:
                        do(b, 1 - u, i)

            pe.wait_ge(s_ctx[0], 16)
            for i in first_plan:
                do(-1, 0, i)
            pe.wait_ge(s_ones, 2)
            batches(pe, batch)
            for s in range(NS - LAG, NS):
                weigh(B - 1, 1, s)
            do(B, 0, TAIL)

        @block.scalar
        def _(act):
            def keep_high(b, i):
                if i == 0 and not (isinstance(b, int) and b == -1):
                    act.wait_ge(s_stack, 12 * 16 * (b + 1))
                    act.wait_ge(s_k16, b + 1)
                lo, hi = THIRDS[i]
                act.wait_ge(s_unit, unit(b, i) + 1)
                act.activation(khigh[:, lo:hi], aux[:, i % SLOTS, 0:hi - lo], ACT.Identity,
                               bias=k["bk2"][:, 0:1]).then_inc(s_high, 1)

            def keep_high_queries(b):
                act.wait_ge(s_ufree, unit(b, 3) + 1)
                if not (isinstance(b, int) and b == -1):
                    act.wait_ge(s_qstack, b + 1)
                act.activation(qparts[:, :, :], qall[:, :, :], ACT.Copy).then_inc(s_qhigh, 1)

            def narrow(b):
                act.wait_ge(s_ufree, unit(b, 3))
                act.wait_ge(s_high, 3 * (b + 2))
                act.activation(k16[:, :], khigh[:, :].bitcast(F32), ACT.Copy).then_inc(s_k16, 1)

            def batch(b, u, nth, prep=True, tail=True):
                for s in range(NS):
                    r = rows(s % CH)
                    if not (isinstance(b, int) and b == 0 and s < 4):
                        act.wait_ge(s_pv, NS * b + s - 3)
                    act.wait_ge(s_score, NS * b + s + 1)
                    for a in range(2):
                        act.activation(p[s % 4][0:r, a * 4 * L:(a + 1) * 4 * L], ring[0:r, (2 * s + a) % SLOTS, 0:4 * L],
                                       ACT.Exp).then_inc(s_exp, 1)
                    if prep and s < 3:
                        keep_high(b, s)
                    if prep and s == 2:
                        keep_high_queries(b)
                        narrow(b)

            for i in range(3):
                keep_high(-1, i)
            keep_high_queries(-1)
            narrow(-1)
            batches(act, batch)

        @block.gpsimd
        def _(pool):
            def stack_queries(b, u):
                pool.wait_ge(s_ufree, unit(b, 3) + 1)
                if not (isinstance(b, int) and b == -1):
                    pool.wait_ge(s_neg, b + 1)
                pool.tensor_tensor(q16[:, :].rearrange("p (h l) -> p h l", h=HEADS), over_heads(k["head_of"][:, :], L),
                                   qT[:, :].unsqueeze(1).to_broadcast([D, HEADS, L]), ALU.mult).then_inc(s_q16, 1)
                pool.wait_ge(s_qhigh, b + 2)
                pool.wait_ge(s_q16, b + 2)
                low = slice(32, 64)
                pool.tensor_tensor(qparts[low, :, :], qall[low, :, :], qparts[low, :, :].bitcast(F32),
                                   ALU.subtract).then_inc(s_qlow, 1)
                pool.wait_ge(s_qlow, b + 2)
                for g in range(4):
                    t = pool.tensor_tensor(
                        qstack[u][0:STACK, 4 * g * L:4 * (g + 1) * L].rearrange("p (h l) -> p h l", h=4),
                        over_heads(k["head_in_four"][0:STACK, :], L),
                        qparts[:, g, :].bitcast(F32).unsqueeze(1).to_broadcast([STACK, 4, L]), ALU.mult)
                t.then_inc(s_qstack, 1)

            def batch(b, u, nth, prep=True, tail=True):
                if prep:
                    stack_queries(b, 1 - u)

            def set_ones(u):
                pool.memset(kstack[u][STACK:STACK + 1, :, :].bitcast(F32), 1.0).then_inc(s_ones, 1)

            set_ones(0)
            pool.wait_ge(s_ones, 1)
            stack_queries(-1, 0)
            pool.wait_ge(s_qstack, 1)
            set_ones(1)
            batches(pool, batch)

        @block.vector
        def _(dve):
            def take(b, u, i):
                dve.wait_ge(s_unit, unit(b, i) + 1)
                bank = aux[:, i % SLOTS, :]
                j = b + 1
                if i < 3:
                    lo, hi = THIRDS[i]
                    dve.wait_ge(s_high, 3 * j + i + 1)
                    dve.scalar_tensor_tensor(out=klow[:, lo:hi], in0=bank[:, 0:hi - lo], scalar=k["bk2"][:, 0:1],
                                             in1=khigh[:, lo:hi].bitcast(F32), op0=ALU.add,
                                             op1=ALU.subtract).then_inc(s_ufree, 1)
                elif i == 3:
                    if not (isinstance(b, int) and b == -1):
                        dve.wait_ge(s_q16, j)
                        dve.wait_ge(s_qlow, j)
                    dve.tensor_scalar(qT[:, :], bank[:, 4 * L:5 * L], k["bq2"][:, 0:1], HD1 ** -0.5, ALU.add, ALU.mult)
                    dve.scalar_tensor_tensor(out=qall[:, :, :], in0=bank[0:STACK, 0:4 * L].rearrange("p (g l) -> p g l", g=4),
                                             scalar=HD1 ** -0.5, in1=over_heads(qbias[:, :], L), op0=ALU.mult,
                                             op1=ALU.add).then_inc(s_ufree, 1)
                elif i < TAIL:
                    c = 4 * (i - 4)
                    r = rows(c)
                    dve.tensor_copy(v[u][0:r, c:c + 4, :].rearrange("p c d -> p (c d)"), bank[0:r, :])\
                       .then_inc(s_ufree, twice(b, i))
                elif i == TAIL:
                    xb = x[:, bass.ds(b - 1, 1), :].rearrange("l b d -> l (b d)")
                    dve.tensor_tensor(xb, xb, bank[0:L, 0:D], ALU.add).then_inc(s_ufree, 1)
                elif i < TURN:
                    t_, part = (i - MAXIMA) // 3, (i - MAXIMA) % 3
                    lo, hi = THIRDS[part]
                    m = min(D, HEADS * L - t_ * D)
                    dve.tensor_reduce(mx[0:m, t_, part:part + 1], bank[0:m, 0:hi - lo], AX_X,
                                      ALU.max).then_inc(s_ufree, 1)
                    if i == TURN - 1:
                        dve.wait_ge(s_ufree, unit(b, i) + 1)
                        dve.tensor_reduce(negmx[:, :], mx[:, :, :], AX_X, ALU.max, negate=True).then_inc(s_neg, 1)
                else:
                    if not (isinstance(b, int) and b == -1):
                        dve.wait_ge(s_row, 16 * j)
                    dve.tensor_copy(neg[:, :], bank[0:TILES, 0:D]).then_inc(s_ufree, 1)

            def take_half(b, half):
                lo = 64 * half
                for dst, src, at in ((own, pvb, lo), (own_den, denb, 64 - lo)):
                    dve.wait_ge(s_pv, NS * b + CH * (half + 1))
                    t = dve.tensor_tensor(dst[lo:lo + 64, :, :],
                                          src[at:at + 64, 0, 0:4 * L].rearrange("p (j l) -> p j l", j=4),
                                          over_heads(k["head_in_four"][at:at + 64, :], L), ALU.mult)
                t.then_inc(s_take, 1)

            def own_sums(b):
                dve.wait_ge(s_take, 2 * b + 2)
                dve.tensor_reduce(rden[:, :], own_den[:, :, :].rearrange("p j l -> p l j"), AX_X, ALU.add).then_inc(s_fin, 1)
                dve.tensor_reduce(cat[:, :], own[:, :, :].rearrange("p j l -> p l j"), AX_X, ALU.add)

            def finish(b):
                dve.wait_ge(s_fin, 3 * b + 1)
                dve.reciprocal(rden[:, :], rden[:, :]).then_inc(s_fin, 1)
                dve.wait_ge(s_fin, 3 * b + 2)
                dve.tensor_tensor(cat[:, :], cat[:, :], rden[:, :], ALU.mult).then_inc(s_fin, 1)
                dve.wait_ge(s_fin, 3 * b + 3)
                dve.tensor_scalar(cat[:, :], cat[:, :], k["bv2"][:, 0:1], None, ALU.add).then_inc(s_cat, 1)

            def batch(b, u, nth, prep=True, tail=True):
                for s in range(NS):
                    if s == LAG and tail:
                        take_half(b - 1, 1)
                    if s == 3 and tail:
                        own_sums(b - 1)
                    if s == 4 and tail:
                        finish(b - 1)
                    if s == CH + LAG:
                        take_half(b, 0)
                    for i in planned(s, prep, tail):
                        take(b, 1 - u, i)

            dve.tensor_scalar(qbias[:, :], k["bq2_thrice"][:, :], HD1 ** -0.5, None, ALU.mult).then_inc(s_one, 1)
            dve.memset(mx[:, :, :], 0.0).then_inc(s_one, 1)
            dve.tensor_tensor(x[:, :, :], x[:, :, :], k["bo2_row"][:, :].unsqueeze(1).to_broadcast([L, B, D]),
                              ALU.add).then_inc(s_one, 1)
            dve.wait_ge(s_one, 3)
            for i in first_plan:
                take(-1, 0, i)
            batches(dve, batch)
            take_half(B - 1, 1)
            own_sums(B - 1)
            finish(B - 1)
            take(B, 0, TAIL)



def decoder(nc, a, out):
    with Net(nc) as n:
        def load(name, shape, src=None, dt=F32):
            t = n.sb(name, shape, dt)
            pairs.append((t[tuple(slice(None) for _ in shape)], a[name] if src is None else src))
            return t

        def row(name, m):
            return load(name, [L if m != HD0 else SP_MAX, m], a[name].partition_broadcast(L if m != HD0 else SP_MAX))

        pairs = []
        k = {}
        k["norms"] = k["projects"] = 0
        k["norm_sems"] = [n.sem(f"s_{v}") for v in ("stats", "sd", "rstd", "normed", "turned", "evacuated", "out")]
        k["project_sems"] = [n.sem(f"s_{v}") for v in ("product", "bias", "sum")]
        k["ones"] = n.sb("ones", [D, D])
        k["eps"] = n.sb("eps", [D, 1])
        k["zero"] = n.sb("zero", [D, 1])
        k["mask_bias"] = n.sb("mask_bias", [SP_MAX, B, CH])
        x = load("x", [L, B, D])
        k["ident"] = load("ident", [D, D])
        k["row_of"] = load("row_of", [SP_MAX, CH])
        k["lens"] = load("lens", [SP_MAX, B], a["lens"].partition_broadcast(SP_MAX), I32)
        for name in ("ln_w", "ln_b", "qnw", "knw"):
            k[name] = load(name, [D, 1])
        for name in ("bq1", "bk2", "bq2", "bv2"):
            k[name] = load(name, [D, 1])
        for name in ("bk1_row", "bv1_row", "bo1_row", "bo2_row"):
            k[name] = row(name, D)
        k["rank_row"] = row("rank_row", E)
        k["pick"] = load("pick", [D, E])
        k["head_of"] = load("head_of", [D, HEADS])
        k["same_head"] = load("same_head", [D, D])
        k["head_in_four"] = load("head_in_four", [D, 4])
        k["wkv1"] = load("wkv1", [D, 2 * D])
        for name in ("wq1", "wo1", "wq2", "wk2", "wv2", "wo2T"):
            k[name] = load(name, [D, D])
        k["wq2_thrice"] = load("wq2_thrice", [D, 4, STACK])
        k["bq2_thrice"] = load("bq2_thrice", [STACK, 4])
        k["qnw_row"] = row("qnw_row", HD0)
        k["knw_row"] = row("knw_row", HD0)
        k["bo0_row"] = row("bo0_row", D)
        k["woT0"] = load("woT0", [D, D])
        xT = n.sb("xT", [D, T])
        def expert_weights(n2, i, width, chunks):
            w_up = n2.sb(f"w_up{i}", [D, E, width])
            b_up = n2.sb(f"b_up{i}", [D, E, 4])
            w_down = n2.sb(f"w_down{i}", [D, E, chunks, D])
            b_downT = n2.sb(f"b_downT{i}", [D, E])
            router = n2.sb(f"router{i}", [D, E])
            r_row = n2.sb(f"router_row{i}", [L, E])
            return (w_up, b_up, w_down, b_downT, router, r_row), [
                (w_up[:, :, :], a[f"w_up{i}"]), (b_up[:, :, :], a[f"b_up{i}"]),
                (w_down[:, :, :, :], a[f"w_down{i}"]), (b_downT[:, :], a[f"b_downT{i}"]),
                (router[:, :], a[f"router{i}"]), (r_row[:, :], a[f"router_row{i}"].partition_broadcast(L))]

        def feed_forward(i, w_up, b_up, w_down, b_downT, router, r_row, gated):
            with Net(nc) as n2:
                w_high, w_low = n2.sb(f"w_high{i}", w_up.shape, F32R), n2.sb(f"w_low{i}", w_up.shape, F32R)
                x_high, x_low = n2.sb(f"x_high{i}", [D, T], F32R), n2.sb(f"x_low{i}", [D, T], F32R)
                shareT = n2.sb(f"shareT{i}", [D, T], F32R)
                pick = n2.sb(f"pick{i}", [D, E, D], F32R)
                parts = [(xT[:, :], x_high[:, :], x_low[:, :]), (over_heads(k["pick"][:, :], D), pick[:, :, :], None)]
                parts.append((k["zero"][:, 0:1].to_broadcast([D, T]), shareT[:, :], None))
                for e in range(0, E, 2):
                    parts.append((w_up[:, e:e + 2, :], w_high[:, e:e + 2, :], w_low[:, e:e + 2, :]))
                route(nc, f"r{i}", k, xT, router[:, :], r_row[:, :], parts, shareT, not gated)
                experts(nc, f"e{i}", k, x, x_high, x_low, w_high, w_low, b_up, w_down, b_downT, shareT, pick, gated)

        with Net(nc) as n2:
            tiles, ahead = expert_weights(n2, 0, 2 * I0, 2)
            with Net(nc) as n3:
                wq0 = n3.sb("wq0", [D, HEADS * HD0])
                wk_high, wk_low = [n3.sb(f"wk_{v}", [D, HEADS * HD0], F32R) for v in ("high", "low")]
                ctx_in = n3.sb("ctx_in", [D, S])
                ctx_high, ctx_low = [n3.sb(f"ctx_{v}0", [D, S], F32R) for v in ("high", "low")]
                wkq, wvo = n3.sb("wkq", [D, HEADS // 2, D]), n3.sb("wvo", [D, HEADS, D])
                with Net(nc) as n4:
                    x_steps = n4.sb("x_steps", [D, L, B])
                    hidden = n4.sb("hidden", [D, L, B])
                    wk0 = n4.sb("wk0", [D, HEADS * HD0])
                    wkT = n4.sb("wkT", [D, HEADS // 2, D])
                    wvT = n4.sb("wvT", [D, HEADS // 2, D])
                    wo = n4.sb("wo0", [D, HEADS // 2, D])
                    y = n4.sb("y", [L, B, D])
                    first = [(x_steps[:, :, :], a["x_steps"])]
                    for name in ("wgT", "wrT", "decay", "bg", "br"):
                        k[name] = n4.sb(name, [D, 1] if name in ("decay", "bg", "br") else [D, D])
                        first.append((k[name][:, :], a[name]))
                    pairs += [(wkT[:, :, :], a["wkT0"]), (wvT[:, :, :], a["wvT0"]),
                              (wo[:, :, :], a["wo0"]), (wq0[:, :], a["wq0"]), (wk0[:, :], a["wk0"]),
                              (ctx_in[:, :], a["ctxT"][0, :, :])]
                    load_first(nc, k, first)
                    recurrence(nc, k, x_steps, hidden, pairs)
                    hidden_to_tokens(nc, k, hidden, y)
                    norm_tokens(nc, "n0", k, y, xT, k["ln_w"][:, 0:1], k["ln_b"][:, 0:1])
                    project_add(nc, k, "p0", xT, k["woT0"][:, :], k["bo0_row"][:, :], x)
                    fold_weights(nc, k, wkT, wvT, wo, wkq, wvo,
                                 [(ctx_in[:, :], ctx_high[:, :], ctx_low[:, :]), (wk0[:, :], wk_high[:, :], wk_low[:, :])])
                norm_tokens(nc, "n1", k, x, xT)
                cross_attention_0(nc, k, a["ctxT"], a["ctxN"], x, xT, wq0, wkq, wvo, ctx_in, ctx_high,
                                  ctx_low, wk_high, wk_low, ahead)
            norm_tokens(nc, "n2", k, x, xT)
            feed_forward(0, *tiles, gated=True)
        norm_tokens(nc, "n3", k, x, xT)
        with Net(nc) as n2:
            tiles, ahead = expert_weights(n2, 1, F1, 4)
            linear_attention(nc, k, x, xT)
            project_add(nc, k, "p4", xT, k["wo1"][:, :], k["bo1_row"][:, :], x)
            norm_tokens(nc, "n4", k, x, xT)
            cross_attention_1(nc, k, a["ctxT"], x, xT, ahead)
            norm_tokens(nc, "n5", k, x, xT)
            feed_forward(1, *tiles, gated=False)
        norm_tokens(nc, "n6", k, x, out=out)



def lay_out(v):
    import numpy as np

    def pairs_T(w):
        return w.T.reshape(HEADS // 2, D, D).transpose(1, 0, 2)

    ctx = v["ctx_1024"]
    short = ctx[:, :SP_FULL * CH].reshape(B, SP_FULL, CH, D)
    last = ctx[:, SP_FULL * CH:]
    parts = [np.concatenate([short[:, :, c]] + ([last[:, c:c + 1]] if c < S % CH else []), axis=1)
             for c in range(CH)]
    ctxT = np.concatenate(parts, axis=1).transpose(0, 2, 1)
    col = lambda w: w.reshape(-1, 1)
    row = lambda w: w.reshape(-1)
    two = lambda w: np.concatenate([w, w]).reshape(-1, 1)
    p = "L0_attn_"
    o = {
        "x": v["x"].transpose(1, 0, 2), "x_steps": v["x"].transpose(2, 1, 0),
        "ctxT": ctxT, "ctxN": ctx.reshape(B, S * D), "lens": v["_lenS2"],
        "ident": np.eye(D, dtype=np.float32),
        "row_of": (np.arange(SP_MAX)[:, None] * CH + np.arange(CH)[None, :]).astype(np.float32),
        "decay": col(v[p + "decay"]), "bg": col(v[p + "bg"]), "br": col(v[p + "br"]),
        "ln_w": col(v[p + "ln_w"]), "ln_b": col(v[p + "ln_b"]), "bo0_row": row(v[p + "bo"]),
        "wgT": v[p + "Wg"].T, "wrT": v[p + "Wr"].T, "woT0": v[p + "Wo"].T,
    }
    p = "L0_xattn_"
    o |= {
        "qnw": two(v[p + "q_norm_w"]), "knw": two(v[p + "k_norm_w"]),
        "qnw_row": row(v[p + "q_norm_w"]), "knw_row": row(v[p + "k_norm_w"]),
        "wq0": v[p + "Wq"], "wk0": v[p + "Wk"], "wkT0": pairs_T(v[p + "Wk"]), "wvT0": pairs_T(v[p + "Wv"]),
        "wo0": v[p + "Wo"].reshape(HEADS // 2, D, D).transpose(1, 0, 2),
    }
    def hidden(b, chunks):
        return b.reshape(E, chunks, D).transpose(2, 0, 1)

    p = "L0_ffn_"
    o |= {
        "router0": v[p + "router_weight"].T, "router_row0": row(v[p + "router_bias"]),
        "w_up0": v[p + "gate_up_proj"].transpose(1, 0, 2), "b_up0": hidden(v[p + "gate_up_bias"], 4),
        "w_down0": v[p + "down_proj"].reshape(E, 2, D, D).transpose(2, 0, 1, 3), "b_downT0": v[p + "down_bias"].T,
        "rank_row": np.arange(E, 0, -1).astype(np.float32),
        "pick": np.concatenate([np.eye(E), np.eye(E), np.zeros((D - 2 * E, E))]).astype(np.float32),
    }
    p = "L1_attn_"
    head = np.arange(D) // HD1
    o |= {
        "wq1": v[p + "Wq"], "wkv1": np.concatenate([v[p + "Wk"], v[p + "Wv"]], axis=1), "wo1": v[p + "Wo"],
        "bq1": col(v[p + "bq"]), "bk1_row": row(v[p + "bk"]), "bv1_row": row(v[p + "bv"]),
        "bo1_row": row(v[p + "bo"]),
        "head_of": (head[:, None] == np.arange(HEADS)[None, :]).astype(np.float32),
        "same_head": (head[:, None] == head[None, :]).astype(np.float32),
        "head_in_four": (head[:, None] % 4 == np.arange(4)[None, :]).astype(np.float32),
    }
    p = "L1_xattn_"
    heads = lambda w: w.transpose(1, 0, 2).reshape(D, D)
    o |= {
        "wq2": heads(v[p + "Wq"]), "wk2": heads(v[p + "Wk"]), "wv2": heads(v[p + "Wv"]), "wo2T": v[p + "Wo"].T,
        "bq2": col(v[p + "bq"]), "bk2": col(v[p + "bk"]), "bv2": col(v[p + "bv"]), "bo2_row": row(v[p + "bo"]),
    }
    thrice = lambda w: np.stack([np.tile(w[:, 32 * g:32 * g + 32], 3) for g in range(4)], axis=1)
    o |= {"wq2_thrice": thrice(o["wq2"]), "bq2_thrice": thrice(o["bq2"].T)[0].T}
    p = "L1_ffn_"
    o |= {
        "router1": v[p + "gate_w"], "router_row1": row(v[p + "gate_b"]),
        "w_up1": v[p + "W1"].transpose(1, 0, 2), "b_up1": hidden(v[p + "b1"], 4),
        "w_down1": v[p + "W2"].reshape(E, 4, D, D).transpose(2, 0, 1, 3), "b_downT1": v[p + "b2"].T,
    }
    return {n: np.ascontiguousarray(w) for n, w in o.items()}


def kernel(**inputs):
    import numpy as _np
    import concourse.bacc as _bacc
    from concourse import mybir as _mybir
    from concourse.bass_utils import run_bass_kernel_spmd as _run

    nc = _bacc.Bacc("TRN2", target_bir_lowering=False, num_devices=1)
    arrays, args = {}, {}
    for name, w in lay_out({n: _np.asarray(w) for n, w in inputs.items()}).items():
        arrays[f"in_{name}"] = w
        args[name] = nc.dram_tensor(f"in_{name}", w.shape, _mybir.dt.from_np(w.dtype), kind="ExternalInput").ap()
    out = nc.dram_tensor("out", (L, B, D), _mybir.dt.float32, kind="ExternalOutput").ap()
    decoder(nc, args, out)
    r = _run(nc, [arrays], core_ids=[0])
    return r.results[0]["out"].transpose(1, 0, 2)
```
